# Optimizing a Trainium2 kernel written in Bass

```python
import numpy as np
import jax
import jax.numpy as jnp

def _softmax(x, axis=-1):
    return jax.nn.softmax(x, axis=axis)

def _gelu(x):
    return jax.nn.gelu(x, approximate=True)

def _silu(x):
    return jax.nn.silu(x)

def _sigmoid(x):
    return jax.nn.sigmoid(x)

def _layernorm(x, axis=-1, eps=1e-05):
    m = jnp.mean(x, axis=axis, keepdims=True)
    v = jnp.var(x, axis=axis, keepdims=True)
    return (x - m) / jnp.sqrt(v + eps)

def _scatter_add(tgt, idx, src, axis=0):
    return tgt.at[idx].add(src)

def _segment_sum(src, seg, n):
    return jax.ops.segment_sum(src, seg, n)
kernel_name = 'mk_seq_preln_d4_jaxref_r8_1d3784'

def setup_inputs(seed: int=0):
    np.random.seed(seed)
    _w = jnp.asarray

    def _L0_attn_setup():
        import jax, jax.numpy as jnp
        import numpy as np
        NH, DK, DV, CHUNK = (4, 32, 32, 32)
        HID = 128
        FLOOR = 0.05
        EPS = 1e-05

        def _l2norm(x):
            return x * jax.lax.rsqrt(jnp.sum(x * x, -1, keepdims=True) + 1e-06)

        def _causal_dw_conv(x, w):
            K = w.shape[-1]
            y = jax.lax.conv_general_dilated(jnp.swapaxes(x, 1, 2), w[:, None, :], (1,), [(K - 1, 0)], dimension_numbers=('NCH', 'OIH', 'NCH'), feature_group_count=w.shape[0])
            return jnp.swapaxes(y, 1, 2)

        def _fir(x, w):
            B, L, H, D = x.shape
            return _causal_dw_conv(x.reshape(B, L, H * D), w.reshape(H * D, -1)).reshape(B, L, H, D)

        def _stats(x):
            mean = jnp.mean(x, -1, keepdims=True)
            var = jnp.var(x, -1, keepdims=True)
            am = jnp.mean(jnp.abs(x), -1, keepdims=True)
            l2 = jnp.linalg.norm(x, axis=-1, keepdims=True)
            return jnp.concatenate([mean, var, am, l2], -1)

        def _delta_rule(q, k, v, beta, c=CHUNK):
            b, h, L, dk = q.shape
            dv = v.shape[-1]
            q = _l2norm(q)
            k = _l2norm(k)
            v = v * beta[..., None]
            kb = k * beta[..., None]
            n = L // c
            rs = lambda t: t.reshape(b, h, n, c, -1)
            q, k, v, kb = (rs(q), rs(k), rs(v), rs(kb))
            strict_low = jnp.tril(jnp.ones((c, c), bool), -1)
            attn = -(kb @ jnp.swapaxes(k, -1, -2)) * strict_low
            col = jnp.arange(c)

            def row_body(i, a):
                upd = jnp.einsum('...k,...kj->...j', a[..., i, :], a)
                return a.at[..., i, :].add(jnp.where(col < i, upd, 0.0))
            attn_inv = jax.lax.fori_loop(1, c, row_body, attn) + jnp.eye(c, dtype=attn.dtype)
            u = attn_inv @ v
            w = attn_inv @ kb
            incl_low = jnp.tril(jnp.ones((c, c), bool))

            def step(S, xs):
                q_i, k_i, u_i, w_i = xs
                attn_loc = jnp.einsum('bhid,bhjd->bhij', q_i, k_i) * incl_low
                u_i = u_i - w_i @ S
                o_i = q_i @ S + attn_loc @ u_i
                return (S + jnp.swapaxes(k_i, -1, -2) @ u_i, o_i)
            mv = lambda t: jnp.moveaxis(t, 2, 0)
            S0 = jnp.zeros((b, h, dk, dv), q.dtype)
            S, o = jax.lax.scan(step, S0, (mv(q), mv(k), mv(u), mv(w)))
            return (jnp.moveaxis(o, 0, 2).reshape(b, h, L, dv), S)
        key = jax.random.key(seed)
        ks = jax.random.split(key, 16)
        B, L = (2, 512)
        s = 0.02
        hs = jax.random.normal(ks[0], (B, L, HID), jnp.float32)
        Wq = jax.random.normal(ks[1], (HID, NH * DK)) * s
        Wk = jax.random.normal(ks[2], (HID, NH * DK)) * s
        Wv = jax.random.normal(ks[3], (HID, NH * DV)) * s
        Wb = jax.random.normal(ks[4], (HID, NH)) * s
        conv_q_w = jax.random.normal(ks[5], (NH * DK, 4)) * 0.1
        conv_k_w = jax.random.normal(ks[6], (NH * DK, 4)) * 0.1
        conv_v_w = jax.random.normal(ks[7], (NH * DV, 4)) * 0.1
        fir_short_w = jnp.zeros((NH, DV, 5)).at[..., -1].set(1.0) + jax.random.normal(ks[8], (NH, DV, 5)) * 0.02
        fir_long_w = jnp.zeros((NH, DV, 64)).at[..., -1].set(1.0) + jax.random.normal(ks[9], (NH, DV, 64)) * 0.02
        gin, hg = (HID + 16, HID * 2 // 2)
        mlp_w1 = jax.random.normal(ks[10], (gin, hg)) * s
        mlp_b1 = jnp.zeros((hg,), jnp.float32)
        mlp_w2 = jax.random.normal(ks[11], (hg, 4)) * s
        mlp_b2 = jnp.array([-0.5, -0.5, 0.5, 1.5], jnp.float32)
        log_temp = jnp.zeros((NH, 1), jnp.float32)
        o_norm_w = jnp.ones((DV,), jnp.float32)
        Wo = jax.random.normal(ks[12], (NH * DV, HID)) * s
        return dict(hidden_states=hs, Wq=Wq, Wk=Wk, Wv=Wv, Wb=Wb, conv_q_w=conv_q_w, conv_k_w=conv_k_w, conv_v_w=conv_v_w, fir_short_w=fir_short_w, fir_long_w=fir_long_w, mlp_w1=mlp_w1, mlp_b1=mlp_b1, mlp_w2=mlp_w2, mlp_b2=mlp_b2, log_temp=log_temp, o_norm_w=o_norm_w, Wo=Wo)
    _L0_attn_in = _L0_attn_setup()

    def _L0_ffn_setup():
        import jax, jax.numpy as jnp
        import numpy as np
        B, N, D = (4, 256, 128)
        SPARSITY = 0.01
        key = jax.random.key(seed)
        k1, k2, k3 = jax.random.split(key, 3)
        x = jax.random.normal(k1, (B, N, D), dtype=jnp.float32)
        spatial = jax.random.normal(k2, (D, D), dtype=jnp.float32) * 0.02
        freq = jnp.fft.fft(spatial, axis=-1)
        k = int(D * SPARSITY)
        mag = jnp.abs(freq)
        kth = jax.lax.top_k(mag, k)[0][:, -1:]
        w_sparse = jnp.where(mag >= kth, freq, 0.0 + 0j)
        bias = jax.random.normal(k3, (D,), dtype=jnp.float32) * 0.01
        return {'x': x, 'w_freq_real': jnp.real(w_sparse).astype(jnp.float32), 'w_freq_imag': jnp.imag(w_sparse).astype(jnp.float32), 'bias': bias}
    _L0_ffn_in = _L0_ffn_setup()

    def _L1_attn_setup():
        import jax, jax.numpy as jnp
        import numpy as np
        DIM = 128
        NUM_HEADS = 16
        DIM_HEAD = DIM // NUM_HEADS

        def _softmax(logits, axis=-1):
            logits = logits - jnp.max(logits, axis=axis, keepdims=True)
            e = jnp.exp(logits)
            return e / jnp.sum(e, axis=axis, keepdims=True)
        key = jax.random.key(seed)
        kx, kq, kk, kv, ko = jax.random.split(key, 5)
        s = 1.0 / np.sqrt(DIM)
        return {'x': jax.random.normal(kx, (4, 256, DIM), dtype=jnp.float32), 'Wq': jax.random.uniform(kq, (DIM, DIM), jnp.float32, -s, s), 'Wk': jax.random.uniform(kk, (DIM, DIM), jnp.float32, -s, s), 'Wv': jax.random.uniform(kv, (DIM, DIM), jnp.float32, -s, s), 'Wo': jax.random.uniform(ko, (DIM, DIM), jnp.float32, -s, s)}
    _L1_attn_in = _L1_attn_setup()

    def _L1_ffn_setup():
        import jax, jax.numpy as jnp
        import numpy as np
        DIM = 128
        DEPTH = 2
        HEADS = 8
        DIM_HEAD = 64
        WINDOW = 64
        INNER = HEADS * DIM_HEAD
        HID = int(DIM * 4 * 2 / 3)
        B, N = (2, 1024)
        QK_SCALE = 8.0

        def shift_token(t):
            t1, t2 = jnp.split(t, 2, axis=-1)
            t2 = jnp.pad(t2, ((0, 0), (1, 0), (0, 0)))[:, :-1]
            return jnp.concatenate([t1, t2], axis=-1)

        def l2norm(t):
            return t / jnp.clip(jnp.linalg.norm(t, axis=-1, keepdims=True), 1e-12)

        def rotate_half(x):
            x1, x2 = jnp.split(x, 2, axis=-1)
            return jnp.concatenate([-x2, x1], axis=-1)

        def rotary_xpos(q, k):
            n = q.shape[-2]
            half_idx = jnp.arange(0, DIM_HEAD, 2, dtype=jnp.float32)
            inv_freq = 1.0 / 10000.0 ** (half_idx / DIM_HEAD)
            t = jnp.arange(n, dtype=jnp.float32)
            freqs = t[:, None] * inv_freq[None, :]
            freqs = jnp.concatenate([freqs, freqs], axis=-1)
            base = (half_idx + 0.4 * DIM_HEAD) / (1.4 * DIM_HEAD)
            power = (t - n // 2) / float(WINDOW // 2)
            scale = base[None, :] ** power[:, None]
            scale = jnp.concatenate([scale, scale], axis=-1)
            cos, sin = (jnp.cos(freqs), jnp.sin(freqs))
            q = q * cos * scale + rotate_half(q) * sin * scale
            k = k * cos / scale + rotate_half(k) * sin / scale
            return (q, k)

        def local_attention(q, k, v):
            b, h, n, d = q.shape
            w = n // WINDOW
            bq = q.reshape(b, h, w, WINDOW, d) * QK_SCALE
            bk = k.reshape(b, h, w, WINDOW, d)
            bv = v.reshape(b, h, w, WINDOW, d)

            def look_around(t):
                p = jnp.pad(t, ((0, 0), (0, 0), (1, 0), (0, 0), (0, 0)))
                return jnp.concatenate([p[:, :, :w], p[:, :, 1:]], axis=3)
            bk, bv = (look_around(bk), look_around(bv))
            bt = jnp.arange(n).reshape(w, WINDOW)
            btp = jnp.pad(bt, ((1, 0), (0, 0)), constant_values=-1)
            btk = jnp.concatenate([btp[:w], btp[1:]], axis=1)
            sim = jnp.einsum('bhwid,bhwjd->bhwij', bq, bk)
            i = bt[:, :, None]
            j = btk[:, None, :]
            mask = (i < j) | (i > j + WINDOW) | (j == -1)
            sim = jnp.where(mask, -jnp.finfo(sim.dtype).max, sim)
            attn = jax.nn.softmax(sim, axis=-1)
            out = jnp.einsum('bhwij,bhwjd->bhwid', attn, bv)
            return out.reshape(b, h, n, d)

        def _layer(x, wqkv, qs, ksc, wo, lg, lb, w1, b1, w2, b2):
            b, n, _ = x.shape
            h = shift_token(x)
            qkv = h @ wqkv
            q, k, v = jnp.split(qkv, 3, axis=-1)
            to_heads = lambda t: t.reshape(b, n, HEADS, DIM_HEAD).transpose(0, 2, 1, 3)
            q, k, v = (to_heads(q), to_heads(k), to_heads(v))
            q = l2norm(q) * qs
            k = l2norm(k) * ksc
            q, k = rotary_xpos(q, k)
            o = local_attention(q, k, v)
            o = o.transpose(0, 2, 1, 3).reshape(b, n, INNER)
            x = x + o @ wo
            h = shift_token(x)
            mu = h.mean(-1, keepdims=True)
            var = h.var(-1, keepdims=True)
            h = (h - mu) / jnp.sqrt(var + 1e-05) * lg + lb
            h = h @ w1 + b1
            a, g = jnp.split(h, 2, axis=-1)
            h = a * jax.nn.gelu(g, approximate=False)
            x = x + h @ w2 + b2
            return x
        key = jax.random.key(seed)
        ks = jax.random.split(key, 6)
        return {'x': jax.random.normal(ks[0], (B, N, DIM), jnp.float32), 'wqkv': jax.random.normal(ks[1], (DEPTH, DIM, 3 * INNER), jnp.float32) * 0.02, 'q_scale': jnp.ones((DEPTH, DIM_HEAD), jnp.float32), 'k_scale': jnp.ones((DEPTH, DIM_HEAD), jnp.float32), 'wo': jax.random.normal(ks[2], (DEPTH, INNER, DIM), jnp.float32) * 0.02, 'ln_g': jnp.ones((DEPTH, DIM), jnp.float32), 'ln_b': jnp.zeros((DEPTH, DIM), jnp.float32), 'w1': jax.random.normal(ks[3], (DEPTH, DIM, 2 * HID), jnp.float32) * 0.02, 'b1': jnp.zeros((DEPTH, 2 * HID), jnp.float32), 'w2': jax.random.normal(ks[4], (DEPTH, HID, DIM), jnp.float32) * 0.02, 'b2': jnp.zeros((DEPTH, DIM), jnp.float32)}
    _L1_ffn_in = _L1_ffn_setup()

    def _L2_attn_setup():
        import jax, jax.numpy as jnp
        import numpy as np
        DIM = 128
        HEADS = 16
        DHEAD = DIM // HEADS
        EPS_NORM = 1e-06
        EPS_DEN = 1e-06

        def rmsnorm(x, w):
            xf = x.astype(jnp.float32)
            return (w * xf * jax.lax.rsqrt(jnp.mean(xf * xf, axis=-1, keepdims=True) + EPS_NORM)).astype(x.dtype)
        key = jax.random.key(seed)
        ks = jax.random.split(key, 6)
        b, n = (4, 512)
        x = jax.random.normal(ks[0], (b, n, DIM), dtype=jnp.float32)
        W_qkv = jax.random.normal(ks[1], (DIM, 3 * DIM), dtype=jnp.float32) * DIM ** (-0.5)
        qn_w = jnp.ones((DIM,), dtype=jnp.float32)
        kn_w = jnp.ones((DIM,), dtype=jnp.float32)
        W_out = jax.random.normal(ks[2], (DIM, DIM), dtype=jnp.float32) * DIM ** (-0.5)
        b_out = jnp.zeros((DIM,), dtype=jnp.float32)
        return {'x': x, 'W_qkv': W_qkv, 'qn_w': qn_w, 'kn_w': kn_w, 'W_out': W_out, 'b_out': b_out}
    _L2_attn_in = _L2_attn_setup()

    def _L2_ffn_setup():
        import jax, jax.numpy as jnp
        import numpy as np
        D = 128
        I = 64
        E = 32
        K = 4
        T = 2 * 256
        C = 2 * T * K // E
        key = jax.random.key(seed)
        ks = jax.random.split(key, 9)
        bf = jnp.bfloat16
        std = 0.02
        x = jax.random.normal(ks[0], (2, 256, D), dtype=jnp.float32).astype(bf)
        gate_w = (std * jax.random.normal(ks[1], (E, D), dtype=jnp.float32)).astype(bf)
        bias = jnp.zeros((E,), jnp.float32)
        W1 = (std * jax.random.normal(ks[2], (E, D, I), dtype=jnp.float32)).astype(bf)
        W3 = (std * jax.random.normal(ks[3], (E, D, I), dtype=jnp.float32)).astype(bf)
        W2 = (std * jax.random.normal(ks[4], (E, I, D), dtype=jnp.float32)).astype(bf)
        sw1 = (std * jax.random.normal(ks[5], (I, D), dtype=jnp.float32)).astype(bf)
        sw3 = (std * jax.random.normal(ks[6], (I, D), dtype=jnp.float32)).astype(bf)
        sw2 = (std * jax.random.normal(ks[7], (D, I), dtype=jnp.float32)).astype(bf)
        return {'x': x, 'gate_w': gate_w, 'bias': bias, 'W1': W1, 'W3': W3, 'W2': W2, 'sw1': sw1, 'sw3': sw3, 'sw2': sw2}
    _L2_ffn_in = _L2_ffn_setup()

    def _L3_attn_setup():
        import jax, jax.numpy as jnp
        import numpy as np
        N_HEADS = 16

        def _rotate_half(t):
            shp = t.shape
            t2 = t.reshape(*shp[:-1], shp[-1] // 2, 2)
            return jnp.stack((-t2[..., 1], t2[..., 0]), axis=-1).reshape(shp)
        key = jax.random.key(seed)
        k1, k2, k3 = jax.random.split(key, 3)
        B, N, D = (2, 256, 128)
        x = jax.random.normal(k1, (B, N, D), dtype=jnp.float32)
        w_qkv = jax.random.normal(k2, (D, 3 * D), dtype=jnp.float32) * D ** (-0.5)
        w_proj = jax.random.normal(k3, (D, D), dtype=jnp.float32) * D ** (-0.5)
        return {'x': x, 'w_qkv': w_qkv, 'w_proj': w_proj}
    _L3_attn_in = _L3_attn_setup()

    def _L3_ffn_setup():
        import jax, jax.numpy as jnp
        import numpy as np
        B, S, D = (2, 128, 128)
        E, K, I = (8, 2, 128)
        LIMIT = 7.0
        ALPHA = 1.702

        def _swiglu(t, limit):
            glu = jnp.minimum(t[..., ::2], limit)
            lin = jnp.clip(t[..., 1::2], -limit, limit)
            return glu * jax.nn.sigmoid(ALPHA * glu) * (lin + 1.0)
        key = jax.random.key(seed)
        k0, k1, k2, k3 = jax.random.split(key, 4)
        return {'x': jax.random.normal(k0, (B, S, D), jnp.float32), 'norm_w': jnp.ones((D,), jnp.float32), 'gate_w': jax.random.normal(k1, (E, D), jnp.float32) / np.sqrt(D).astype(np.float32), 'gate_b': jnp.zeros((E,), jnp.float32), 'mlp1_w': jax.random.normal(k2, (E, 2 * I, D), jnp.float32) / np.sqrt(D).astype(np.float32), 'mlp1_b': jnp.zeros((E, 2 * I), jnp.float32), 'mlp2_w': jax.random.normal(k3, (E, D, I), jnp.float32) / np.sqrt(I).astype(np.float32), 'mlp2_b': jnp.zeros((E, D), jnp.float32)}
    _L3_ffn_in = _L3_ffn_setup()
    _d = {'L0_attn_hidden_states': _L0_attn_in['hidden_states'], 'L0_attn_Wq': _L0_attn_in['Wq'], 'L0_attn_Wk': _L0_attn_in['Wk'], 'L0_attn_Wv': _L0_attn_in['Wv'], 'L0_attn_Wb': _L0_attn_in['Wb'], 'L0_attn_conv_q_w': _L0_attn_in['conv_q_w'], 'L0_attn_conv_k_w': _L0_attn_in['conv_k_w'], 'L0_attn_conv_v_w': _L0_attn_in['conv_v_w'], 'L0_attn_fir_short_w': _L0_attn_in['fir_short_w'], 'L0_attn_fir_long_w': _L0_attn_in['fir_long_w'], 'L0_attn_mlp_w1': _L0_attn_in['mlp_w1'], 'L0_attn_mlp_b1': _L0_attn_in['mlp_b1'], 'L0_attn_mlp_w2': _L0_attn_in['mlp_w2'], 'L0_attn_mlp_b2': _L0_attn_in['mlp_b2'], 'L0_attn_log_temp': _L0_attn_in['log_temp'], 'L0_attn_o_norm_w': _L0_attn_in['o_norm_w'], 'L0_attn_Wo': _L0_attn_in['Wo'], 'L0_ffn_w_freq_real': _L0_ffn_in['w_freq_real'], 'L0_ffn_w_freq_imag': _L0_ffn_in['w_freq_imag'], 'L0_ffn_bias': _L0_ffn_in['bias'], 'L1_attn_Wq': _L1_attn_in['Wq'], 'L1_attn_Wk': _L1_attn_in['Wk'], 'L1_attn_Wv': _L1_attn_in['Wv'], 'L1_attn_Wo': _L1_attn_in['Wo'], 'L1_ffn_wqkv': _L1_ffn_in['wqkv'], 'L1_ffn_q_scale': _L1_ffn_in['q_scale'], 'L1_ffn_k_scale': _L1_ffn_in['k_scale'], 'L1_ffn_wo': _L1_ffn_in['wo'], 'L1_ffn_ln_g': _L1_ffn_in['ln_g'], 'L1_ffn_ln_b': _L1_ffn_in['ln_b'], 'L1_ffn_w1': _L1_ffn_in['w1'], 'L1_ffn_b1': _L1_ffn_in['b1'], 'L1_ffn_w2': _L1_ffn_in['w2'], 'L1_ffn_b2': _L1_ffn_in['b2'], 'L2_attn_W_qkv': _L2_attn_in['W_qkv'], 'L2_attn_qn_w': _L2_attn_in['qn_w'], 'L2_attn_kn_w': _L2_attn_in['kn_w'], 'L2_attn_W_out': _L2_attn_in['W_out'], 'L2_attn_b_out': _L2_attn_in['b_out'], 'L2_ffn_gate_w': _L2_ffn_in['gate_w'], 'L2_ffn_bias': _L2_ffn_in['bias'], 'L2_ffn_W1': _L2_ffn_in['W1'], 'L2_ffn_W3': _L2_ffn_in['W3'], 'L2_ffn_W2': _L2_ffn_in['W2'], 'L2_ffn_sw1': _L2_ffn_in['sw1'], 'L2_ffn_sw3': _L2_ffn_in['sw3'], 'L2_ffn_sw2': _L2_ffn_in['sw2'], 'L3_attn_w_qkv': _L3_attn_in['w_qkv'], 'L3_attn_w_proj': _L3_attn_in['w_proj'], 'L3_ffn_norm_w': _L3_ffn_in['norm_w'], 'L3_ffn_gate_w': _L3_ffn_in['gate_w'], 'L3_ffn_gate_b': _L3_ffn_in['gate_b'], 'L3_ffn_mlp1_w': _L3_ffn_in['mlp1_w'], 'L3_ffn_mlp1_b': _L3_ffn_in['mlp1_b'], 'L3_ffn_mlp2_w': _L3_ffn_in['mlp2_w'], 'L3_ffn_mlp2_b': _L3_ffn_in['mlp2_b']}
    _x0 = _d['L0_attn_hidden_states']
    _d['L0_attn_hidden_states'] = jax.random.normal(jax.random.fold_in(jax.random.key(seed), 1), (8, 512, 128), dtype=_x0.dtype)
    del _x0
    return _d

def reference(L0_attn_hidden_states, L0_attn_Wq, L0_attn_Wk, L0_attn_Wv, L0_attn_Wb, L0_attn_conv_q_w, L0_attn_conv_k_w, L0_attn_conv_v_w, L0_attn_fir_short_w, L0_attn_fir_long_w, L0_attn_mlp_w1, L0_attn_mlp_b1, L0_attn_mlp_w2, L0_attn_mlp_b2, L0_attn_log_temp, L0_attn_o_norm_w, L0_attn_Wo, L0_ffn_w_freq_real, L0_ffn_w_freq_imag, L0_ffn_bias, L1_attn_Wq, L1_attn_Wk, L1_attn_Wv, L1_attn_Wo, L1_ffn_wqkv, L1_ffn_q_scale, L1_ffn_k_scale, L1_ffn_wo, L1_ffn_ln_g, L1_ffn_ln_b, L1_ffn_w1, L1_ffn_b1, L1_ffn_w2, L1_ffn_b2, L2_attn_W_qkv, L2_attn_qn_w, L2_attn_kn_w, L2_attn_W_out, L2_attn_b_out, L2_ffn_gate_w, L2_ffn_bias, L2_ffn_W1, L2_ffn_W3, L2_ffn_W2, L2_ffn_sw1, L2_ffn_sw3, L2_ffn_sw2, L3_attn_w_qkv, L3_attn_w_proj, L3_ffn_norm_w, L3_ffn_gate_w, L3_ffn_gate_b, L3_ffn_mlp1_w, L3_ffn_mlp1_b, L3_ffn_mlp2_w, L3_ffn_mlp2_b):

    def _L0_attn_ref(hidden_states, Wq, Wk, Wv, Wb, conv_q_w, conv_k_w, conv_v_w, fir_short_w, fir_long_w, mlp_w1, mlp_b1, mlp_w2, mlp_b2, log_temp, o_norm_w, Wo):
        import jax, jax.numpy as jnp
        import numpy as np
        NH, DK, DV, CHUNK = (4, 32, 32, 32)
        HID = 128
        FLOOR = 0.05
        EPS = 1e-05

        def _l2norm(x):
            return x * jax.lax.rsqrt(jnp.sum(x * x, -1, keepdims=True) + 1e-06)

        def _causal_dw_conv(x, w):
            K = w.shape[-1]
            y = jax.lax.conv_general_dilated(jnp.swapaxes(x, 1, 2), w[:, None, :], (1,), [(K - 1, 0)], dimension_numbers=('NCH', 'OIH', 'NCH'), feature_group_count=w.shape[0])
            return jnp.swapaxes(y, 1, 2)

        def _fir(x, w):
            B, L, H, D = x.shape
            return _causal_dw_conv(x.reshape(B, L, H * D), w.reshape(H * D, -1)).reshape(B, L, H, D)

        def _stats(x):
            mean = jnp.mean(x, -1, keepdims=True)
            var = jnp.var(x, -1, keepdims=True)
            am = jnp.mean(jnp.abs(x), -1, keepdims=True)
            l2 = jnp.linalg.norm(x, axis=-1, keepdims=True)
            return jnp.concatenate([mean, var, am, l2], -1)

        def _delta_rule(q, k, v, beta, c=CHUNK):
            b, h, L, dk = q.shape
            dv = v.shape[-1]
            q = _l2norm(q)
            k = _l2norm(k)
            v = v * beta[..., None]
            kb = k * beta[..., None]
            n = L // c
            rs = lambda t: t.reshape(b, h, n, c, -1)
            q, k, v, kb = (rs(q), rs(k), rs(v), rs(kb))
            strict_low = jnp.tril(jnp.ones((c, c), bool), -1)
            attn = -(kb @ jnp.swapaxes(k, -1, -2)) * strict_low
            col = jnp.arange(c)

            def row_body(i, a):
                upd = jnp.einsum('...k,...kj->...j', a[..., i, :], a)
                return a.at[..., i, :].add(jnp.where(col < i, upd, 0.0))
            attn_inv = jax.lax.fori_loop(1, c, row_body, attn) + jnp.eye(c, dtype=attn.dtype)
            u = attn_inv @ v
            w = attn_inv @ kb
            incl_low = jnp.tril(jnp.ones((c, c), bool))

            def step(S, xs):
                q_i, k_i, u_i, w_i = xs
                attn_loc = jnp.einsum('bhid,bhjd->bhij', q_i, k_i) * incl_low
                u_i = u_i - w_i @ S
                o_i = q_i @ S + attn_loc @ u_i
                return (S + jnp.swapaxes(k_i, -1, -2) @ u_i, o_i)
            mv = lambda t: jnp.moveaxis(t, 2, 0)
            S0 = jnp.zeros((b, h, dk, dv), q.dtype)
            S, o = jax.lax.scan(step, S0, (mv(q), mv(k), mv(u), mv(w)))
            return (jnp.moveaxis(o, 0, 2).reshape(b, h, L, dv), S)
        B, L, _ = hidden_states.shape
        q = jax.nn.silu(_causal_dw_conv(hidden_states @ Wq, conv_q_w)).reshape(B, L, NH, DK)
        k = jax.nn.silu(_causal_dw_conv(hidden_states @ Wk, conv_k_w)).reshape(B, L, NH, DK)
        v_direct = jax.nn.silu(_causal_dw_conv(hidden_states @ Wv, conv_v_w)).reshape(B, L, NH, DV)
        beta = jax.nn.sigmoid(hidden_states @ Wb)
        bhld = lambda t: jnp.transpose(t, (0, 2, 1, 3))
        delta_bh, _ = _delta_rule(bhld(q), bhld(k), bhld(v_direct), jnp.transpose(beta, (0, 2, 1)))
        delta_out = jnp.transpose(delta_bh, (0, 2, 1, 3))
        local_short = _fir(v_direct, fir_short_w)
        local_long = _fir(v_direct, fir_long_w)
        stats_vec = jnp.concatenate([_stats(local_short), _stats(local_long), _stats(delta_out), _stats(v_direct)], -1)
        hs_exp = jnp.broadcast_to(hidden_states[:, :, None, :], (B, L, NH, HID))
        gate_in = jnp.concatenate([hs_exp, stats_vec], -1)
        h1 = jax.nn.gelu(gate_in @ mlp_w1 + mlp_b1, approximate=False)
        logits = h1 @ mlp_w2 + mlp_b2
        probs = jax.nn.softmax(logits / jnp.exp(log_temp), -1)
        probs = FLOOR + (1.0 - 4.0 * FLOOR) * probs
        o = probs[..., 0:1] * local_short + probs[..., 1:2] * local_long + probs[..., 2:3] * delta_out + probs[..., 3:4] * v_direct
        o = o * jax.lax.rsqrt(jnp.mean(o * o, -1, keepdims=True) + EPS) * o_norm_w
        return o.reshape(B, L, NH * DV) @ Wo

    def _L0_ffn_ref(x, w_freq_real, w_freq_imag, bias):
        import jax, jax.numpy as jnp
        import numpy as np
        B, N, D = (4, 256, 128)
        SPARSITY = 0.01
        w = jax.lax.complex(w_freq_real, w_freq_imag)
        x_freq = jnp.fft.fft(x, axis=-1)
        y_freq = jnp.einsum('bnd,do->bno', x_freq, w)
        y = jnp.real(jnp.fft.ifft(y_freq, axis=-1))
        return y + bias

    def _L1_attn_ref(x, Wq, Wk, Wv, Wo):
        import jax, jax.numpy as jnp
        import numpy as np
        DIM = 128
        NUM_HEADS = 16
        DIM_HEAD = DIM // NUM_HEADS

        def _softmax(logits, axis=-1):
            logits = logits - jnp.max(logits, axis=axis, keepdims=True)
            e = jnp.exp(logits)
            return e / jnp.sum(e, axis=axis, keepdims=True)
        B, T, D = x.shape
        H, Dh = (NUM_HEADS, DIM_HEAD)
        q = (x @ Wq.T).reshape(B, T, H, Dh).transpose(0, 2, 1, 3)
        k = (x @ Wk.T).reshape(B, T, H, Dh).transpose(0, 2, 1, 3)
        v = (x @ Wv.T).reshape(B, T, H, Dh).transpose(0, 2, 1, 3)
        scale = Dh ** (-0.5)
        logits = jnp.einsum('bhqd,bhkd->bhqk', q, k) * scale
        causal_mask = jnp.triu(jnp.ones((T, T), dtype=bool), k=1)
        neg = -jnp.finfo(logits.dtype).max
        logits = jnp.where(causal_mask, neg, logits)
        attn = _softmax(logits, axis=-1)
        out = jnp.einsum('bhqk,bhkd->bhqd', attn, v)
        out = out.transpose(0, 2, 1, 3).reshape(B, T, D)
        return out @ Wo.T

    def _L1_ffn_ref(x, wqkv, q_scale, k_scale, wo, ln_g, ln_b, w1, b1, w2, b2):
        import jax, jax.numpy as jnp
        import numpy as np
        DIM = 128
        DEPTH = 2
        HEADS = 8
        DIM_HEAD = 64
        WINDOW = 64
        INNER = HEADS * DIM_HEAD
        HID = int(DIM * 4 * 2 / 3)
        B, N = (2, 1024)
        QK_SCALE = 8.0

        def shift_token(t):
            t1, t2 = jnp.split(t, 2, axis=-1)
            t2 = jnp.pad(t2, ((0, 0), (1, 0), (0, 0)))[:, :-1]
            return jnp.concatenate([t1, t2], axis=-1)

        def l2norm(t):
            return t / jnp.clip(jnp.linalg.norm(t, axis=-1, keepdims=True), 1e-12)

        def rotate_half(x):
            x1, x2 = jnp.split(x, 2, axis=-1)
            return jnp.concatenate([-x2, x1], axis=-1)

        def rotary_xpos(q, k):
            n = q.shape[-2]
            half_idx = jnp.arange(0, DIM_HEAD, 2, dtype=jnp.float32)
            inv_freq = 1.0 / 10000.0 ** (half_idx / DIM_HEAD)
            t = jnp.arange(n, dtype=jnp.float32)
            freqs = t[:, None] * inv_freq[None, :]
            freqs = jnp.concatenate([freqs, freqs], axis=-1)
            base = (half_idx + 0.4 * DIM_HEAD) / (1.4 * DIM_HEAD)
            power = (t - n // 2) / float(WINDOW // 2)
            scale = base[None, :] ** power[:, None]
            scale = jnp.concatenate([scale, scale], axis=-1)
            cos, sin = (jnp.cos(freqs), jnp.sin(freqs))
            q = q * cos * scale + rotate_half(q) * sin * scale
            k = k * cos / scale + rotate_half(k) * sin / scale
            return (q, k)

        def local_attention(q, k, v):
            b, h, n, d = q.shape
            w = n // WINDOW
            bq = q.reshape(b, h, w, WINDOW, d) * QK_SCALE
            bk = k.reshape(b, h, w, WINDOW, d)
            bv = v.reshape(b, h, w, WINDOW, d)

            def look_around(t):
                p = jnp.pad(t, ((0, 0), (0, 0), (1, 0), (0, 0), (0, 0)))
                return jnp.concatenate([p[:, :, :w], p[:, :, 1:]], axis=3)
            bk, bv = (look_around(bk), look_around(bv))
            bt = jnp.arange(n).reshape(w, WINDOW)
            btp = jnp.pad(bt, ((1, 0), (0, 0)), constant_values=-1)
            btk = jnp.concatenate([btp[:w], btp[1:]], axis=1)
            sim = jnp.einsum('bhwid,bhwjd->bhwij', bq, bk)
            i = bt[:, :, None]
            j = btk[:, None, :]
            mask = (i < j) | (i > j + WINDOW) | (j == -1)
            sim = jnp.where(mask, -jnp.finfo(sim.dtype).max, sim)
            attn = jax.nn.softmax(sim, axis=-1)
            out = jnp.einsum('bhwij,bhwjd->bhwid', attn, bv)
            return out.reshape(b, h, n, d)

        def _layer(x, wqkv, qs, ksc, wo, lg, lb, w1, b1, w2, b2):
            b, n, _ = x.shape
            h = shift_token(x)
            qkv = h @ wqkv
            q, k, v = jnp.split(qkv, 3, axis=-1)
            to_heads = lambda t: t.reshape(b, n, HEADS, DIM_HEAD).transpose(0, 2, 1, 3)
            q, k, v = (to_heads(q), to_heads(k), to_heads(v))
            q = l2norm(q) * qs
            k = l2norm(k) * ksc
            q, k = rotary_xpos(q, k)
            o = local_attention(q, k, v)
            o = o.transpose(0, 2, 1, 3).reshape(b, n, INNER)
            x = x + o @ wo
            h = shift_token(x)
            mu = h.mean(-1, keepdims=True)
            var = h.var(-1, keepdims=True)
            h = (h - mu) / jnp.sqrt(var + 1e-05) * lg + lb
            h = h @ w1 + b1
            a, g = jnp.split(h, 2, axis=-1)
            h = a * jax.nn.gelu(g, approximate=False)
            x = x + h @ w2 + b2
            return x
        for l in range(DEPTH):
            x = _layer(x, wqkv[l], q_scale[l], k_scale[l], wo[l], ln_g[l], ln_b[l], w1[l], b1[l], w2[l], b2[l])
        return x

    def _L2_attn_ref(x, W_qkv, qn_w, kn_w, W_out, b_out):
        import jax, jax.numpy as jnp
        import numpy as np
        DIM = 128
        HEADS = 16
        DHEAD = DIM // HEADS
        EPS_NORM = 1e-06
        EPS_DEN = 1e-06

        def rmsnorm(x, w):
            xf = x.astype(jnp.float32)
            return (w * xf * jax.lax.rsqrt(jnp.mean(xf * xf, axis=-1, keepdims=True) + EPS_NORM)).astype(x.dtype)
        b, n, _ = x.shape
        qkv = x @ W_qkv
        q, k, v = jnp.split(qkv, 3, axis=-1)
        q = rmsnorm(q, qn_w)
        k = rmsnorm(k, kn_w)

        def split_heads(t):
            return t.reshape(b, n, HEADS, DHEAD).transpose(0, 2, 1, 3)
        q, k, v = map(split_heads, (q, k, v))
        q = jax.nn.relu(q).astype(jnp.float32)
        k = jax.nn.relu(k).astype(jnp.float32)
        v = v.astype(jnp.float32)
        kv = jnp.einsum('bhnd,bhne->bhde', k, v)
        out = jnp.einsum('bhnd,bhde->bhne', q, kv)
        k_sum = k.sum(axis=2)
        normalizer = jnp.einsum('bhnd,bhd->bhn', q, k_sum) + EPS_DEN
        out = out / normalizer[..., None]
        out = out.transpose(0, 2, 1, 3).reshape(b, n, DIM)
        return out @ W_out + b_out

    def _L2_ffn_ref(x, gate_w, bias, W1, W3, W2, sw1, sw3, sw2):
        import jax, jax.numpy as jnp
        import numpy as np
        D = 128
        I = 64
        E = 32
        K = 4
        T = 2 * 256
        C = 2 * T * K // E
        X = x.reshape(-1, D)
        logits = (X @ gate_w.T).astype(jnp.float32)
        scores = jax.nn.sigmoid(logits)
        _, idx = jax.lax.top_k(scores + bias[None, :], K)
        w = jnp.take_along_axis(scores, idx, axis=-1)
        w = w / jnp.clip(jnp.sum(w, axis=-1, keepdims=True), 1e-12, None)
        w = w.astype(x.dtype)
        eid = idx.reshape(-1)
        onehot = (eid[:, None] == jnp.arange(E)[None, :]).astype(jnp.int32)
        pos = jnp.take_along_axis(jnp.cumsum(onehot, axis=0) - 1, eid[:, None], axis=1)[:, 0]
        valid = pos < C
        posc = jnp.minimum(pos, C - 1)
        Xrep = jnp.repeat(X, K, axis=0)
        xe = jnp.zeros((E, C, D), x.dtype).at[eid, posc].add(jnp.where(valid[:, None], Xrep, jnp.zeros((), x.dtype)))
        h = jax.nn.silu(jnp.einsum('ecd,edi->eci', xe, W1)) * jnp.einsum('ecd,edi->eci', xe, W3)
        ye = jnp.einsum('eci,eid->ecd', h, W2)
        gflat = jnp.where(valid, w.reshape(-1), jnp.zeros((), x.dtype))
        yrows = ye[eid, posc] * gflat[:, None]
        out = yrows.reshape(-1, K, D).sum(axis=1)
        out = out + jax.nn.silu(X @ sw1.T) * (X @ sw3.T) @ sw2.T
        return out.reshape(x.shape)

    def _L3_attn_ref(x, w_qkv, w_proj):
        import jax, jax.numpy as jnp
        import numpy as np
        N_HEADS = 16

        def _rotate_half(t):
            shp = t.shape
            t2 = t.reshape(*shp[:-1], shp[-1] // 2, 2)
            return jnp.stack((-t2[..., 1], t2[..., 0]), axis=-1).reshape(shp)
        B, N, D = x.shape
        H = N_HEADS
        hd = D // H
        qkv = x @ w_qkv
        qkv = qkv.reshape(B, N, 3, H, hd).transpose(2, 0, 3, 1, 4)
        q, k, v = (qkv[0], qkv[1], qkv[2])
        inv_freq = 1.0 / 10000.0 ** (jnp.arange(0, hd, 2, dtype=jnp.float32) / hd)
        freqs = jnp.arange(N, dtype=jnp.float32)[:, None] * inv_freq[None, :]
        sin = jnp.repeat(jnp.sin(freqs), 2, axis=-1)[None, None]
        cos = jnp.repeat(jnp.cos(freqs), 2, axis=-1)[None, None]
        q = q * cos + _rotate_half(q) * sin
        k = k * cos + _rotate_half(k) * sin
        scale = hd ** (-0.5)
        attn = jax.nn.softmax(jnp.einsum('bhqd,bhkd->bhqk', q, k) * scale, axis=-1)
        out = jnp.einsum('bhqk,bhkd->bhqd', attn, v)
        out = out.transpose(0, 2, 1, 3).reshape(B, N, D)
        return out @ w_proj

    def _L3_ffn_ref(x, norm_w, gate_w, gate_b, mlp1_w, mlp1_b, mlp2_w, mlp2_b):
        import jax, jax.numpy as jnp
        import numpy as np
        B, S, D = (2, 128, 128)
        E, K, I = (8, 2, 128)
        LIMIT = 7.0
        ALPHA = 1.702

        def _swiglu(t, limit):
            glu = jnp.minimum(t[..., ::2], limit)
            lin = jnp.clip(t[..., 1::2], -limit, limit)
            return glu * jax.nn.sigmoid(ALPHA * glu) * (lin + 1.0)
        eps = jnp.finfo(x.dtype).eps
        h = x * jax.lax.rsqrt(jnp.mean(x * x, axis=-1, keepdims=True) + eps) * norm_w
        flat = h.reshape(-1, D)
        logits = flat @ gate_w.T + gate_b
        vals, idx = jax.lax.top_k(logits, K)
        wts = jax.nn.softmax(vals, axis=-1)
        t1 = jnp.einsum('td,efd->tef', flat, mlp1_w) + mlp1_b
        act = _swiglu(t1, LIMIT)
        y = jnp.einsum('tei,edi->ted', act, mlp2_w) + mlp2_b
        sel = jnp.take_along_axis(y, idx[:, :, None], axis=1)
        out = jnp.sum(sel * wts[:, :, None], axis=1).reshape(x.shape)
        return x + out
    x = L0_attn_hidden_states
    x = x + _L0_attn_ref(_layernorm(x, axis=-1), L0_attn_Wq, L0_attn_Wk, L0_attn_Wv, L0_attn_Wb, L0_attn_conv_q_w, L0_attn_conv_k_w, L0_attn_conv_v_w, L0_attn_fir_short_w, L0_attn_fir_long_w, L0_attn_mlp_w1, L0_attn_mlp_b1, L0_attn_mlp_w2, L0_attn_mlp_b2, L0_attn_log_temp, L0_attn_o_norm_w, L0_attn_Wo)
    x = x + _L0_ffn_ref(_layernorm(x, axis=-1), L0_ffn_w_freq_real, L0_ffn_w_freq_imag, L0_ffn_bias)
    x = x + _L1_attn_ref(_layernorm(x, axis=-1), L1_attn_Wq, L1_attn_Wk, L1_attn_Wv, L1_attn_Wo)
    x = x + _L1_ffn_ref(_layernorm(x, axis=-1), L1_ffn_wqkv, L1_ffn_q_scale, L1_ffn_k_scale, L1_ffn_wo, L1_ffn_ln_g, L1_ffn_ln_b, L1_ffn_w1, L1_ffn_b1, L1_ffn_w2, L1_ffn_b2)
    x = x + _L2_attn_ref(_layernorm(x, axis=-1), L2_attn_W_qkv, L2_attn_qn_w, L2_attn_kn_w, L2_attn_W_out, L2_attn_b_out)
    x = x + _L2_ffn_ref(_layernorm(x, axis=-1), L2_ffn_gate_w, L2_ffn_bias, L2_ffn_W1, L2_ffn_W3, L2_ffn_W2, L2_ffn_sw1, L2_ffn_sw3, L2_ffn_sw2)
    x = x + _L3_attn_ref(_layernorm(x, axis=-1), L3_attn_w_qkv, L3_attn_w_proj)
    x = x + _L3_ffn_ref(_layernorm(x, axis=-1), L3_ffn_norm_w, L3_ffn_gate_w, L3_ffn_gate_b, L3_ffn_mlp1_w, L3_ffn_mlp1_b, L3_ffn_mlp2_w, L3_ffn_mlp2_b)
    return x

_drawn_inputs = setup_inputs


def setup_inputs(seed=0):
    import zlib

    import numpy as np

    out = dict(_drawn_inputs(seed))
    spreads = {'L0_attn_mlp_b1': (0.0, 0.8),
     'L0_attn_log_temp': (0.0, 0.8),
     'L0_attn_o_norm_w': (1.0, 0.2),
     'L1_ffn_q_scale': (1.0, 0.6),
     'L1_ffn_k_scale': (1.0, 0.6),
     'L1_ffn_ln_g': (1.0, 0.6),
     'L1_ffn_ln_b': (0.0, 0.8),
     'L1_ffn_b1': (0.0, 0.609),
     'L1_ffn_b2': (0.0, 0.1),
     'L2_attn_qn_w': (1.0, 0.6),
     'L2_attn_kn_w': (1.0, 0.6),
     'L2_attn_b_out': (0.0, 0.1),
     'L2_ffn_bias': (0.0, 0.8),
     'L3_ffn_norm_w': (1.0, 0.2),
     'L3_ffn_gate_b': (0.0, 0.1),
     'L3_ffn_mlp1_b': (0.0, 0.303),
     'L3_ffn_mlp2_b': (0.0, 0.351)}
    factors = {'L0_attn_Wb': 4.862,
     'L0_attn_mlp_w1': 8.0,
     'L0_attn_mlp_w2': 8.0,
     'L1_ffn_w1': 3.423,
     'L1_ffn_w2': 3.561,
     'L2_ffn_gate_w': 8.0,
     'L2_ffn_W1': 8.0,
     'L2_ffn_W3': 8.0,
     'L2_ffn_W2': 8.0,
     'L2_ffn_sw1': 8.0,
     'L2_ffn_sw3': 8.0,
     'L2_ffn_sw2': 8.0}
    for name, (base, spread) in spreads.items():
        noise = np.random.default_rng([zlib.crc32(name.encode()), seed]).standard_normal(out[name].shape)
        drawn = base * np.exp(spread * noise) if base else spread * noise
        out[name] = jnp.asarray(drawn.astype(out[name].dtype))
    for name, factor in factors.items():
        out[name] = (out[name] * factor).astype(out[name].dtype)
    return out
```

```python
from contextlib import ExitStack

import numpy as np

import concourse.bass as bass
from concourse import mybir

ALU = mybir.AluOpType
ACT = mybir.ActivationFunctionType
AX = mybir.AxisListType
F32 = mybir.dt.float32
BF16 = mybir.dt.bfloat16

P = 128
NSEQ = 8
SEQ = 512
TPS = SEQ // P
NT = NSEQ * TPS
TOK = NSEQ * SEQ
EPS = 1e-5

PHASES = (0, 1, 2, 3, 4, 5, 6, 7)


class Phase:

    def __init__(self, nc, ctx, name):
        self.nc, self.ctx, self.name, self.sems = nc, ctx, name, []

    def sb(self, name, shape, dt=F32):
        return self.ctx.enter_context(self.nc.sbuf_tensor(f"{self.name}_{name}", list(shape), dt))

    def ps(self, name, shape, dt=F32):
        return self.ctx.enter_context(self.nc.psum_tensor(f"{self.name}_{name}", list(shape), dt))

    def sem(self, name):
        self.sems.append(self.ctx.enter_context(self.nc.semaphore(f"{self.name}_{name}")))
        return self.sems[-1]


def at_least(engine, sem, n):
    if n > 0:
        engine.wait_ge(sem, n)


def clear(nc, sems):
    ids = sorted(s.num for s in sems)
    nc.gpsimd.sem_clear(range(ids[0], ids[-1] + 1))
    nc.all_engine_barrier()


def bcast(ap, n):
    return ap.unsqueeze(2).to_broadcast([ap.shape[0], ap.shape[1], n])


def cols(x, b, n=1):
    return x[:, bass.ds(b * SEQ, n * SEQ)]


def normalize(nc, xT, xnT, c, name, eps, center=True):
    U = 4
    with ExitStack() as ctx:
        ph = Phase(nc, ctx, name)
        sq, ln, rstd = (ph.sb(n, [P, U, SEQ]) for n in ("sq", "ln", "rstd"))
        epst = ph.sb("eps", [P, 1])
        ps_c, ps_v = (ph.ps(n, [P, U, SEQ]) for n in ("psc", "psv"))
        centered, squared, var_ready, logged, rstd_ready, normed, eps_set = (
            ph.sem(n) for n in ("centered", "squared", "var_ready", "logged", "rstd_ready", "normed", "eps_set"))
        ctx.callback(clear, nc, ph.sems)
        block = ctx.enter_context(nc.Block())

        @block.tensor
        def _(pe):
            pe.sem_inc(logged, U)
            with pe.Fori(0, NSEQ // U) as i:
                for j in range(U):
                    pe.wait_ge(normed, U * i + j + 1)
                    pe.matmul(ps_c[:, j, :], c["center" if center else "ident"][:], cols(xT, U * i + j), start=True,
                              stop=True).then_inc(centered, 1)
                for j in range(U):
                    pe.wait_ge(squared, U * i + j + 1)
                    pe.wait_ge(logged, U * i + j + 1)
                    pe.matmul(ps_v[:, j, :], c["mean"][:], sq[:, j, :], start=True, stop=True).then_inc(var_ready, 1)

        @block.scalar
        def _(act):
            act.wait_ge(eps_set, 1)
            with act.Fori(0, NSEQ // U) as i:
                for j in range(U):
                    act.wait_ge(centered, U * i + j + 1)
                    act.activation(sq[:, j, :], ps_c[:, j, :], ACT.Square).then_inc(squared, 1)
                for j in range(U):
                    act.wait_ge(var_ready, U * i + j + 1)
                    act.activation(ln[:, j, :], ps_v[:, j, :], ACT.Ln, bias=epst[:]).then_inc(logged, 1)
                act.drain()
                for j in range(U):
                    act.wait_ge(normed, U * i + j + 1)
                    act.activation(rstd[:, j, :], ln[:, j, :], ACT.Exp, scale=-0.5).then_inc(rstd_ready, 1)

        @block.vector
        def _(dve):
            dve.sem_inc(normed, U)
            dve.memset(epst[:], eps).then_inc(eps_set, 1)
            with dve.Fori(0, NSEQ // U) as i:
                for j in range(U):
                    dve.wait_ge(rstd_ready, U * i + j + 1)
                    dve.tensor_tensor(cols(xnT, U * i + j), ps_c[:, j, :], rstd[:, j, :], ALU.mult).then_inc(normed, 1)


def add_normed(nc, xT, xnT):
    with nc.Block() as block:
        half = TOK // 2

        @block.vector
        def _(dve):
            dve.tensor_tensor(xT[:, 0:half], xT[:, 0:half], xnT[:, 0:half], ALU.add)

        @block.gpsimd
        def _(pool):
            pool.tensor_tensor(xT[:, half:], xT[:, half:], xnT[:, half:], ALU.add)


def l0_attn(nc, xT, xnT, c, t):
    normalize(nc, xT, xnT, c, "l0an", EPS)
    with ExitStack() as outer:
        ph = Phase(nc, outer, "l0a")
        k, v = ph.sb("k", [P, TOK]), ph.sb("v", [P, TOK])
        heads, tri = ph.sb("heads", [P, L0_H]), ph.sb("tri", [P, 3, L0_C])
        loaded = ph.sem("loaded")
        with nc.Block() as block:
            @block.sync
            def _(sp):
                sp.dma_start(heads[:], t["heads4"]).then_inc(loaded, 16)
                sp.dma_start(tri[:], t["tri32"]).then_inc(loaded, 16)
                sp.wait_ge(loaded, 16 * 2)
        clear(nc, ph.sems)
        with ExitStack() as inner:
            ph = Phase(nc, inner, "l0d")
            q, att, tt = (ph.sb(n, [P, TOK]) for n in ("q", "att", "tt"))
            beta = ph.sb("beta", [P, NSEQ * L0_N])
            delta_inputs(nc, xnT, t, q, k, v, att, tt, beta, heads, tri)
            delta_inverse(nc, tt)
            delta_chunks(nc, q, k, v, att, tt, beta, heads, tri)
            s = ph.sb("s", [P, TOK])
            delta_scan(nc, att, tt, s, heads)
            delta_outputs(nc, q, k, s, heads)
        with ExitStack() as inner:
            ph = Phase(nc, inner, "l0m")
            short, long = ph.sb("short", [P, TOK]), ph.sb("long", [P, TOK])
            filters(nc, c, t, v, short, long)
            gated_mix(nc, xT, xnT, t, (short, long, k, v))


L0_H, L0_C = 4, 32
L0_N = SEQ // L0_C


def chunks(ap):
    return ap.rearrange("p (n d) -> p n d", d=L0_C)


def each_chunk(ap, n):
    return ap.unsqueeze(1).to_broadcast([P, n, L0_C])


def diagonal(engine, out, x, heads, n):
    return engine.tensor_tensor(out, x.unsqueeze(2).to_broadcast([P, n, L0_H, L0_C]),
                                heads[:].unsqueeze(1).unsqueeze(3).to_broadcast([P, n, L0_H, L0_C]), ALU.mult)


def delta_inputs(nc, xnT, t, q, k, v, att, tt, beta, heads, tri):
    H, C, N, TAPS = L0_H, L0_C, L0_N, 4
    with ExitStack() as ctx:
        ph = Phase(nc, ctx, "l0i")
        w, cw = ph.sb("w", [P, 4, P]), ph.sb("cw", [P, 3, TAPS])
        eps = ph.sb("eps", [P, 1])
        y = ph.sb("y", [P, 4, SEQ])
        yK = ph.sb("yk", [P, 3, SEQ])
        bt, kb = ph.sb("bt", [P, SEQ]), ph.sb("kb", [P, SEQ])
        sq = ph.sb("sq", [P, 2, SEQ])
        ss, rn = ph.sb("ss", [P, 2, N]), ph.sb("rn", [P, 2, N])
        kF, kbq = ph.sb("kf", [P, SEQ]), ph.sb("kbq", [P, 2, SEQ])
        kbd = ph.sb("kbd", [P, N, H, C])
        ps_p, ps_am = ph.ps("psp", [P, 4, SEQ]), ph.ps("psam", [P, 2, SEQ])
        (loaded, proj_ready, tapped, conv_ready, silu_ready, beta_ready, turned, squared, ss_ready, root_ready, kf_ready, kbd_ready, kbq_ready,
         am_ready, normed) = (ph.sem(n) for n in (
             "loaded", "proj_ready", "tapped", "conv_ready", "silu_ready", "beta_ready", "turned", "squared", "ss_ready", "root_ready",
             "kf_ready", "kbd_ready", "kbq_ready", "am_ready", "normed"))
        with nc.Block() as block:
            @block.sync
            def _(sp):
                for n, name in enumerate(("Wq", "Wk", "Wv", "Wb_wide")):
                    sp.dma_start(w[:, n, :], t[f"L0_attn_{name}"]).then_inc(loaded, 16)
                for n, name in enumerate(("q", "k", "v")):
                    sp.dma_start(cw[:, n, :], t[f"L0_attn_conv_{name}_w"]).then_inc(loaded, 16)
                sp.wait_ge(loaded, 16 * 7)

            @block.vector
            def _(dve):
                dve.memset(eps[:], 1e-6)
        clear(nc, ph.sems)

        def section(block, b):
            beta_b = beta[:, bass.ds(b * N, N)]

            @block.tensor
            def _(pe):
                for n in range(4):
                    pe.matmul(ps_p[:, n, :], w[:, n, :], cols(xnT, b), start=True, stop=True).then_inc(proj_ready, 1)
                pe.wait_ge(kbd_ready, H)
                pe.wait_ge(kbq_ready, 2)
                for n in range(N):
                    pe.matmul(ps_am[:, n // 8, (n % 8) * 2 * C:(n % 8 + 1) * 2 * C], kbd[:, n, :, :].rearrange("p h c -> p (h c)"),
                              kbq[:, :, n * C:(n + 1) * C], start=True, stop=True).then_inc(am_ready, 1)

            @block.scalar
            def _(act):
                for n in range(3):
                    act.wait_ge(proj_ready, n + 1)
                    act.activation(y[:, n, :], ps_p[:, n, :], ACT.Copy, scale=cw[:, n, TAPS - 1:TAPS]).then_inc(tapped, 1)
                act.wait_ge(proj_ready, 4)
                act.activation(y[:, 3, :], ps_p[:, 3, :], ACT.Sigmoid).then_inc(beta_ready, 1)
                for n in range(3):
                    act.wait_ge(conv_ready, n + 1)
                    act.activation(y[:, n, :], y[:, n, :], ACT.Silu).then_inc(silu_ready, 1)
                for n in range(2):
                    act.wait_ge(turned, n + 1)
                    act.activation(sq[:, n, :], yK[:, n, :], ACT.Square).then_inc(squared, 1)
                act.wait_ge(ss_ready, 2)
                act.activation(rn[:], ss[:], ACT.Sqrt, bias=eps[:]).then_inc(root_ready, 1)
                act.wait_ge(kf_ready, 1)
                for h in range(H):
                    act.activation(kbd[:, :, h, :], chunks(kF[:]), ACT.Copy, scale=heads[:, h:h + 1]).then_inc(kbd_ready, 1)

            @block.gpsimd
            def _(pool):
                pool.wait_ge(turned, 3)
                pool.tensor_copy(cols(v, b), yK[:, 2, :])
                pool.wait_ge(normed, 2)
                pool.tensor_copy(cols(k, b), yK[:, 1, :])
                pool.tensor_copy(cols(q, b), yK[:, 0, :])

            @block.vector
            def _(dve):
                for n in range(3):
                    dve.wait_ge(tapped, n + 1)
                    for s in range(1, TAPS):
                        stt = dve.scalar_tensor_tensor(out=y[:, n, s:], in0=ps_p[:, n, 0:SEQ - s], scalar=cw[:, n, TAPS - 1 - s:TAPS - s],
                                                       in1=y[:, n, s:], op0=ALU.mult, op1=ALU.add)
                        if s < TAPS - 1:
                            dve.drain()
                    stt.then_inc(conv_ready, 1)
                dve.wait_ge(beta_ready, 1)
                dve.transpose(bt[:], y[:, 3, :])
                dve.drain()
                dve.tensor_copy(beta_b.unsqueeze(2), chunks(bt[:])[:, :, 0:1])
                for n in range(3):
                    dve.wait_ge(silu_ready, n + 1)
                    dve.transpose(yK[:, n, :], y[:, n, :]).then_inc(turned, 1)
                for n in range(2):
                    dve.wait_ge(squared, n + 1)
                    dve.tensor_reduce(ss[:, n, :], chunks(sq[:, n, :]), AX.X, ALU.add).then_inc(ss_ready, 1)
                dve.wait_ge(root_ready, 1)
                dve.reciprocal(rn[:], rn[:])
                dve.drain()
                for n in (1, 0):
                    dve.tensor_tensor(chunks(yK[:, n, :]), chunks(yK[:, n, :]), bcast(rn[:, n, :], C), ALU.mult).then_inc(normed, 1)
                dve.drain()
                dve.transpose(kF[:], yK[:, 1, :]).then_inc(kf_ready, 1)
                dve.tensor_tensor(chunks(kb[:]), chunks(yK[:, 1, :]), bcast(beta_b, C), ALU.mult)
                dve.transpose(kbq[:, 1, :], yK[:, 0, :]).then_inc(kbq_ready, 1)
                dve.drain()
                dve.transpose(kbq[:, 0, :], kb[:]).then_inc(kbq_ready, 1)
                for r in range(2):
                    dve.wait_ge(am_ready, 8 * (r + 1))
                    both = ps_am[:, r, :].rearrange("p (n w d) -> p n w d", w=2, d=C)
                    dve.tensor_tensor(chunks(cols(tt, b))[:, 8 * r:8 * r + 8, :], both[:, :, 0, :], each_chunk(tri[:, 0, :], 8), ALU.mult)
                    dve.tensor_tensor(chunks(cols(att, b))[:, 8 * r:8 * r + 8, :], both[:, :, 1, :], each_chunk(tri[:, 1, :], 8), ALU.mult)

        with nc.Fori(0, NSEQ) as b:
            with nc.Block() as block:
                section(block, b)
            clear(nc, ph.sems)


def delta_inverse(nc, tt):
    H, C = L0_H, L0_C
    with ExitStack() as ctx:
        ph = Phase(nc, ctx, "l0t")
        a, x, tmp = (ph.sb(n, [P, H, C, C]) for n in ("a", "x", "tmp"))
        a_scratch = nc.dram_tensor("l0_a_scratch", (P, P, C), F32, kind="Internal").ap()
        t_scratch = nc.dram_tensor("l0_t_scratch", (P, P, C), F32, kind="Internal").ap()
        a_stored, a_loaded, t_stored, t_loaded, solved = (ph.sem(n) for n in ("a_stored", "a_loaded", "t_stored", "t_loaded", "solved"))
        ctx.callback(clear, nc, ph.sems)
        block = ctx.enter_context(nc.Block())
        shares = {"dve": (0, 3), "pool": (3, 4)}

        def solve(engine, lo, hi):
            n = hi - lo
            xs = x[:, lo:hi]
            engine.memset(xs, 0.0)
            engine.drain()
            engine.memset(xs.rearrange("p h c i -> p h (c i)")[:, :, 0:C * C:C + 1], 1.0)
            engine.drain()
            engine.wait_ge(a_loaded, 16 * H)
            for j in range(C - 1):
                rows, rest = j + 1, C - 1 - j
                m = tmp[:, lo:hi, 0:rows, 0:rest]
                engine.tensor_tensor(m, a[:, lo:hi, j:j + 1, j + 1:].to_broadcast([P, n, rows, rest]),
                                     xs[:, :, 0:rows, j:j + 1].to_broadcast([P, n, rows, rest]), ALU.mult)
                engine.drain()
                engine.tensor_tensor(xs[:, :, 0:rows, j + 1:], xs[:, :, 0:rows, j + 1:], m, ALU.subtract)
                engine.drain()
            engine.sem_inc(solved, 1)

        @block.sync
        def _(sp):
            sp.dma_start(a_scratch, tt[:].rearrange("p (n i) -> p n i", i=C)).then_inc(a_stored, 16)
            sp.wait_ge(a_stored, 16)
            for h in range(H):
                sp.dma_start(a[:, h], a_scratch[h * C:(h + 1) * C].rearrange("j n i -> n j i")).then_inc(a_loaded, 16)
            sp.wait_ge(a_loaded, 16 * H)
            sp.wait_ge(solved, 2)
            sp.dma_start(t_scratch, x[:].rearrange("p h c i -> p (h c) i")).then_inc(t_stored, 16)
            sp.wait_ge(t_stored, 16)
            for h in range(H):
                sp.dma_start(tt[h * C:(h + 1) * C].rearrange("p (n i) -> p n i", i=C),
                             t_scratch[:, h * C:(h + 1) * C].rearrange("n c i -> c n i")).then_inc(t_loaded, 16)
            sp.wait_ge(t_loaded, 16 * H)

        @block.vector
        def _(dve):
            solve(dve, *shares["dve"])

        @block.gpsimd
        def _(pool):
            solve(pool, *shares["pool"])


def delta_chunks(nc, q, k, v, att, tt, beta, heads, tri):
    H, C, N = L0_H, L0_C, L0_N
    with ExitStack() as ctx:
        ph = Phase(nc, ctx, "l0c")
        vk, uw = ph.sb("vk", [P, N, 2, C]), ph.sb("uw", [P, N, 2, C])
        tbd, kbd, abd = (ph.sb(n, [P, N, H, C]) for n in ("tbd", "kbd", "abd"))
        qp, qpT, kw, kwT = (ph.sb(n, [P, SEQ]) for n in ("qp", "qpt", "kw", "kwt"))
        ps_uw, ps_k, ps_a = (ph.ps(n, [P, 2, SEQ]) for n in ("psuw", "psk", "psa"))
        vk_ready, tbd_ready, kbd_ready, abd_ready, uw_done, uw_ready, k_done, a_done, q_turned = (ph.sem(n) for n in (
            "vk_ready", "tbd_ready", "kbd_ready", "abd_ready", "uw_done", "uw_ready", "k_done", "a_done", "q_turned"))
        flat = lambda x, n: x[:, n, :, :].rearrange("p h c -> p (h c)")
        half = lambda ps, r: ps[:, r, :].rearrange("p (n w d) -> p n w d", w=2, d=C)
        place = lambda n: (slice(None), n // 8, slice((n % 8) * 2 * C, (n % 8 + 1) * 2 * C))

        def section(block, b):
            beta_b = beta[:, bass.ds(b * N, N)]
            at = lambda x, r: chunks(cols(x, b))[:, 8 * r:8 * r + 8, :]

            @block.tensor
            def _(pe):
                pe.wait_ge(vk_ready, 2)
                pe.wait_ge(tbd_ready, H)
                for n in range(N):
                    pe.matmul(ps_uw[place(n)], flat(tbd, n), vk[:, n, :, :], start=True, stop=True).then_inc(uw_done, 1)
                pe.wait_ge(kbd_ready, 1)
                for n in range(N):
                    if n % 8 == 0:
                        pe.wait_ge(uw_ready, n // 8 + 1)
                    pe.matmul(ps_k[place(n)], flat(kbd, n), uw[:, n, :, :], start=True, stop=True).then_inc(k_done, 1)
                pe.wait_ge(abd_ready, 1)
                for n in range(N):
                    pe.matmul(ps_a[place(n)], flat(abd, n), uw[:, n, :, :], start=True, stop=True).then_inc(a_done, 1)

            @block.scalar
            def _(act):
                for h in range(H):
                    act.activation(tbd[:, :, h, :], chunks(cols(tt, b)), ACT.Copy, scale=heads[:, h:h + 1]).then_inc(tbd_ready, 1)
                for r in range(2):
                    act.wait_ge(uw_done, 8 * (r + 1))
                    act.copy(uw[:, 8 * r:8 * r + 8, :, :], half(ps_uw, r)).then_inc(uw_ready, 1)
                act.wait_ge(q_turned, 1)
                act.copy(cols(q, b), qpT[:])

            @block.gpsimd
            def _(pool):
                diagonal(pool, kbd[:], chunks(cols(k, b)), heads, N).then_inc(kbd_ready, 1)

            @block.vector
            def _(dve):
                dve.tensor_tensor(vk[:, :, 0, :], chunks(cols(v, b)), bcast(beta_b, C), ALU.mult).then_inc(vk_ready, 1)
                dve.tensor_tensor(vk[:, :, 1, :], chunks(cols(k, b)), bcast(beta_b, C), ALU.mult).then_inc(vk_ready, 1)
                diagonal(dve, abd[:], chunks(cols(att, b)), heads, N).then_inc(abd_ready, 1)
                for r in range(2):
                    dve.wait_ge(k_done, 8 * (r + 1))
                    if r == 0:
                        dve.drain()
                    dve.tensor_copy(at(att, r), half(ps_k, r)[:, :, 0, :])
                    dve.tensor_copy(chunks(kw[:])[:, 8 * r:8 * r + 8, :], half(ps_k, r)[:, :, 1, :])
                dve.drain()
                dve.transpose(kwT[:], kw[:])
                dve.drain()
                dve.tensor_tensor(chunks(cols(tt, b)), each_chunk(tri[:, 2, :], N), chunks(kwT[:]), ALU.subtract)
                for r in range(2):
                    dve.wait_ge(a_done, 8 * (r + 1))
                    dve.tensor_copy(at(k, r), half(ps_a, r)[:, :, 0, :])
                    dve.tensor_tensor(chunks(qp[:])[:, 8 * r:8 * r + 8, :], at(q, r), half(ps_a, r)[:, :, 1, :], ALU.subtract)
                dve.drain()
                dve.transpose(qpT[:], qp[:]).then_inc(q_turned, 1)

        with nc.Fori(0, NSEQ) as b:
            with nc.Block() as block:
                section(block, b)
            clear(nc, ph.sems)


def delta_scan(nc, bs, ms, s, heads):
    H, C, N = L0_H, L0_C, L0_N
    with ExitStack() as ctx:
        ph = Phase(nc, ctx, "l0s")
        mbd = ph.sb("mbd", [P, 2, NSEQ, H, C])
        ps = ph.ps("ps", [P, 2, SEQ])
        mbd_ready, ms_done, s_ready = (ph.sem(n) for n in ("mbd_ready", "ms_done", "s_ready"))
        at = lambda x, n: x[:].rearrange("p (b n d) -> p b n d", n=N, d=C)[:, :, n, :]
        ctx.callback(clear, nc, ph.sems)
        block = ctx.enter_context(nc.Block())

        @block.gpsimd
        def _(pool):
            for n in range(N - 1):
                at_least(pool, ms_done, n - 1)
                diagonal(pool, mbd[:, n % 2], at(ms, n), heads, NSEQ).then_inc(mbd_ready, 1)

        @block.tensor
        def _(pe):
            for n in range(N - 1):
                pe.wait_ge(mbd_ready, n + 1)
                pe.wait_ge(s_ready, n + 1)
                for b in range(NSEQ):
                    mm = pe.matmul(ps[:, n % 2, b * C:(b + 1) * C], mbd[:, n % 2, b, :, :].rearrange("p h c -> p (h c)"),
                                   at(s, n)[:, b, :], start=True, stop=True)
                mm.then_inc(ms_done, 1)

        @block.vector
        def _(dve):
            dve.memset(at(s, 0), 0.0).then_inc(s_ready, 1)
            for n in range(N - 1):
                dve.wait_ge(ms_done, n + 1)
                dve.tensor_tensor(at(s, n + 1), ps[:, n % 2, 0:NSEQ * C].rearrange("p (b d) -> p b d", d=C), at(bs, n),
                                  ALU.add).then_inc(s_ready, 1)


def delta_outputs(nc, q, o, s, heads):
    H, C, N = L0_H, L0_C, L0_N
    with ExitStack() as ctx:
        ph = Phase(nc, ctx, "l0o")
        qbd = ph.sb("qbd", [P, 2, N, H, C])
        ps = ph.ps("ps", [P, 2, SEQ])
        qbd_ready, o_done = (ph.sem(n) for n in ("qbd_ready", "o_done"))

        def section(block, b):
            @block.scalar
            def _(act):
                for h in range(H):
                    act.activation(qbd[:, 0, :, h, :], chunks(cols(q, b)), ACT.Copy, scale=heads[:, h:h + 1]).then_inc(qbd_ready, 1)

            @block.gpsimd
            def _(pool):
                diagonal(pool, qbd[:, 1], chunks(cols(q, b + 1)), heads, N).then_inc(qbd_ready, H)

            @block.tensor
            def _(pe):
                pe.wait_ge(qbd_ready, 2 * H)
                for r in range(2):
                    for n in range(N):
                        pe.matmul(ps[:, r, n * C:(n + 1) * C], qbd[:, r, n, :, :].rearrange("p h c -> p (h c)"),
                                  cols(s, b + r)[:, n * C:(n + 1) * C], start=True, stop=True).then_inc(o_done, 1)

            @block.vector
            def _(dve):
                for r in range(2):
                    dve.wait_ge(o_done, N * (r + 1))
                    dve.tensor_tensor(cols(o, b + r), cols(o, b + r), ps[:, r, :], ALU.add)

        with nc.Fori(0, NSEQ // 2) as i:
            with nc.Block() as block:
                section(block, 2 * i)
            clear(nc, ph.sems)


def filters(nc, c, t, v, short, long):
    C, SHORT, LONG = L0_C, 5, 64
    PE_TAPS, POOL_TAPS = 26, 11
    pe_taps = range(PE_TAPS)
    pool_taps = range(PE_TAPS, PE_TAPS + POOL_TAPS)
    dve_taps = range(PE_TAPS + POOL_TAPS, LONG)
    with ExitStack() as ctx:
        ph = Phase(nc, ctx, "l0r")
        ws, wl = ph.sb("ws", [P, SHORT]), ph.sb("wl", [P, LONG])
        vF = ph.sb("vf", [P, NSEQ, LONG + SEQ])
        acc, pacc, ptmp = (ph.sb(n, [P, NSEQ, SEQ]) for n in ("acc", "pacc", "ptmp"))
        diag = ph.sb("diag", [P, PE_TAPS, P])
        ps = ph.ps("ps", [P, NSEQ, SEQ])
        loaded, v_ready, diag_ready, pe_done, pool_done = (ph.sem(n) for n in ("loaded", "v_ready", "diag_ready", "pe_done", "pool_done"))
        ctx.callback(clear, nc, ph.sems)
        block = ctx.enter_context(nc.Block())
        shifted = lambda s: vF[:, :, LONG - s:LONG - s + SEQ]
        wide = lambda x: x[:].rearrange("p b s -> p (b s)")

        @block.sync
        def _(sp):
            sp.dma_start(ws[:], t["L0_attn_fir_short_wp"]).then_inc(loaded, 16)
            sp.dma_start(wl[:], t["L0_attn_fir_long_wp"]).then_inc(loaded, 16)

        @block.scalar
        def _(act):
            act.wait_ge(loaded, 32)
            for j in pe_taps:
                act.activation(diag[:, j, :], c["ident"][:], ACT.Copy, scale=wl[:, j:j + 1]).then_inc(diag_ready, 1)

        @block.tensor
        def _(pe):
            pe.wait_ge(v_ready, 1)
            for j in pe_taps:
                pe.wait_ge(diag_ready, j + 1)
                for b in range(NSEQ):
                    mm = pe.matmul(ps[:, b, :], diag[:, j, :], shifted(LONG - 1 - j)[:, b, :], start=(j == 0), stop=(j == PE_TAPS - 1))
            mm.then_inc(pe_done, 1)

        @block.gpsimd
        def _(pool):
            pool.wait_ge(loaded, 32)
            pool.wait_ge(v_ready, 1)
            for n, j in enumerate(pool_taps):
                out = pacc if n == 0 else ptmp
                pool.tensor_scalar(out[:], shifted(LONG - 1 - j), wl[:, j:j + 1], None, ALU.mult)
                pool.drain()
                if n:
                    pool.tensor_tensor(pacc[:], pacc[:], ptmp[:], ALU.add)
                    pool.drain()
            pool.sem_inc(pool_done, 1)

        @block.vector
        def _(dve):
            dve.memset(vF[:, :, 0:LONG], 0.0)
            for b in range(NSEQ):
                dve.transpose(vF[:, b, LONG:], cols(v, b))
            dve.drain().then_inc(v_ready, 1)
            dve.wait_ge(loaded, 32)

            def fir(w, taps, total):
                for n, j in enumerate(taps):
                    if n == 0:
                        dve.tensor_scalar(acc[:], shifted(total - 1 - j), w[:, j:j + 1], None, ALU.mult)
                    else:
                        dve.scalar_tensor_tensor(out=acc[:], in0=shifted(total - 1 - j), scalar=w[:, j:j + 1], in1=acc[:], op0=ALU.mult,
                                                 op1=ALU.add)
                    dve.drain()

            fir(ws, range(SHORT), SHORT)
            dve.transpose(short[:], wide(acc))
            dve.drain()
            fir(wl, dve_taps, LONG)
            dve.wait_ge(pool_done, 1)
            dve.tensor_tensor(acc[:], acc[:], pacc[:], ALU.add)
            dve.drain()
            dve.wait_ge(pe_done, 1)
            dve.tensor_tensor(acc[:], acc[:], ps[:], ALU.add)
            dve.drain()
            dve.transpose(long[:], wide(acc))


def gated_mix(nc, xT, xnT, t, branches):
    H, C, N = L0_H, L0_C, L0_N
    FLOOR = 0.05
    with ExitStack() as ctx:
        ph = Phase(nc, ctx, "l0g")
        w1a, w1b, w2, wo = ph.sb("w1a", [P, P]), ph.sb("w1b", [P, P]), ph.sb("w2", [P, C]), ph.sb("wo", [P, P])
        b1, b2, temp, onorm, eps = (ph.sb(n, [P, 1]) for n in ("b1", "b2", "temp", "onorm", "eps"))
        xc, sq, ab = (ph.sb(n, [P, 4, SEQ]) for n in ("xc", "sq", "ab"))
        mean, sumc, sums, sumsq = (ph.sb(n, [P, 4, N]) for n in ("mean", "sumc", "sums", "sumsq"))
        st, stF = ph.sb("st", [P, N, C]), ph.sb("stf", [P, SEQ])
        h1 = ph.sb("h1", [P, 2, SEQ])
        lg, lgK = ph.sb("lg", [P, SEQ]), ph.sb("lgk", [P, N, C])
        pr = ph.sb("pr", [P, N, 4])
        m, r = ph.sb("m", [P, N]), ph.sb("r", [P, N])
        mix, mix2 = ph.sb("mix", [P, SEQ]), ph.sb("mix2", [P, SEQ])
        oF = ph.sb("of", [P, SEQ])
        ps_h, ps_l, ps_y = ph.ps("psh", [P, 2, SEQ]), ph.ps("psl", [P, SEQ]), ph.ps("psy", [P, SEQ])
        (loaded, mean_ready, centered, absed, squared, sumsq_ready, st_ready, h_ready, h1_ready, l_done, lg_ready, exp_ready, pr_ready, mix_ready,
         mix_added, mix_squared, rms_ready, root_ready, turned, o_ready, y_ready) = (ph.sem(n) for n in (
             "loaded", "mean_ready", "centered", "absed", "squared", "sumsq_ready", "st_ready", "h_ready", "h1_ready", "l_done", "lg_ready",
             "exp_ready", "pr_ready", "mix_ready", "mix_added", "mix_squared", "rms_ready", "root_ready", "turned", "o_ready", "y_ready"))
        with nc.Block() as block:
            @block.sync
            def _(sp):
                loads = ((w1a, "w1a"), (w1b, "w1b"), (w2, "w2p"), (wo, "Wo"), (b1, "b1"), (b2, "b2p"), (temp, "temp"), (onorm, "onorm"))
                for dst, name in loads:
                    sp.dma_start(dst[:], t[f"L0_attn_{name}"]).then_inc(loaded, 16)
                sp.wait_ge(loaded, 16 * len(loads))

            @block.scalar
            def _(act):
                act.wait_ge(loaded, 16 * 8)
                act.activation(temp[:], temp[:], ACT.Exp, scale=-1.0)

            @block.vector
            def _(dve):
                dve.memset(eps[:], EPS)
                dve.memset(st[:], 0.0)
        clear(nc, ph.sems)

        def section(block, b):
            stats = st[:, :, 0:16].rearrange("p n (x s) -> p x s n", s=4)

            @block.tensor
            def _(pe):
                def gate(h):
                    pe.wait_ge(h1_ready, h + 1)
                    pe.matmul(ps_l[h * C:(h + 1) * C, :], w2[:], h1[:, h % 2, :], start=True, stop=True).then_inc(l_done, 1)

                for h in range(H):
                    at_least(pe, h1_ready, h - 1)
                    pe.matmul(ps_h[:, h % 2, :], w1a[:], cols(xnT, b), start=True, stop=False)
                    pe.wait_ge(st_ready, 1)
                    pe.matmul(ps_h[:, h % 2, :], w1b[h * C:(h + 1) * C, :], stF[h * C:(h + 1) * C, :], start=False, stop=True,
                              tile_position=(h * C, 0)).then_inc(h_ready, 1)
                    if h:
                        gate(h - 1)
                gate(H - 1)
                pe.wait_ge(o_ready, 1)
                pe.matmul(ps_y[:], wo[:], oF[:], start=True, stop=True).then_inc(y_ready, 1)

            @block.scalar
            def _(act):
                for n, x in enumerate(branches):
                    act.activation(ab[:, n, :], cols(x, b), ACT.Abs).then_inc(absed, 1)
                for n in range(4):
                    act.wait_ge(centered, n + 1)
                    act.activation(sq[:, n, :], xc[:, n, :], ACT.Square).then_inc(squared, 1)
                act.wait_ge(sumsq_ready, 1)
                act.activation(stats[:, :, 3, :], sumsq[:], ACT.Sqrt).then_inc(root_ready, 1)
                for h in range(H):
                    act.wait_ge(h_ready, h + 1)
                    at_least(act, l_done, h - 1)
                    act.activation(h1[:, h % 2, :], ps_h[:, h % 2, :], ACT.Gelu, bias=b1[:]).then_inc(h1_ready, 1)
                act.wait_ge(lg_ready, 1)
                act.activation(pr[:], pr[:], ACT.Exp).then_inc(exp_ready, 1)
                act.wait_ge(mix_ready, 1)
                act.activation(sq[:, 0, :], mix[:], ACT.Square).then_inc(mix_squared, 1)
                act.wait_ge(rms_ready, 1)
                act.activation(r[:], m[:], ACT.Sqrt, scale=1.0 / C, bias=eps[:]).then_inc(root_ready, 1)
                act.wait_ge(turned, 1)
                act.activation(oF[:], lg[:], ACT.Copy, scale=onorm[:]).then_inc(o_ready, 1)

            @block.gpsimd
            def _(pool):
                for n, x in enumerate(branches):
                    pool.wait_ge(mean_ready, n + 1)
                    pool.tensor_tensor(chunks(xc[:, n, :]), chunks(cols(x, b)), bcast(mean[:, n, :], C), ALU.subtract).then_inc(centered, 1)
                pool.wait_ge(pr_ready, 1)
                pool.wait_ge(squared, 4)
                pool.tensor_tensor(chunks(xc[:, 3, :]), chunks(cols(branches[3], b)), bcast(pr[:, :, 3], C), ALU.mult).then_inc(mix_added, 1)

            @block.vector
            def _(dve):
                for n, x in enumerate(branches):
                    dve.tensor_reduce(sums[:, n, :], chunks(cols(x, b)), AX.X, ALU.add)
                    dve.drain()
                    dve.tensor_scalar(mean[:, n, :], sums[:, n, :], 1.0 / C, None, ALU.mult).then_inc(mean_ready, 1)
                dve.drain()
                dve.tensor_copy(stats[:, :, 0, :], mean[:])
                for n in range(4):
                    dve.wait_ge(absed, n + 1)
                    dve.tensor_reduce(sums[:, n, :], chunks(ab[:, n, :]), AX.X, ALU.add)
                dve.drain()
                dve.tensor_scalar(stats[:, :, 2, :], sums[:], 1.0 / C, None, ALU.mult)
                for n in range(4):
                    dve.wait_ge(squared, n + 1)
                    dve.tensor_reduce(sumc[:, n, :], chunks(sq[:, n, :]), AX.X, ALU.add)
                dve.drain()
                dve.tensor_scalar(stats[:, :, 1, :], sumc[:], 1.0 / C, None, ALU.mult)
                dve.tensor_tensor(sumsq[:], mean[:], mean[:], ALU.mult)
                dve.drain()
                dve.scalar_tensor_tensor(out=sumsq[:], in0=sumsq[:], scalar=float(C), in1=sumc[:], op0=ALU.mult,
                                         op1=ALU.add).then_inc(sumsq_ready, 1)
                dve.wait_ge(root_ready, 1)
                dve.drain()
                dve.transpose(stF[:], st[:].rearrange("p n c -> p (n c)")).then_inc(st_ready, 1)
                dve.wait_ge(l_done, H)
                dve.tensor_scalar(lg[:], ps_l[:], b2[:], temp[:], ALU.add, ALU.mult)
                dve.drain()
                dve.transpose(lgK[:].rearrange("p n c -> p (n c)"), lg[:])
                dve.drain()
                dve.tensor_reduce(m[:], lgK[:, :, 0:4], AX.X, ALU.max)
                dve.drain()
                dve.tensor_tensor(pr[:], lgK[:, :, 0:4], bcast(m[:], 4), ALU.subtract).then_inc(lg_ready, 1)
                dve.wait_ge(exp_ready, 1)
                dve.tensor_reduce(m[:], pr[:], AX.X, ALU.add)
                dve.drain()
                dve.reciprocal(m[:], m[:])
                dve.drain()
                dve.tensor_tensor(pr[:], pr[:], bcast(m[:], 4), ALU.mult)
                dve.drain()
                dve.tensor_scalar(pr[:], pr[:], 1.0 - 4 * FLOOR, FLOOR, ALU.mult, ALU.add)
                dve.drain().then_inc(pr_ready, 1)
                dve.tensor_tensor(chunks(mix[:]), chunks(cols(branches[0], b)), bcast(pr[:, :, 0], C), ALU.mult)
                for n in (1, 2):
                    dve.tensor_tensor(chunks(mix2[:]), chunks(cols(branches[n], b)), bcast(pr[:, :, n], C), ALU.mult)
                    dve.drain()
                    dve.tensor_tensor(mix[:], mix[:], mix2[:], ALU.add)
                    dve.drain()
                dve.wait_ge(mix_added, 1)
                dve.tensor_tensor(mix[:], mix[:], xc[:, 3, :], ALU.add).then_inc(mix_ready, 1)
                dve.wait_ge(mix_squared, 1)
                dve.tensor_reduce(m[:], chunks(sq[:, 0, :]), AX.X, ALU.add).then_inc(rms_ready, 1)
                dve.wait_ge(root_ready, 2)
                dve.reciprocal(r[:], r[:])
                dve.drain()
                dve.tensor_tensor(chunks(mix[:]), chunks(mix[:]), bcast(r[:], C), ALU.mult)
                dve.drain()
                dve.transpose(lg[:], mix[:]).then_inc(turned, 1)
                dve.wait_ge(y_ready, 1)
                dve.tensor_tensor(cols(xT, b), cols(xT, b), ps_y[:], ALU.add)

        with nc.Fori(0, NSEQ) as b:
            with nc.Block() as block:
                section(block, b)
            clear(nc, ph.sems)


def l0_ffn(nc, xT, xnT, c, t):
    normalize(nc, xT, xnT, c, "l0fn", EPS)
    with ExitStack() as ctx:
        ph = Phase(nc, ctx, "l0f")
        wr, wi, cs, sn, csd, snd, snn = (ph.sb(n, [P, P]) for n in ("wr", "wi", "cs", "sn", "csd", "snd", "snn"))
        bias = ph.sb("bias", [P, 1])
        gt, ht, m = (ph.sb(n, [P, P]) for n in ("gt", "ht", "m"))
        ps_m = ph.ps("psm", [P, 2, P])
        ps_y = ph.ps("psy", [P, 2, SEQ])
        loaded, gh_ready, gh_copied, m_ready, m_copied, y_ready, x_done = (
            ph.sem(n) for n in ("loaded", "gh_ready", "gh_copied", "m_ready", "m_copied", "y_ready", "x_done"))
        ctx.callback(clear, nc, ph.sems)
        block = ctx.enter_context(nc.Block())

        @block.sync
        def _(sp):
            for dst, src in ((wr, t["L0_ffn_w_freq_real"]), (wi, t["L0_ffn_w_freq_imag"]), (cs, t["dft"][0]),
                             (sn, t["dft"][1]), (csd, t["dft"][2]), (snd, t["dft"][3]), (snn, t["dft"][4]),
                             (bias, t["L0_ffn_bias"].unsqueeze(1))):
                sp.dma_start(dst[:], src).then_inc(loaded, 16)

        @block.tensor
        def _(pe):
            pe.wait_ge(loaded, 16 * 8)
            pe.matmul(ps_m[:, 0, :], wr[:], cs[:], start=True, stop=False)
            pe.matmul(ps_m[:, 0, :], wi[:], sn[:], start=False, stop=True)
            pe.matmul(ps_m[:, 1, :], wi[:], cs[:], start=True, stop=False)
            pe.matmul(ps_m[:, 1, :], wr[:], snn[:], start=False, stop=True).then_inc(gh_ready, 1)
            pe.wait_ge(gh_copied, 2)
            pe.matmul(ps_m[:, 0, :], gt[:], csd[:], start=True, stop=False)
            pe.matmul(ps_m[:, 0, :], ht[:], snd[:], start=False, stop=True).then_inc(m_ready, 1)
            pe.wait_ge(m_copied, 1)
            with pe.Fori(0, NSEQ // 2) as i:
                pe.wait_ge(x_done, 2 * i + 1)
                for j in range(2):
                    pe.matmul(ps_y[:, j, :], m[:], cols(xnT, 2 * i + j), start=True, stop=True).then_inc(y_ready, 1)

        @block.scalar
        def _(act):
            act.wait_ge(gh_ready, 1)
            act.copy(gt[:], ps_m[:, 0, :]).then_inc(gh_copied, 1)
            act.copy(ht[:], ps_m[:, 1, :]).then_inc(gh_copied, 1)
            act.wait_ge(m_ready, 1)
            act.copy(m[:], ps_m[:, 0, :]).then_inc(m_copied, 1)

        @block.vector
        def _(dve):
            dve.sem_inc(x_done, 1)
            dve.wait_ge(loaded, 16 * 8)
            with dve.Fori(0, NSEQ // 2) as i:
                for j in range(2):
                    dve.wait_ge(y_ready, 2 * i + j + 1)
                    dve.scalar_tensor_tensor(out=cols(xT, 2 * i + j), in0=ps_y[:, j, :], scalar=bias[:], in1=cols(xT, 2 * i + j),
                                             op0=ALU.add, op1=ALU.add).then_inc(x_done, 1)


def attention(nc, xT, xnT, c, t, name, wq, wk, wv, wo, causal, rope):
    normalize(nc, xT, xnT, c, name + "n", EPS)
    H, D, PARTS = 16, 8, 3
    QPART = (0, 1, 0, 2, 0, 1)
    KPART = (0, 0, 1, 0, 2, 1)
    ROWS = 96
    MAXROWS = 2
    SCALE = float(D) ** -0.5
    projections = ["q", "qs", "k", "ks", "v"] if rope else ["q", "k", "v"]
    NPROJ = len(projections)
    V_AT, FIN_FROM, A_FROM, A_TO, PROJECT_FROM = 1, 2, 2, 15, 7
    a_upto = lambda h, kt: ((h - A_FROM) * TPS + kt) * H // (A_TO - A_FROM)
    width = lambda n: (TPS - n) * P if causal else SEQ
    kts = lambda qt: range(qt + 1) if causal else range(TPS)
    with ExitStack() as ctx:
        ph = Phase(nc, ctx, name)
        w = {n: ph.sb("w" + n, [P, P]) for n in projections}
        wo_sb = ph.sb("wo", [P, P])
        if rope:
            cos, sin = ph.sb("cos", [P, SEQ]), ph.sb("sin", [P, SEQ])
        identb = ph.sb("identb", [P, P], BF16)
        maskq, maskk = ph.sb("maskq", [P, P]), ph.sb("maskk", [P, P])
        maskqb, maskkb = ph.sb("maskqb", [P, P], BF16), ph.sb("maskkb", [P, P], BF16)
        full = ph.sb("full", [P, 2, SEQ])
        rot = ph.sb("rot", [P, SEQ])
        parts = ph.sb("parts", [P, 2 * PARTS, SEQ], BF16)
        xb = ph.sb("xb", [P, SEQ])
        qst, kst = (ph.sb(n, [ROWS + MAXROWS, 2, H, SEQ], BF16) for n in ("qst", "kst"))
        v = ph.sb("v", [P, 2, TPS, H // 2, 2, 4, D])
        pt = ph.sb("pt", [P, 2, TPS, SEQ])
        mx = ph.sb("mx", [P, TPS, H])
        negmax = ph.sb("negmax", [H, SEQ])
        nm = ph.sb("nm", [H, MAXROWS, SEQ], BF16)
        rsum = ph.sb("rsum", [P, TPS, H])
        sums = ph.sb("sums", [P, 2, SEQ])
        o = ph.sb("o", [P, TPS, H, D])
        oT = ph.sb("oT", [P, SEQ])
        scratch = nc.dram_tensor(f"{name}_scratch", (2, P, 2 * PARTS, SEQ), BF16, kind="Internal").ap()
        max_scratch = nc.dram_tensor(f"{name}_max_scratch", (2, H, MAXROWS, SEQ), BF16, kind="Internal").ap()
        max_stored = ph.sem("max_stored")
        ps_m = ph.ps("psm", [P, SEQ])
        ps_a = ph.ps("psa", [P, 2, SEQ])
        ps_s = ph.ps("pss", [P, 2, SEQ])
        ps_o = ph.ps("pso", [P, 2, SEQ])
        (loaded, filled, emptied, xb_ready, full_ready, full_taken, v_ready, parts_ready, parts_stored, stacked, a_ready, a_taken,
         maxed, nm_ready, max_stacked, s_ready, exped, pv_done, o_ready, sums_ready) = (
            ph.sem(n) for n in ("loaded", "filled", "emptied", "xb_ready", "full_ready", "full_taken", "v_ready", "parts_ready",
                                "parts_stored", "stacked", "a_ready", "a_taken", "maxed", "nm_ready", "max_stacked",
                                "s_ready", "exped", "pv_done", "o_ready", "sums_ready"))
        NLOAD = NPROJ + 1 + 2 + (2 if rope else 0)


        with nc.Block() as block:
            @block.sync
            def _(sp):
                src = {"q": wq, "k": wk, "v": wv}
                if rope:
                    src.update(qs=t["L3_attn_w_swapped"][:, 0, :], ks=t["L3_attn_w_swapped"][:, 1, :])
                    sp.dma_start(cos[:], t["rope8"][0]).then_inc(loaded, 16)
                    sp.dma_start(sin[:], t["rope8"][1]).then_inc(loaded, 16)
                for n in projections:
                    sp.dma_start(w[n][:], src[n]).then_inc(loaded, 16)
                sp.dma_start(wo_sb[:], wo).then_inc(loaded, 16)
                sp.dma_start(maskq[:], t["causal"][0]).then_inc(loaded, 16)
                sp.dma_start(maskk[:], t["causal"][1]).then_inc(loaded, 16)
                sp.wait_ge(loaded, 16 * NLOAD)

            @block.scalar
            def _(act):
                act.wait_ge(loaded, 16 * NLOAD)
                act.copy(identb[:], c["ident"][:])
                act.copy(maskqb[:], maskq[:])
                act.copy(maskkb[:], maskk[:])
                act.copy(kst[ROWS:, 1, :, :].rearrange("p h (k q) -> p (h k) q", q=P), c["ones"][ROWS:ROWS + MAXROWS, :].unsqueeze(1).to_broadcast([MAXROWS, H * TPS, P]))

            @block.vector
            def _(dve):
                dve.memset(v[:], 0.0)
                dve.drain()
                for e in range(2):
                    dve.memset(v[:, :, :, :, e, 2 * e + 1, :], 1.0)
                dve.memset(qst[0:ROWS, :, :, :].bitcast(F32), 0.0)

            @block.gpsimd
            def _(pool):
                pool.memset(kst[0:ROWS, :, :, :].bitcast(F32), 0.0)
                pool.memset(kst[ROWS:, 0, :, :], 1.0)

        def section(block, b, prep, nsteps, last):
            preps = 1 if prep else nsteps - (1 if last else 0)
            projs = 2 if prep else 0 if last else nsteps
            proj_seq = lambda p: b + p if prep else b + p + 2
            prep_seq = lambda p: b + p if prep else b + p + 1
            prep_buf = lambda p: p % 2 if prep else (p + 1) % 2
            side = {}
            for r in range(max(nsteps, 1)):
                if r < preps:
                    side.setdefault((r, V_AT), []).append(("value", r, 0))
                for p in range(projs) if prep else [r] if r < projs else []:
                    for n in range(NPROJ - 1):
                        side.setdefault((r, 2 + p * (NPROJ - 1) + n if prep else PROJECT_FROM + n), []).append(("project", p, n))
                if r > 0:
                    for n, kind in enumerate(("unturn0", "unturn1", "turn", "output")):
                        side.setdefault((r, FIN_FROM + n), []).append((kind, r - 1, 0))
                if r < preps:
                    side.setdefault((r, H if prep else A_TO), []).append(("maxima", r, 0))
            if nsteps:
                side.setdefault((nsteps - 1, H), []).extend((kind, nsteps - 1, 0) for kind in ("unturn0", "unturn1", "turn", "output"))
            order = [x for at in sorted(side) for x in side[at]]
            fill = {x: n for n, x in enumerate(order)}
            @block.tensor
            def _(pe):
                def project(p, s):
                    at_least(pe, emptied, fill["project", p, s])
                    pe.matmul(ps_m[:], w[projections[s]][:], cols(xnT, proj_seq(p)), start=True, stop=True).then_inc(filled, 1)

                def value(p):
                    at_least(pe, emptied, fill["value", p, 0])
                    pe.wait_ge(xb_ready, p + 1)
                    for k in range(TPS):
                        mm = pe.matmul(ps_m[:, k * P:(k + 1) * P], xb[:, k * P:(k + 1) * P], w["v"][:], start=True, stop=True)
                    mm.then_inc(filled, 1)

                def maxima(p, h, qt):
                    j = prep_buf(p)
                    if h == 0 and qt == 0:
                        pe.wait_ge(stacked, 16 * 2 * len(QPART) * (p + 1))
                    at_least(pe, a_taken, (p * H + h) * TPS + qt - 1)
                    wd = (qt + 1) * P if causal else SEQ
                    mm = pe.matmul(ps_a[:, qt % 2, 0:wd], qst[0:ROWS, j, h, qt * P:(qt + 1) * P], kst[0:ROWS, j, h, 0:wd],
                                   start=True, stop=not causal)
                    if causal:
                        mm = pe.matmul(ps_a[:, qt % 2, qt * P:wd], identb[:], maskqb[:], start=False, stop=True)
                    mm.then_inc(a_ready, 1)

                def turn_maxima(p):
                    at_least(pe, emptied, fill["maxima", p, 0])
                    pe.wait_ge(maxed, p + 1)
                    for qt in range(TPS):
                        mm = pe.transpose(ps_m[0:H, qt * P:(qt + 1) * P], mx[:, qt, :], c["ident"][:])
                    mm.then_inc(filled, 1)

                def scores(r, h, kt):
                    if h == 0 and kt == 0:
                        at_least(pe, max_stacked, 16 * r)
                    j, bank = r % 2, kt % 2
                    at_least(pe, exped, (r * H + h) * TPS + kt - 1)
                    q0 = kt * P if causal else 0
                    mm = pe.matmul(ps_s[:, bank, q0:SEQ], kst[0:ROWS + MAXROWS, j, h, kt * P:(kt + 1) * P],
                                   qst[0:ROWS + MAXROWS, j, h, q0:SEQ], start=True, stop=not causal)
                    if causal:
                        mm = pe.matmul(ps_s[:, bank, q0:q0 + P], identb[:], maskkb[:], start=False, stop=True)
                    mm.then_inc(s_ready, 1)

                def weigh(r, h, kt):
                    if h == 0 and kt == 0:
                        at_least(pe, v_ready, r)
                        at_least(pe, sums_ready, r)
                    if kt == 0:
                        pe.wait_ge(exped, (r * H + h + 1) * TPS)
                    q0 = kt * P if causal else 0
                    g = h // 2 % 4
                    mm = pe.matmul(ps_o[32 * g:32 * (g + 1), h // 8, q0:SEQ],
                                   v[:, r % 2, kt, h // 2, h % 2, :, :].rearrange("p a d -> p (a d)"),
                                   pt[:, h % 2, kt, q0:SEQ], start=(h % 2 == 0 and kt == 0), stop=(h % 2 == 1 and kt == TPS - 1),
                                   tile_position=(0, 32 * g))
                    if kt == TPS - 1:
                        mm.then_inc(pv_done, 1)

                def unturn(r, half):
                    at_least(pe, emptied, fill[f"unturn{half}", r, 0])
                    pe.wait_ge(sums_ready, r + 1)
                    for k in range(TPS):
                        mm = pe.transpose(ps_m[:, k * P:(k + 1) * P], sums[:, half, k * P:(k + 1) * P], c["ident"][:])
                    mm.then_inc(filled, 1)

                def turn(r):
                    at_least(pe, emptied, fill["turn", r, 0])
                    pe.wait_ge(o_ready, 2 * r + 2)
                    for k in range(TPS):
                        mm = pe.transpose(ps_m[:, k * P:(k + 1) * P], o[:, k, :, :].rearrange("p h d -> p (h d)"), c["ident"][:])
                    mm.then_inc(filled, 1)

                def output(r):
                    pe.wait_ge(emptied, fill["output", r, 0])
                    pe.matmul(ps_m[:], wo_sb[:], oT[:], start=True, stop=True).then_inc(filled, 1)

                def beside(r, h):
                    for kind, n, m in side.get((r, h), []):
                        {"project": lambda: project(n, m), "value": lambda: value(n), "maxima": lambda: turn_maxima(n), "unturn0": lambda: unturn(n, 0),
                         "unturn1": lambda: unturn(n, 1), "turn": lambda: turn(n), "output": lambda: output(n)}[kind]()

                if prep:
                    for h in range(H):
                        beside(0, h)
                    for h in range(H):
                        for qt in range(TPS):
                            maxima(0, h, qt)
                    beside(0, H)
                for r in range(nsteps):
                    tiles = [(h, qt) for h in range(H) for qt in range(TPS)] if r < preps else []
                    for h in range(H):
                        beside(r, h)
                        for kt in range(TPS):
                            scores(r, h, kt)
                            if A_FROM <= h < A_TO:
                                for a in tiles[a_upto(h, kt):a_upto(h, kt + 1)]:
                                    maxima(r, *a)
                            if h >= 1:
                                weigh(r, h - 1, kt)
                    for kt in range(TPS):
                        weigh(r, H - 1, kt)
                    beside(r, H)

            @block.scalar
            def _(act):
                def take_v(p):
                    act.wait_ge(filled, fill["value", p, 0] + 1)
                    at_least(act, pv_done, p * H)
                    ps = ps_m[:].rearrange("p (k i e d) -> p k i e d", k=TPS, e=2, d=D)
                    for e in range(2):
                        act.copy(v[:, prep_buf(p), :, :, e, 2 * e, :], ps[:, :, :, e, :])
                    act.drain().then_inc(v_ready, 1)
                    act.sem_inc(emptied, 1)

                def exps(r, h):
                    for kt in range(TPS):
                        act.wait_ge(s_ready, (r * H + h) * TPS + kt + 1)
                        if kt == 0:
                            at_least(act, pv_done, r * H + h - 1)
                        q0 = kt * P if causal else 0
                        act.activation(pt[:, h % 2, kt, q0:SEQ], ps_s[:, kt % 2, q0:SEQ], ACT.Exp, scale=SCALE).then_inc(exped, 1)

                def beside(r, h):
                    for kind, n, m in side.get((r, h), []):
                        if kind == "value":
                            take_v(n)
                        if kind == "turn":
                            act.wait_ge(filled, fill[kind, n, 0] + 1)
                            act.copy(oT[:], ps_m[:]).then_inc(emptied, 1)

                if prep:
                    take_v(0)
                for r in range(nsteps):
                    for h in range(H):
                        exps(r, h)
                        beside(r, h)
                    act.wait_ge(pv_done, (r + 1) * H)
                    if r > 0:
                        act.wait_ge(filled, fill["unturn1", r - 1, 0] + 1)
                    act.copy(sums[:], ps_o[:]).then_inc(sums_ready, 1)
                    beside(r, H)

            @block.vector
            def _(dve):
                def take(p, s):
                    which = 0 if projections[s][0] == "q" else 1
                    dve.wait_ge(filled, fill["project", p, s] + 1)
                    if not rope:
                        at_least(dve, full_taken, 2 * p - 1 + which)
                        dve.tensor_copy(full[:, which, :], ps_m[:]).then_inc(full_ready, 1)
                        dve.drain().then_inc(emptied, 1)
                    elif len(projections[s]) == 1:
                        at_least(dve, full_taken, 2 * p - 1 + which)
                        dve.tensor_tensor(full[:, which, :], ps_m[:], cos[:], ALU.mult).then_inc(emptied, 1)
                    else:
                        dve.tensor_tensor(rot[:], ps_m[:], sin[:], ALU.mult).then_inc(emptied, 1)
                        dve.drain()
                        dve.tensor_tensor(full[:, which, :], full[:, which, :], rot[:], ALU.add).then_inc(full_ready, 1)
                        dve.drain()

                def maxima(p, tiles):
                    for h, qt in tiles:
                        dve.wait_ge(a_ready, (p * H + h) * TPS + qt + 1)
                        wd = (qt + 1) * P if causal else SEQ
                        dve.tensor_reduce(mx[:, qt, h:h + 1], ps_a[:, qt % 2, 0:wd], AX.X, ALU.max).then_inc(a_taken, 1)

                def take_maxima(p):
                    dve.wait_ge(filled, fill["maxima", p, 0] + 1)
                    at_least(dve, max_stored, 16 * p)
                    dve.tensor_scalar(negmax[:], ps_m[0:H, :], -1.0, None, ALU.mult).then_inc(emptied, 1)
                    dve.drain()
                    dve.tensor_copy(nm[:, 0, :], negmax[:])
                    dve.drain()
                    dve.tensor_tensor(nm[:, 1, :], negmax[:], nm[:, 0, :], ALU.subtract).then_inc(nm_ready, 1)
                    dve.drain()

                def normalize_heads(r, half):
                    dve.wait_ge(filled, fill[f"unturn{half}", r, 0] + 1)
                    if half == 0 and r > 0:
                        dve.wait_ge(filled, fill["turn", r - 1, 0] + 1)
                    ps = ps_m[:].rearrange("p (k h a d) -> p k h a d", k=TPS, a=2, d=D)
                    rs = rsum[:, :, half * H // 2:(half + 1) * H // 2]
                    for qt in range(TPS):
                        dve.reciprocal(rs[:, qt, :].unsqueeze(2), ps[:, qt, :, 1, 0:1])
                    dve.drain()
                    for qt in range(TPS):
                        dve.tensor_tensor(o[:, qt, half * H // 2:(half + 1) * H // 2, :], ps[:, qt, :, 0, :], bcast(rs[:, qt, :], D), ALU.mult)
                    dve.drain().then_inc(o_ready, 1)
                    dve.sem_inc(emptied, 1)

                def beside(r, h):
                    for kind, n, m in side.get((r, h), []):
                        if kind == "project":
                            take(n, m)
                        if kind == "maxima":
                            dve.drain().then_inc(maxed, 1)
                            take_maxima(n)
                        if kind in ("unturn0", "unturn1"):
                            normalize_heads(n, int(kind[-1]))
                        if kind == "output":
                            dve.wait_ge(filled, fill[kind, n, 0] + 1)
                            dve.tensor_tensor(cols(xT, b + n), cols(xT, b + n), ps_m[:], ALU.add).then_inc(emptied, 1)

                tiles = [(h, qt) for h in range(H) for qt in range(TPS)]
                if prep:
                    for h in range(H):
                        beside(0, h)
                    maxima(0, tiles)
                    beside(0, H)
                for r in range(nsteps):
                    for h in range(H):
                        beside(r, h)
                        if A_FROM <= h < A_TO and r < preps:
                            maxima(r, tiles[a_upto(h, 0):a_upto(h + 1, 0)])
                    beside(r, H)

            @block.gpsimd
            def _(pool):
                for p in range(max(preps, projs)):
                    if p < preps:
                        at_least(pool, v_ready, p)
                        pool.tensor_copy(xb[:], cols(xnT, prep_seq(p))).then_inc(xb_ready, 1)
                    for which in range(2) if p < projs else ():
                        pool.wait_ge(full_ready, 2 * p + which + 1)
                        if which == 0:
                            at_least(pool, parts_stored, 16 * p)
                        left, part = full[:, which, :], parts[:, which * PARTS:(which + 1) * PARTS, :]
                        pool.tensor_copy(part[:, 0, :], left)
                        pool.drain()
                        pool.tensor_tensor(left, left, part[:, 0, :], ALU.subtract)
                        pool.drain()
                        pool.tensor_copy(part[:, 1, :], left)
                        pool.drain()
                        pool.tensor_tensor(part[:, 2, :], left, part[:, 1, :], ALU.subtract).then_inc(parts_ready, 1)
                        pool.drain().then_inc(full_taken, 1)

            @block.sync
            def _(sp):
                def store_parts(p):
                    sp.wait_ge(parts_ready, 2 * p + 2)
                    sp.dma_start(scratch[p % 2], parts[:]).then_inc(parts_stored, 16)
                    sp.wait_ge(parts_stored, 16 * (p + 1))

                if prep:
                    store_parts(0)
                for p in range(max(preps, projs if not prep else 0)):
                    j = prep_buf(p)
                    if p < preps:
                        at_least(sp, pv_done, p * H)
                        for m in range(len(QPART)):
                            for dst, part in ((qst, QPART[m]), (kst, PARTS + KPART[m])):
                                sp.dma_start(dst[D * m:D * (m + 1), j, :, :],
                                             scratch[j, :, part, :].rearrange("(h d) t -> d h t", d=D)).then_inc(stacked, 16)
                        sp.wait_ge(stacked, 16 * 2 * len(QPART) * (p + 1))
                    if prep:
                        store_parts(1)
                    elif p < projs:
                        store_parts(p)
                    if p < preps:
                        sp.wait_ge(nm_ready, p + 1)
                        sp.dma_start(max_scratch[j], nm[:]).then_inc(max_stored, 16)
                        sp.wait_ge(max_stored, 16 * (p + 1))
                        sp.dma_start(qst[ROWS:ROWS + MAXROWS, j, :, :], max_scratch[j].rearrange("h m t -> m h t")).then_inc(max_stacked, 16)
                        sp.wait_ge(max_stacked, 16 * (p + 1))

        with nc.Block() as block:
            section(block, 0, True, 0, False)
        clear(nc, ph.sems)
        with nc.Fori(0, NSEQ // 2 - 1) as i:
            with nc.Block() as block:
                section(block, 2 * i, False, 2, False)
            clear(nc, ph.sems)
        with nc.Block() as block:
            section(block, NSEQ - 2, False, 2, True)
        clear(nc, ph.sems)


def l1_attn(nc, xT, xnT, c, t):
    attention(nc, xT, xnT, c, t, "l1a", t["L1_attn_WqT"], t["L1_attn_WkT"], t["L1_attn_WvT"], t["L1_attn_WoT"], causal=True, rope=False)


def l3_attn(nc, xT, xnT, c, t):
    w = t["L3_attn_w_qkv"]
    attention(nc, xT, xnT, c, t, "l3a", w[:, 0:P], w[:, P:2 * P], w[:, 2 * P:3 * P], t["L3_attn_w_proj"], causal=False, rope=True)


def l2_attn(nc, xT, xnT, c, t):
    normalize(nc, xT, xnT, c, "l2an", EPS)
    H, D = 16, 8
    NUM = P + H
    EPS_NORM, EPS_DEN = 1e-6, 1e-6
    with ExitStack() as ctx:
        ph = Phase(nc, ctx, "l2a")
        w = ph.sb("w", [P, 3 * P])
        wo, blocks = ph.sb("wo", [P, P]), ph.sb("blocks", [P, NUM])
        nw = ph.sb("nw", [P, 2, P])
        bout = ph.sb("bout", [P, 1])
        xb = ph.sb("xb", [P, 2, SEQ])
        sq = ph.sb("sq", [P, TPS, 2 * P])
        sqsum, var, std, rstd = (ph.sb(n, [P, TPS, 2]) for n in ("sqsum", "var", "std", "rstd"))
        scaled = ph.sb("scaled", [P, TPS, 2, P])
        qk = ph.sb("qk", [P, TPS, 2 * P])
        vo = ph.sb("vo", [P, TPS, P + 1])
        kv = ph.sb("kv", [P, NUM])
        qT = ph.sb("qT", [P, SEQ])
        den = ph.sb("den", [P, TPS, H])
        o = ph.sb("o", [P, TPS, P])
        oT = ph.sb("oT", [P, SEQ])
        ps_qkv = ph.ps("psqkv", [P, TPS, SEQ])
        ps_kv = ph.ps("pskv", [P, SEQ])
        ps_m = ph.ps("psm", [P, SEQ])
        ps_n = ph.ps("psn", [P, 2, SEQ])
        num = lambda k: ps_n[:, k // 2, (k % 2) * NUM:(k % 2 + 1) * NUM]
        (loaded, xb_ready, qkv_ready, squared, var_ready, std_ready, scaled_ready, qk_ready, vo_ready, kv_ready, kv_taken, qT_ready,
         qT_taken, num_ready, o_ready, oT_ready, oT_taken, y_ready, y_taken) = (
            ph.sem(n) for n in ("loaded", "xb_ready", "qkv_ready", "squared", "var_ready", "std_ready", "scaled_ready", "qk_ready",
                                "vo_ready", "kv_ready", "kv_taken", "qT_ready", "qT_taken", "num_ready", "o_ready", "oT_ready",
                                "oT_taken", "y_ready", "y_taken"))
        with nc.Block() as block:
            @block.sync
            def _(sp):
                for dst, src in ((w[:], t["L2_attn_W_qkv"]), (wo[:], t["L2_attn_W_out"]), (blocks[:], t["blocks8"]),
                                 (nw[:, 0, :], t["L2_attn_qn_w"].unsqueeze(0).to_broadcast([P, P])),
                                 (nw[:, 1, :], t["L2_attn_kn_w"].unsqueeze(0).to_broadcast([P, P])),
                                 (bout[:], t["L2_attn_b_out"].unsqueeze(1))):
                    sp.dma_start(dst, src).then_inc(loaded, 16)
                sp.wait_ge(loaded, 16 * 6)

            @block.vector
            def _(dve):
                dve.memset(vo[:], 1.0)
        clear(nc, ph.sems)

        def section(block, b):
            @block.gpsimd
            def _(pool):
                for r in range(2):
                    pool.tensor_copy(xb[:, r, :], cols(xnT, b + r)).then_inc(xb_ready, 1)

            @block.tensor
            def _(pe):
                def project(r):
                    pe.wait_ge(xb_ready, r + 1)
                    at_least(pe, scaled_ready, r)
                    at_least(pe, vo_ready, r)
                    for k in range(TPS):
                        pe.matmul(ps_qkv[:, k, 0:3 * P], xb[:, r, k * P:(k + 1) * P], w[:], start=True, stop=True).then_inc(qkv_ready, 1)

                project(0)
                for r in range(2):
                    pe.wait_ge(qk_ready, r + 1)
                    pe.wait_ge(vo_ready, r + 1)
                    at_least(pe, kv_taken, r)
                    for k in range(TPS):
                        mm = pe.matmul(ps_kv[:, 0:P + 1], qk[:, k, P:2 * P], vo[:, k, :], start=(k == 0), stop=(k == TPS - 1))
                    mm.then_inc(kv_ready, 1)
                    at_least(pe, y_taken, r)
                    for k in range(TPS):
                        mm = pe.transpose(ps_m[:, k * P:(k + 1) * P], qk[:, k, 0:P], c["ident"][:])
                    mm.then_inc(qT_ready, 1)
                    if r == 0:
                        project(1)
                    pe.wait_ge(kv_taken, r + 1)
                    pe.wait_ge(qT_taken, r + 1)
                    at_least(pe, o_ready, r)
                    for k in range(TPS):
                        mm = pe.matmul(num(k), qT[:, k * P:(k + 1) * P], kv[:], start=True, stop=True)
                    mm.then_inc(num_ready, 1)
                    pe.wait_ge(o_ready, r + 1)
                    for k in range(TPS):
                        mm = pe.transpose(ps_m[:, k * P:(k + 1) * P], o[:, k, :], c["ident"][:])
                    mm.then_inc(oT_ready, 1)
                    pe.wait_ge(oT_taken, r + 1)
                    pe.matmul(ps_m[:], wo[:], oT[:], start=True, stop=True).then_inc(y_ready, 1)

            @block.scalar
            def _(act):
                for r in range(2):
                    act.wait_ge(qkv_ready, TPS * (r + 1))
                    act.activation(sq[:], ps_qkv[:, :, 0:2 * P], ACT.Square).then_inc(squared, 1)
                    at_least(act, kv_ready, r)
                    act.copy(vo[:, :, 0:P], ps_qkv[:, :, 2 * P:3 * P]).then_inc(vo_ready, 1)
                    act.wait_ge(var_ready, r + 1)
                    act.activation(std[:], var[:], ACT.Sqrt).then_inc(std_ready, 1)
                    act.wait_ge(scaled_ready, r + 1)
                    at_least(act, qT_ready, r)
                    act.activation(qk[:], scaled[:].rearrange("p k a d -> p k (a d)"), ACT.Relu).then_inc(qk_ready, 1)
                    act.wait_ge(qT_ready, r + 1)
                    act.copy(qT[:], ps_m[:]).then_inc(qT_taken, 1)
                    act.wait_ge(oT_ready, r + 1)
                    act.copy(oT[:], ps_m[:]).then_inc(oT_taken, 1)

            @block.vector
            def _(dve):
                for r in range(2):
                    dve.wait_ge(squared, r + 1)
                    dve.tensor_reduce(sqsum[:], sq[:].rearrange("p k (a d) -> p k a d", a=2), AX.X, ALU.add)
                    dve.drain()
                    dve.tensor_scalar(var[:], sqsum[:], 1.0 / P, EPS_NORM, ALU.mult, ALU.add).then_inc(var_ready, 1)
                    dve.wait_ge(std_ready, r + 1)
                    dve.reciprocal(rstd[:], std[:])
                    dve.drain()
                    dve.wait_ge(vo_ready, r + 1)
                    at_least(dve, qk_ready, r)
                    for k in range(TPS):
                        for a in range(2):
                            dve.scalar_tensor_tensor(out=scaled[:, k, a, :], in0=ps_qkv[:, k, a * P:(a + 1) * P], scalar=rstd[:, k, a:a + 1],
                                                     in1=nw[:, a, :], op0=ALU.mult, op1=ALU.mult)
                    dve.drain().then_inc(scaled_ready, 1)
                    dve.wait_ge(kv_ready, r + 1)
                    dve.tensor_tensor(kv[:, 0:P], ps_kv[:, 0:P], blocks[:, 0:P], ALU.mult)
                    dve.tensor_scalar(kv[:, P:NUM], blocks[:, P:NUM], ps_kv[:, P:P + 1], None, ALU.mult)
                    dve.drain().then_inc(kv_taken, 1)
                    dve.wait_ge(num_ready, r + 1)
                    for k in range(TPS):
                        dve.tensor_scalar(den[:, k, :], num(k)[:, P:NUM], EPS_DEN, None, ALU.add)
                    dve.drain()
                    dve.reciprocal(den[:], den[:])
                    dve.drain()
                    for k in range(TPS):
                        dve.tensor_tensor(o[:, k, :].rearrange("p (h d) -> p h d", d=D), num(k)[:, 0:P].rearrange("p (h d) -> p h d", d=D),
                                          bcast(den[:, k, :], D), ALU.mult)
                    dve.drain().then_inc(o_ready, 1)
                    dve.wait_ge(y_ready, r + 1)
                    x = cols(xT, b + r)
                    dve.scalar_tensor_tensor(out=x, in0=ps_m[:], scalar=bout[:], in1=x, op0=ALU.add, op1=ALU.add).then_inc(y_taken, 1)

        with nc.Fori(0, NSEQ // 2) as i:
            with nc.Block() as block:
                section(block, 2 * i)
            clear(nc, ph.sems)


def spread_gates(nc, c, ph, gT, parts, tmp, block_done):
    with nc.Block() as block:
        @block.vector
        def _(dve):
            E = gT.shape[0]
            dve.tensor_copy(parts[0:E, :], gT[:])
            dve.drain()
            dve.tensor_tensor(gT[:], gT[:], parts[0:E, :], ALU.subtract)
            dve.drain()
            dve.tensor_copy(tmp[:], gT[:])
            dve.drain()
            dve.tensor_copy(parts[32:32 + E, :], tmp[:])
            dve.tensor_tensor(gT[:], gT[:], tmp[:], ALU.subtract)
            dve.drain()
            dve.tensor_copy(parts[64:64 + E, :], gT[:])


def experts(nc, xT, xnT, c, ph, U, wa, wb, wo, parts, sel, kind, b_glu=None, b_lin=None, b_out=None, shared=None, bias=None):
    swiglu, gates = kind == "swiglu", kind != "geglu"
    LIMIT, ALPHA = 7.0, 1.702
    with ExitStack() as ctx:
        ph2 = Phase(nc, ctx, ph.name + "x")
        NU = U + (1 if shared else 0)
        rows = lambda u: P if u < U else P // 2
        gl, sg, lt, pr, gated = (ph2.sb(n, [P, 2, SEQ]) for n in ("gl", "sg", "lt", "pr", "gated"))
        ps_a, ps_b, ps_g, ps_o = (ph2.ps(n, [P, 2, SEQ]) for n in ("psa", "psb", "psg", "pso"))
        a_ready, b_ready, g_ready, a_taken, b_taken, sg_ready, pr_ready, gated_ready, out_done, y_ready, y_taken = (
            ph2.sem(n) for n in ("a_ready", "b_ready", "g_ready", "a_taken", "b_taken", "sg_ready", "pr_ready", "gated_ready",
                                 "out_done", "y_ready", "y_taken"))

        def section(block, b):
            @block.tensor
            def _(pe):
                def front(r, u):
                    n, m = r * NU + u, rows(u)
                    at_least(pe, a_taken, n - 1)
                    A, B = (wa[:, u, :], wb[:, u, :]) if u < U else (shared[0][:], shared[1][:])
                    pe.matmul(ps_a[0:m, n % 2, :], A, cols(xnT, b + r), start=True, stop=True).then_inc(a_ready, 1)
                    at_least(pe, b_taken, n - 1)
                    pe.matmul(ps_b[0:m, n % 2, :], B, cols(xnT, b + r), start=True, stop=True).then_inc(b_ready, 1)
                    at_least(pe, gated_ready, n - 1)
                    if u < U and gates:
                        pe.matmul(ps_g[:, n % 2, :], sel[:, u, :], cols(parts, b + r), start=True, stop=True).then_inc(g_ready, 1)

                def back(r, u):
                    n, m = r * NU + u, rows(u)
                    pe.wait_ge(gated_ready, n + 1)
                    O = wo[:, u, :] if u < U else shared[2][:]
                    more = b_out is not None
                    pe.matmul(ps_o[:, r, :], O, gated[0:m, n % 2, :], start=(u == 0), stop=(u == NU - 1 and not more)).then_inc(out_done, 1)
                    if u == NU - 1:
                        if more:
                            for q in range(3):
                                pe.matmul(ps_o[:, r, :], b_out[:, q, :], cols(parts, b + r), start=False, stop=(q == 2))
                        pe.drain().then_inc(y_ready, 1)

                steps = [(r, u) for r in range(2) for u in range(NU)]
                for i, s in enumerate(steps):
                    front(*s)
                    if i:
                        back(*steps[i - 1])
                back(*steps[-1])

            @block.scalar
            def _(act):
                for r in range(2):
                    for u in range(NU):
                        n, m = r * NU + u, rows(u)
                        if swiglu:
                            act.wait_ge(a_taken, n + 1)
                            at_least(act, pr_ready, n - 1)
                            act.activation(sg[:, n % 2, :], gl[:, n % 2, :], ACT.Sigmoid, scale=ALPHA).then_inc(sg_ready, 1)
                        elif kind == "geglu":
                            act.wait_ge(b_ready, n + 1)
                            at_least(act, gated_ready, n - 1)
                            act.activation(sg[:, n % 2, :], ps_b[:, n % 2, :], ACT.Gelu, bias=b_lin[:, u:u + 1]).then_inc(sg_ready, 1)
                            act.drain().then_inc(b_taken, 1)
                        else:
                            act.wait_ge(a_ready, n + 1)
                            at_least(act, pr_ready, n - 1)
                            act.activation(sg[0:m, n % 2, :], ps_a[0:m, n % 2, :], ACT.Silu).then_inc(sg_ready, 1)
                            act.drain().then_inc(a_taken, 1)

            if swiglu:
                @block.gpsimd
                def _(pool):
                    for n in range(2 * NU):
                        pool.wait_ge(sg_ready, n + 1)
                        at_least(pool, gated_ready, n - 1)
                        pool.tensor_tensor(pr[:, n % 2, :], gl[:, n % 2, :], sg[:, n % 2, :], ALU.mult).then_inc(pr_ready, 1)

            def finish(dve, r):
                dve.wait_ge(y_ready, r + 1)
                x = cols(xT, b + r)
                if bias is None:
                    dve.tensor_tensor(x, x, ps_o[:, r, :], ALU.add).then_inc(y_taken, 1)
                else:
                    dve.scalar_tensor_tensor(out=x, in0=ps_o[:, r, :], scalar=bias[:], in1=x, op0=ALU.add, op1=ALU.add).then_inc(y_taken, 1)

            @block.vector
            def _(dve):
                def front(r, u):
                    n, m = r * NU + u, rows(u)
                    if swiglu:
                        dve.wait_ge(a_ready, n + 1)
                        at_least(dve, pr_ready, n - 1)
                        dve.tensor_scalar(gl[:, n % 2, :], ps_a[:, n % 2, :], b_glu[:, u:u + 1], LIMIT, ALU.add, ALU.min).then_inc(a_taken, 1)
                        dve.wait_ge(b_ready, n + 1)
                        dve.tensor_scalar(lt[:, n % 2, :], ps_b[:, n % 2, :], b_lin[:, u:u + 1], 1.0 - LIMIT, ALU.add, ALU.max).then_inc(b_taken, 1)

                def back(r, u):
                    n, m = r * NU + u, rows(u)
                    if kind == "geglu":
                        dve.wait_ge(sg_ready, n + 1)
                        dve.wait_ge(a_ready, n + 1)
                        at_least(dve, out_done, n - 1)
                        dve.scalar_tensor_tensor(out=gated[:, n % 2, :], in0=ps_a[:, n % 2, :], scalar=b_glu[:, u:u + 1], in1=sg[:, n % 2, :],
                                                 op0=ALU.add, op1=ALU.mult).then_inc(gated_ready, 1)
                        dve.drain().then_inc(a_taken, 1)
                        return
                    if swiglu:
                        dve.drain()
                        dve.wait_ge(pr_ready, n + 1)
                        dve.scalar_tensor_tensor(out=lt[:, n % 2, :], in0=lt[:, n % 2, :], scalar=1.0 + LIMIT, in1=pr[:, n % 2, :],
                                                 op0=ALU.min, op1=ALU.mult)
                    else:
                        dve.wait_ge(sg_ready, n + 1)
                        dve.wait_ge(b_ready, n + 1)
                        at_least(dve, out_done, n - 1)
                        dst = lt if u < U else gated
                        dve.tensor_tensor(dst[0:m, n % 2, :], sg[0:m, n % 2, :], ps_b[0:m, n % 2, :], ALU.mult).then_inc(pr_ready, 1)
                        dve.drain().then_inc(b_taken, 1)
                    if u == U:
                        dve.sem_inc(gated_ready, 1)
                        return
                    if swiglu:
                        dve.drain()
                    dve.wait_ge(g_ready, r * U + u + 1)
                    at_least(dve, out_done, n - 1)
                    dve.tensor_tensor(gated[:, n % 2, :], lt[:, n % 2, :], ps_g[:, n % 2, :], ALU.mult).then_inc(gated_ready, 1)

                steps = [(r, u) for r in range(2) for u in range(NU)]
                for i, s in enumerate(steps):
                    front(*s)
                    if i:
                        back(*steps[i - 1])
                        if steps[i - 1][1] == NU - 1:
                            finish(dve, 0)
                back(*steps[-1])
                finish(dve, 1)

        with nc.Fori(0, NSEQ // 2) as i:
            with nc.Block() as block:
                section(block, 2 * i)
            clear(nc, ph2.sems)


def l3_ffn(nc, xT, xnT, c, t):
    normalize(nc, xT, xnT, c, "l3fn", EPS)
    add_normed(nc, xT, xnT)
    normalize(nc, xnT, xnT, c, "l3fm", float(np.finfo(np.float32).eps), center=False)
    E = 8
    with ExitStack() as ctx:
        ph = Phase(nc, ctx, "l3f")
        wa, wb, wo = (ph.sb(n, [P, E, P]) for n in ("wa", "wb", "wo"))
        gw, gb = ph.sb("gw", [P, E]), ph.sb("gb", [P, E])
        b_glu, b_lin = ph.sb("b_glu", [P, E]), ph.sb("b_lin", [P, E])
        normw = ph.sb("normw", [P, 1])
        selF, sel = ph.sb("self", [96, E, P]), ph.sb("sel", [96, E, P], BF16)
        b2, b2left = ph.sb("b2", [96, P]), ph.sb("b2left", [96, P])
        b2p = ph.sb("b2p", [96, 3, P], BF16)
        parts = ph.sb("parts", [96, TOK], BF16)
        with ExitStack() as ctx2:
            g = Phase(nc, ctx2, "l3g")
            logits, e, gate = (g.sb(n, [P, NT, E]) for n in ("logits", "e", "gate"))
            top = g.sb("top", [P, NT, 8])
            total, rtotal = g.sb("total", [P, NT]), g.sb("rtotal", [P, NT])
            gT, tmp = g.sb("gT", [E, TOK]), g.sb("tmp", [E, TOK], BF16)
            ps_l = g.ps("psl", [P, NT, E])
            ps_t = g.ps("pst", [P, 4, SEQ])
            loaded, zeroed, scaled, logits_ready, shifted, e_ready, gate_ready, turned, taken = (
                g.sem(n) for n in ("loaded", "zeroed", "scaled", "logits_ready", "shifted", "e_ready", "gate_ready", "turned", "taken"))
            with nc.Block() as block:
                @block.sync
                def _(sp):
                    sp.dma_start(normw[:], t["L3_ffn_norm_w"].unsqueeze(1)).then_inc(loaded, 16)
                    sp.dma_start(gw[:], t["L3_ffn_gate_wT"]).then_inc(loaded, 16)
                    sp.dma_start(gb[:], t["L3_ffn_gate_b"].unsqueeze(0).to_broadcast([P, E])).then_inc(loaded, 16)
                    sp.dma_start(b_glu[:], t["L3_ffn_b1T"][:, 0, :]).then_inc(loaded, 16)
                    sp.dma_start(b_lin[:], t["L3_ffn_b1T"][:, 1, :]).then_inc(loaded, 16)
                    sp.dma_start(selF[:], t["sel8"]).then_inc(loaded, 16)
                    sp.wait_ge(zeroed, 1)
                    for q in range(3):
                        sp.dma_start(b2[32 * q:32 * q + E, :], t["L3_ffn_mlp2_b"]).then_inc(loaded, 16)
                    sp.dma_start(wa[:], t["L3_ffn_w1T"][:, :, 0, :]).then_inc(loaded, 16)
                    sp.dma_start(wb[:], t["L3_ffn_w1T"][:, :, 1, :]).then_inc(loaded, 16)
                    sp.dma_start(wo[:], t["L3_ffn_w2T"]).then_inc(loaded, 16)

                @block.gpsimd
                def _(pool):
                    pool.memset(parts[:], 0.0)
                    pool.memset(b2[:], 0.0).then_inc(zeroed, 1)

                @block.scalar
                def _(act):
                    act.wait_ge(loaded, 16 * 12)
                    for b in range(NSEQ):
                        act.activation(cols(xnT, b), cols(xnT, b), ACT.Copy, scale=normw[:]).then_inc(scaled, 1)
                    act.copy(sel[:], selF[:])
                    act.wait_ge(shifted, 1)
                    act.activation(e[:], e[:], ACT.Exp).then_inc(e_ready, 1)
                    for b in range(NSEQ):
                        act.wait_ge(turned, b + 1)
                        act.copy(cols(gT, b), ps_t[0:E, b % 4, :]).then_inc(taken, 1)

                @block.tensor
                def _(pe):
                    for k in range(NT):
                        if k % TPS == 0:
                            pe.wait_ge(scaled, k // TPS + 1)
                        mm = pe.matmul(ps_l[:, k, :], xnT[:, k * P:(k + 1) * P], gw[:], start=True, stop=True)
                    mm.then_inc(logits_ready, 1)
                    pe.wait_ge(gate_ready, 1)
                    for b in range(NSEQ):
                        at_least(pe, taken, b - 3)
                        for k in range(TPS):
                            mm = pe.transpose(ps_t[0:E, b % 4, k * P:(k + 1) * P], gate[:, b * TPS + k, :], c["ident"][:])
                        mm.then_inc(turned, 1)

                @block.vector
                def _(dve):
                    dve.wait_ge(loaded, 16 * 12)
                    dve.tensor_scalar(b_lin[:], b_lin[:], 1.0, None, ALU.add)
                    dve.wait_ge(logits_ready, 1)
                    dve.tensor_tensor(logits[:], ps_l[:], gb[:].unsqueeze(1).to_broadcast([P, NT, E]), ALU.add)
                    dve.drain()
                    for k in range(NT):
                        dve.max(top[:, k, :], logits[:, k, :])
                    dve.drain()
                    dve.tensor_tensor(e[:], logits[:], bcast(top[:, :, 0], E), ALU.subtract).then_inc(shifted, 1)
                    dve.tensor_tensor(gate[:], logits[:], bcast(top[:, :, 1], E), ALU.is_ge)
                    dve.wait_ge(e_ready, 1)
                    dve.drain()
                    dve.tensor_tensor(gate[:], gate[:], e[:], ALU.mult)
                    dve.drain()
                    dve.tensor_reduce(total[:], gate[:], AX.X, ALU.add)
                    dve.drain()
                    dve.reciprocal(rtotal[:], total[:])
                    dve.drain()
                    dve.tensor_tensor(gate[:], gate[:], bcast(rtotal[:], E), ALU.mult).then_inc(gate_ready, 1)
            clear(nc, g.sems)
            spread_gates(nc, c, g, gT, parts, tmp, None)
        with nc.Block() as block:
            @block.vector
            def _(dve):
                dve.tensor_copy(b2p[:, 0, :], b2[:])
                dve.drain()
                dve.tensor_tensor(b2left[:], b2[:], b2p[:, 0, :], ALU.subtract)
                dve.drain()
                dve.tensor_copy(b2p[:, 1, :], b2left[:])
                dve.drain()
                dve.tensor_tensor(b2p[:, 2, :], b2left[:], b2p[:, 1, :], ALU.subtract)
        experts(nc, xT, xnT, c, ph, E, wa, wb, wo, parts, sel, "swiglu", b_glu, b_lin, b2p)


def l2_ffn(nc, xT, xnT, c, t):
    normalize(nc, xT, xnT, c, "l2fn", EPS)
    E, TOP, CAPACITY = 32, 4, 2 * 512 * 4 // 32
    U = E // 2
    with ExitStack() as ctx:
        ph = Phase(nc, ctx, "l2f")
        wa, wb, wo = (ph.sb(n, [P, U, P]) for n in ("wa", "wb", "wo"))
        s1, s3, s2 = ph.sb("s1", [P, P // 2]), ph.sb("s3", [P, P // 2]), ph.sb("s2", [P // 2, P])
        sel = ph.sb("sel", [96, U, P], BF16)
        parts = ph.sb("parts", [96, TOK], BF16)
        with ExitStack() as ctx2:
            g = Phase(nc, ctx2, "l2g")
            raw = g.sb("raw", [P, U, P], BF16)
            raws = g.sb("raws", [P, 4, P], BF16)
            selF = g.sb("self", [96, U // 4, P])
            gw, gb = g.sb("gw", [P, E]), g.sb("gb", [P, E])
            scores, biased, mask, gate = (g.sb(n, [P, NT, E]) for n in ("scores", "biased", "mask", "gate"))
            top = g.sb("top", [P, NT, 8])
            total, rtotal = g.sb("total", [P, NT]), g.sb("rtotal", [P, NT])
            gT, maskT, zeros, tmp = g.sb("gT", [E, TOK]), g.sb("maskT", [E, TOK]), g.sb("zeros", [E, TOK]), g.sb("tmp", [E, TOK], BF16)
            ps_l = g.ps("psl", [P, NT, E])
            ps_t = g.ps("pst", [P, 4, SEQ])
            loaded, reused, small_ready, logits_ready, scores_ready, gate_ready, turned, taken = (
                g.sem(n) for n in ("loaded", "reused", "small_ready", "logits_ready", "scores_ready", "gate_ready", "turned", "taken"))
            with nc.Block() as block:
                @block.sync
                def _(sp):
                    sp.dma_start(gb[:], t["L2_ffn_bias"].unsqueeze(0).to_broadcast([P, E])).then_inc(loaded, 16)
                    sp.dma_start(raws[:, 0, 0:E], t["L2_ffn_gate_wT"]).then_inc(loaded, 16)
                    sp.dma_start(raws[:, 1, 0:P // 2], t["L2_ffn_sw1T"]).then_inc(loaded, 16)
                    sp.dma_start(raws[:, 2, 0:P // 2], t["L2_ffn_sw3T"]).then_inc(loaded, 16)
                    sp.dma_start(raws[0:P // 2, 3, :], t["L2_ffn_sw2T"]).then_inc(loaded, 16)
                    sp.wait_ge(loaded, 16 * 5)
                    for n, name in enumerate(("L2_ffn_W1p", "L2_ffn_W3p", "L2_ffn_W2p")):
                        at_least(sp, reused, n)
                        sp.dma_start(raw[:], t[name]).then_inc(loaded, 16)
                    for n in range(4):
                        at_least(sp, reused, 3 + n)
                        sp.dma_start(selF[:], t["sel32"][:, 4 * n:4 * n + 4, :]).then_inc(loaded, 16)

                @block.gpsimd
                def _(pool):
                    pool.memset(parts[:], 0.0)
                    pool.memset(zeros[:], 0.0)
                    for n, dst in enumerate((wa, wb, wo)):
                        pool.wait_ge(loaded, 16 * (6 + n))
                        pool.tensor_copy(dst[:], raw[:]).then_inc(reused, 1)
                    for n in range(4):
                        pool.wait_ge(loaded, 16 * (9 + n))
                        pool.tensor_copy(sel[:, 4 * n:4 * n + 4, :], selF[:]).then_inc(reused, 1)

                @block.scalar
                def _(act):
                    act.wait_ge(loaded, 16 * 5)
                    act.copy(gw[:], raws[:, 0, 0:E]).then_inc(small_ready, 1)
                    act.copy(s1[:], raws[:, 1, 0:P // 2])
                    act.copy(s3[:], raws[:, 2, 0:P // 2])
                    act.copy(s2[:], raws[0:P // 2, 3, :])
                    act.wait_ge(logits_ready, 1)
                    act.activation(scores[:], ps_l[:], ACT.Sigmoid).then_inc(scores_ready, 1)
                    for n in range(2 * NSEQ):
                        act.wait_ge(turned, n + 1)
                        act.copy(cols(gT if n % 2 else maskT, n // 2), ps_t[0:E, n % 4, :]).then_inc(taken, 1)

                @block.tensor
                def _(pe):
                    pe.wait_ge(small_ready, 1)
                    for k in range(NT):
                        mm = pe.matmul(ps_l[:, k, :], xnT[:, k * P:(k + 1) * P], gw[:], start=True, stop=True)
                    mm.then_inc(logits_ready, 1)
                    pe.wait_ge(gate_ready, 1)
                    for n in range(2 * NSEQ):
                        at_least(pe, taken, n - 3)
                        for k in range(TPS):
                            mm = pe.transpose(ps_t[0:E, n % 4, k * P:(k + 1) * P], (gate if n % 2 else mask)[:, n // 2 * TPS + k, :], c["ident"][:])
                        mm.then_inc(turned, 1)

                @block.vector
                def _(dve):
                    dve.wait_ge(loaded, 16 * 5)
                    dve.wait_ge(scores_ready, 1)
                    dve.tensor_tensor(biased[:], scores[:], gb[:].unsqueeze(1).to_broadcast([P, NT, E]), ALU.add)
                    dve.drain()
                    for k in range(NT):
                        dve.max(top[:, k, :], biased[:, k, :])
                    dve.drain()
                    dve.tensor_tensor(mask[:], biased[:], bcast(top[:, :, TOP - 1], E), ALU.is_ge)
                    dve.drain()
                    dve.tensor_tensor(gate[:], mask[:], scores[:], ALU.mult)
                    dve.drain()
                    dve.tensor_reduce(total[:], gate[:], AX.X, ALU.add)
                    dve.drain()
                    dve.tensor_scalar(total[:], total[:], 1e-12, None, ALU.max)
                    dve.drain()
                    dve.reciprocal(rtotal[:], total[:])
                    dve.drain()
                    dve.tensor_tensor(gate[:], gate[:], bcast(rtotal[:], E), ALU.mult).then_inc(gate_ready, 1)
            with nc.Block() as block:
                @block.vector
                def _(dve):
                    dve.tensor_tensor_scan(maskT[:], maskT[:], zeros[:], 0.0, ALU.add, ALU.add)
                    dve.drain()
                    dve.scalar_tensor_tensor(out=gT[:], in0=maskT[:], scalar=float(CAPACITY), in1=gT[:], op0=ALU.is_le, op1=ALU.mult)
            clear(nc, g.sems)
            spread_gates(nc, c, g, gT, parts, tmp, None)
        experts(nc, xT, xnT, c, ph, U, wa, wb, wo, parts, sel, "silu", shared=(s1, s3, s2))


def l1_ffn(nc, xT, xnT, c, t):
    normalize(nc, xT, xnT, c, "l1fn", EPS)
    for layer in range(2):
        local_attention(nc, xnT, c, t, layer)
        geglu(nc, xnT, c, t, layer)
    add_normed(nc, xT, xnT)


def local_attention(nc, yT, c, t, layer):
    H, D, WINDOW, PARTS = 8, 64, 64, 3
    PAIRS = H // 2
    INNER = H * D
    TURN_AT = 4
    NQK = 2 * PAIRS
    with ExitStack() as ctx:
        ph = Phase(nc, ctx, f"l1l{layer}")
        w = ph.sb("w", [P, 3 * INNER])
        wswap = ph.sb("wswap", [P, NQK, P])
        wo = ph.sb("wo", [P, PAIRS, P])
        tables = ph.sb("tables", [P, 4, SEQ])
        scales = ph.sb("scales", [P, 4])
        statsel = ph.sb("statsel", [P, NQK, 2 * H])
        spreadF, spread = ph.sb("spreadf", [96, NQK, P]), ph.sb("spread", [96, NQK, P], BF16)
        lselF, lsel = ph.sb("lself", [PARTS * H, H, P]), ph.sb("lsel", [PARTS * H, H, P], BF16)
        identb = ph.sb("identb", [P, P], BF16)
        maskF, maskA, maskT = ph.sb("maskf", [P, 2, P + WINDOW]), ph.sb("maska", [P, P + WINDOW], BF16), ph.sb("maskt", [P, P + WINDOW], BF16)
        h = ph.sb("h", [P, SEQ])
        sq, t1, t2 = (ph.sb(n, [P, 2, SEQ]) for n in ("sq", "t1", "t2"))
        raw = ph.sb("raw", [P, NQK, SEQ])
        q = ph.sb("q", [P, PAIRS, SEQ])
        kz = ph.sb("kz", [P, 2, PAIRS, SEQ])
        v = ph.sb("v", [P, TPS, INNER])
        norm, rnorm, left = (ph.sb(n, [2 * H, SEQ]) for n in ("norm", "rnorm", "left"))
        mid = ph.sb("mid", [2 * H, SEQ], BF16)
        rparts = ph.sb("rparts", [96, SEQ], BF16)
        nm, s, shift = (ph.sb(n, [P, TPS, H]) for n in ("nm", "s", "shift"))
        sparts, spart = ph.sb("sparts", [P, TPS, PARTS, H]), ph.sb("spart", [P, TPS, H], BF16)
        junk = ph.sb("junk", [P, P + WINDOW], BF16)
        lrows = ph.sb("lrows", [PARTS * H, SEQ], BF16)
        pt = ph.sb("pt", [P, 4, 2, P + WINDOW])
        oT = ph.sb("ot", [P, PAIRS, SEQ])
        zeros = ph.sb("zeros", [P, SEQ], BF16)
        ps_w = ph.ps("psw", [P, 4, SEQ])
        ps_s = ph.ps("pss", [P, SEQ])
        ps_t = ph.ps("pst", [P, SEQ])
        ps_o = ph.ps("pso", [P, 2, SEQ])
        names = ("loaded", "h_ready", "proj_ready", "swap_ready", "squared", "t1_ready", "t2_ready", "t_taken", "v_ready", "v_taken",
                 "stats_done", "stats_ready", "norm_ready", "rparts_ready", "spread_ready", "spread_taken", "sa_ready", "max_ready", "sum_ready",
                 "ln_ready", "shift_ready", "turned", "lrows_ready", "st_ready", "p_ready", "pv_done", "o_taken", "y_ready")
        (loaded, h_ready, proj_ready, swap_ready, squared, t1_ready, t2_ready, t_taken, v_ready, v_taken, stats_done, stats_ready,
         norm_ready, rparts_ready, spread_ready, spread_taken, sa_ready, max_ready, sum_ready, ln_ready, shift_ready, turned, lrows_ready,
         st_ready, p_ready, pv_done, o_taken, y_ready) = (ph.sem(n) for n in names)
        with nc.Block() as block:
            @block.sync
            def _(sp):
                for dst, src in ((w[:], t["L1_ffn_wqkv"][layer]), (wswap[:], t["L1_ffn_wswap"][layer]),
                                 (wo[:], t["L1_ffn_wo"][layer].rearrange("(i p) d -> p i d", p=P)), (tables[:], t["xpos"]),
                                 (scales[:], t["L1_ffn_scales"][layer]), (statsel[:], t["statsel"]), (spreadF[:], t["spread"]),
                                 (lselF[:], t["lsel"]), (maskF[:], t["band"])):
                    sp.dma_start(dst, src).then_inc(loaded, 16)
                sp.wait_ge(loaded, 16 * 9)

            @block.scalar
            def _(act):
                act.wait_ge(loaded, 16 * 9)
                for n in range(4):
                    act.activation(tables[:, n, :], tables[:, n, :], ACT.Copy, scale=scales[:, n:n + 1])
                act.copy(identb[:], c["ident"][:])
                act.copy(spread[:], spreadF[:])
                act.copy(lsel[:], lselF[:])
                act.copy(maskA[:], maskF[:, 0, :])
                act.copy(maskT[:], maskF[:, 1, :])

            @block.gpsimd
            def _(pool):
                pool.memset(h[:], 0.0)
                pool.memset(rparts[:], 0.0)
                pool.memset(zeros[:], 0.0)

            @block.vector
            def _(dve):
                dve.memset(kz[:], 0.0)
        clear(nc, ph.sems)

        units_a = [(hd, qt) for hd in range(H) for qt in range(TPS)]
        units_b = [(i, kt) for i in range(PAIRS) for kt in range(TPS)]
        wide = lambda kt: min(P + WINDOW, SEQ - kt * P)

        NA, NB = len(units_a), len(units_b)

        def section(block, b, main, front):
            y = cols(yT, b) if main else None
            yn = cols(yT, b + 1) if front else None

            @block.gpsimd
            def _(pool):
                if not front:
                    return
                pool.tensor_copy(h[0:64, :], yn[0:64, :])
                pool.tensor_copy(h[64:P, 1:SEQ], yn[64:P, 0:SEQ - 1])
                pool.drain().then_inc(h_ready, 1)
                for m in range(NQK):
                    pool.wait_ge(t2_ready, m + 1)
                    pool.tensor_tensor(raw[:, m, :], t1[:, m % 2, :], t2[:, m % 2, :], ALU.add).then_inc(t_taken, 1)

            @block.tensor
            def _(pe):
                def stats(m):
                    pe.wait_ge(squared, m + 1)
                    mm = pe.matmul(ps_s[0:2 * H, :], statsel[:, m, :], sq[:, m % 2, :], start=(m == 0), stop=(m == NQK - 1))
                    mm.then_inc(stats_done, 1)

                def turn_shift():
                    pe.wait_ge(shift_ready, 1)
                    for k in range(TPS):
                        mm = pe.transpose(ps_t[0:PARTS * H, k * P:(k + 1) * P], sparts[:, k, :, :].rearrange("p a h -> p (a h)"), c["ident"][:])
                    mm.then_inc(turned, 1)

                def weigh(n):
                    i, kt = units_b[n]
                    wd = wide(kt)
                    pe.wait_ge(p_ready, n + 1)
                    if kt == 0:
                        at_least(pe, o_taken, i - 1)
                        pe.matmul(ps_o[:, i % 2, :], zeros[:, 0:P], zeros[:], start=True, stop=True)
                    for e in range(2):
                        mm = pe.matmul(ps_o[64 * e:64 * e + 64, i % 2, kt * P:kt * P + wd], v[:, kt, (2 * i + e) * D:(2 * i + e + 1) * D],
                                       pt[:, n % 4, e, 0:wd], start=False, stop=True, skip_group_check=True)
                    mm.then_inc(pv_done, 1)

                if main:
                    for n, (hd, qt) in enumerate(units_a):
                        i, e = hd // 2, hd % 2
                        at_least(pe, sum_ready, n - 3)
                        k0 = max(qt * P - WINDOW, 0)
                        wd = (qt + 1) * P - k0
                        pe.matmul(ps_w[:, n % 4, 0:wd], q[:, i, qt * P:(qt + 1) * P], kz[:, e, i, k0:k0 + wd], start=True, stop=False)
                        pe.matmul(ps_w[:, n % 4, 0:wd], identb[:], maskA[:, P + WINDOW - wd:], start=False, stop=True).then_inc(sa_ready, 1)
                if front:
                    pe.wait_ge(h_ready, 1)
                    if main:
                        pe.wait_ge(sum_ready, NA)
                    for m in range(NQK):
                        at_least(pe, t1_ready, m - 1)
                        pe.matmul(ps_w[:, m % 2, :], w[:, m * P:(m + 1) * P], h[:], start=True, stop=True).then_inc(proj_ready, 1)
                        at_least(pe, t2_ready, m - 1)
                        pe.matmul(ps_w[:, 2 + m % 2, :], wswap[:, m, :], h[:], start=True, stop=True).then_inc(swap_ready, 1)
                        if m:
                            stats(m - 1)
                        if main and m == TURN_AT:
                            turn_shift()
                    stats(NQK - 1)
                    pe.wait_ge(t2_ready, NQK)
                elif main:
                    turn_shift()
                if main:
                    pe.wait_ge(sum_ready, NA)
                    pe.wait_ge(lrows_ready, 1)
                    for n, (i, kt) in enumerate(units_b):
                        wd = wide(kt)
                        at_least(pe, p_ready, n - 1)
                        for e in range(2):
                            out = ps_w[:, 2 * (n % 2) + e, 0:wd]
                            pe.matmul(out, kz[:, e, i, kt * P:(kt + 1) * P], q[:, i, kt * P:kt * P + wd], start=True, stop=False)
                            pe.matmul(out, identb[:], maskT[:, 0:wd], start=False, stop=False)
                            mm = pe.matmul(out, lsel[:, 2 * i + e, :], lrows[:, kt * P:kt * P + wd], start=False, stop=True)
                        mm.then_inc(st_ready, 1)
                        if n >= 2:
                            weigh(n - 2)
                    weigh(NB - 2)
                    weigh(NB - 1)
                for m in range(NQK) if front else ():
                    if m == 0:
                        pe.wait_ge(rparts_ready, 1)
                    at_least(pe, spread_taken, m - 1)
                    pe.matmul(ps_w[:, 2 + m % 2, :], spread[:, m, :], rparts[:], start=True, stop=True).then_inc(spread_ready, 1)
                    if m == 1 and main:
                        for i in range(PAIRS):
                            pe.wait_ge(o_taken, i + 1)
                            mm = pe.matmul(ps_s[:], wo[:, i, :], oT[:, i, :], start=(i == 0), stop=(i == PAIRS - 1))
                        mm.then_inc(y_ready, 1)
                for k in range(TPS) if front else ():
                    at_least(pe, v_taken, k - 1)
                    pe.matmul(ps_w[:, k % 2, :], h[:, k * P:(k + 1) * P], w[:, 2 * INNER:], start=True, stop=True).then_inc(v_ready, 1)
                if main and not front:
                    for i in range(PAIRS):
                        pe.wait_ge(o_taken, i + 1)
                        mm = pe.matmul(ps_s[:], wo[:, i, :], oT[:, i, :], start=(i == 0), stop=(i == PAIRS - 1))
                    mm.then_inc(y_ready, 1)

            @block.scalar
            def _(act):
                def take_shift():
                    act.wait_ge(turned, 1)
                    act.copy(lrows[:], ps_t[0:PARTS * H, :]).then_inc(lrows_ready, 1)

                if main:
                    for n, (hd, qt) in enumerate(units_a):
                        wd = (qt + 1) * P - max(qt * P - WINDOW, 0)
                        act.wait_ge(max_ready, n + 1)
                        act.activation(junk[:, 0:wd], ps_w[:, n % 4, 0:wd], ACT.Exp, bias=nm[:, qt, hd:hd + 1], accum_out=s[:, qt, hd:hd + 1])
                        act.drain().then_inc(sum_ready, 1)
                    act.activation(shift[:], s[:], ACT.Ln).then_inc(ln_ready, 1)
                if front:
                    for m in range(NQK):
                        act.wait_ge(proj_ready, m + 1)
                        at_least(act, stats_done, m - 1)
                        act.activation(sq[:, m % 2, :], ps_w[:, m % 2, :], ACT.Square).then_inc(squared, 1)
                        if main and m == TURN_AT + 1:
                            take_shift()
                    act.wait_ge(stats_done, NQK)
                    act.activation(norm[:], ps_s[0:2 * H, :], ACT.Sqrt).then_inc(norm_ready, 1)
                elif main:
                    take_shift()
                for n, (i, kt) in enumerate(units_b) if main else ():
                    wd = wide(kt)
                    act.wait_ge(st_ready, n + 1)
                    at_least(act, pv_done, n - 3)
                    act.activation(pt[:, n % 4, :, 0:wd], ps_w[:, 2 * (n % 2):2 * (n % 2) + 2, 0:wd], ACT.Exp).then_inc(p_ready, 1)
                for k in range(TPS) if front else ():
                    act.wait_ge(v_ready, k + 1)
                    act.copy(v[:, k, :], ps_w[:, k % 2, :]).then_inc(v_taken, 1)

            @block.vector
            def _(dve):
                for n, (hd, qt) in enumerate(units_a) if main else ():
                    wd = (qt + 1) * P - max(qt * P - WINDOW, 0)
                    dve.wait_ge(sa_ready, n + 1)
                    dve.tensor_reduce(nm[:, qt, hd:hd + 1], ps_w[:, n % 4, 0:wd], AX.X, ALU.max, negate=True).then_inc(max_ready, 1)
                if main:
                    dve.wait_ge(ln_ready, 1)
                    dve.tensor_tensor(shift[:], nm[:], shift[:], ALU.subtract)
                    dve.drain()
                    for n in range(PARTS):
                        dve.tensor_copy(spart[:], shift[:])
                        dve.drain()
                        dve.tensor_copy(sparts[:, :, n, :], spart[:])
                        if n < PARTS - 1:
                            dve.tensor_tensor(shift[:], shift[:], spart[:], ALU.subtract)
                        dve.drain()
                    dve.sem_inc(shift_ready, 1)
                if front:
                    for m in range(NQK):
                        tab = 0 if m < PAIRS else 2
                        dve.wait_ge(squared, m + 1)
                        at_least(dve, t_taken, m - 1)
                        dve.tensor_tensor(t1[:, m % 2, :], ps_w[:, m % 2, :], tables[:, tab, :], ALU.mult).then_inc(t1_ready, 1)
                        dve.wait_ge(swap_ready, m + 1)
                        dve.tensor_tensor(t2[:, m % 2, :], ps_w[:, 2 + m % 2, :], tables[:, tab + 1, :], ALU.mult)
                        dve.drain().then_inc(t2_ready, 1)
                    dve.wait_ge(norm_ready, 1)
                    dve.tensor_scalar(norm[:], norm[:], 1e-12, None, ALU.max)
                    dve.drain()
                    dve.reciprocal(rnorm[:], norm[:])
                    dve.drain()
                    R = 2 * H
                    dve.tensor_copy(rparts[0:R, :], rnorm[:])
                    dve.drain()
                    dve.tensor_tensor(left[:], rnorm[:], rparts[0:R, :], ALU.subtract)
                    dve.drain()
                    dve.tensor_copy(mid[:], left[:])
                    dve.drain()
                    dve.tensor_copy(rparts[32:32 + R, :], mid[:])
                    dve.tensor_tensor(left[:], left[:], mid[:], ALU.subtract)
                    dve.drain()
                    dve.tensor_copy(rparts[64:64 + R, :], left[:])
                    dve.drain().then_inc(rparts_ready, 1)
                for i in range(PAIRS) if main else ():
                    dve.wait_ge(pv_done, TPS * (i + 1))
                    dve.tensor_copy(oT[:, i, :], ps_o[:, i % 2, :]).then_inc(o_taken, 1)
                if front:
                    dve.wait_ge(t_taken, NQK)
                    for m in range(NQK):
                        dve.wait_ge(spread_ready, m + 1)
                        if m < PAIRS:
                            dve.tensor_tensor(q[:, m, :], raw[:, m, :], ps_w[:, 2 + m % 2, :], ALU.mult).then_inc(spread_taken, 1)
                        else:
                            for e in range(2):
                                rows = slice(64 * e, 64 * e + 64)
                                tt = dve.tensor_tensor(kz[rows, e, m - PAIRS, :], raw[rows, m, :], ps_w[rows, 2 + m % 2, :], ALU.mult)
                            tt.then_inc(spread_taken, 1)
                        if m == 2 and main:
                            dve.wait_ge(y_ready, 1)
                            dve.tensor_tensor(y, y, ps_s[:], ALU.add)
                elif main:
                    dve.wait_ge(y_ready, 1)
                    dve.tensor_tensor(y, y, ps_s[:], ALU.add)

        with nc.Block() as block:
            section(block, -1, False, True)
        clear(nc, ph.sems)
        with nc.Fori(0, NSEQ - 1) as b:
            with nc.Block() as block:
                section(block, b, True, True)
            clear(nc, ph.sems)
        with nc.Block() as block:
            section(block, NSEQ - 1, True, False)
        clear(nc, ph.sems)


def geglu(nc, yT, c, t, layer):
    U = 3
    with ExitStack() as ctx:
        ph = Phase(nc, ctx, f"l1g{layer}")
        hT = ph.sb("ht", [P, TOK])
        wa, wb, wo = (ph.sb(n, [P, U, P]) for n in ("wa", "wb", "wo"))
        b_a, b_g = ph.sb("b_a", [P, U]), ph.sb("b_g", [P, U])
        b2, lg, lb = ph.sb("b2", [P, 1]), ph.sb("lg", [P, 1]), ph.sb("lb", [P, 1])
        loaded = ph.sem("loaded")
        with nc.Block() as block:
            @block.sync
            def _(sp):
                for dst, src in ((wa, t["L1_ffn_w1u"][layer, :, 0]), (wb, t["L1_ffn_w1u"][layer, :, 1]), (wo, t["L1_ffn_w2u"][layer]),
                                 (b_a, t["L1_ffn_b1u"][layer, :, 0]), (b_g, t["L1_ffn_b1u"][layer, :, 1]),
                                 (b2, t["L1_ffn_b2"][layer].unsqueeze(1)), (lg, t["L1_ffn_ln_g"][layer].unsqueeze(1)),
                                 (lb, t["L1_ffn_ln_b"][layer].unsqueeze(1))):
                    sp.dma_start(dst[:], src).then_inc(loaded, 16)
                sp.wait_ge(loaded, 16 * 8)

            h3 = hT[:].rearrange("p (b s) -> p b s", s=SEQ)
            y3 = yT[:].rearrange("p (b s) -> p b s", s=SEQ)

            @block.vector
            def _(dve):
                dve.tensor_copy(hT[0:64, :], yT[0:64, :])
                dve.memset(h3[64:P, :, 0:1], 0.0)

            @block.scalar
            def _(act):
                act.copy(h3[64:P, :, 1:SEQ], y3[64:P, :, 0:SEQ - 1])
        clear(nc, ph.sems)
        normalize(nc, hT, hT, c, f"l1gn{layer}", EPS)
        with nc.Block() as block:
            @block.scalar
            def _(act):
                act.activation(hT[:], hT[:], ACT.Identity, scale=lg[:], bias=lb[:])
        experts(nc, yT, hT, c, ph, U, wa, wb, wo, None, None, "geglu", b_a, b_g, None, bias=b2)


def load_x(nc, xT, c, t):
    with ExitStack() as ctx:
        ph = Phase(nc, ctx, "load")
        x = ph.sb("x", [P, NT, P])
        ps = ph.ps("ps", [P, 4, TPS, P])
        loaded, turned, copied = (ph.sem(n) for n in ("loaded", "turned", "copied"))
        ctx.callback(clear, nc, ph.sems)
        block = ctx.enter_context(nc.Block())

        @block.sync
        def _(sp):
            for n in c:
                sp.dma_start(c[n][:], t[n]).then_inc(loaded, 16)
            sp.dma_start(x[:], t["L0_attn_hidden_states"].rearrange("b (k p) d -> p (b k) d", p=P)).then_inc(loaded, 16)

        @block.tensor
        def _(pe):
            pe.wait_ge(loaded, 16 * (len(c) + 1))
            for b in range(NSEQ):
                if b >= 4:
                    pe.wait_ge(copied, b - 3)
                for k in range(TPS):
                    mm = pe.transpose(ps[:, b % 4, k, :], x[:, b * TPS + k, :], c["ident"][:])
                mm.then_inc(turned, 1)

        @block.scalar
        def _(act):
            for b in range(NSEQ):
                act.wait_ge(turned, b + 1)
                act.copy(cols(xT, b), ps[:, b % 4, :, :].rearrange("p k q -> p (k q)")).then_inc(copied, 1)


def store_x(nc, xT, c, out):
    with ExitStack() as ctx:
        ph = Phase(nc, ctx, "store")
        x = ph.sb("x", [P, NT, P])
        ps = ph.ps("ps", [P, 4, TPS, P])
        turned, copied, stored = (ph.sem(n) for n in ("turned", "copied", "stored"))
        ctx.callback(clear, nc, ph.sems)
        block = ctx.enter_context(nc.Block())

        @block.tensor
        def _(pe):
            for b in range(NSEQ):
                if b >= 4:
                    pe.wait_ge(copied, b - 3)
                for k in range(TPS):
                    mm = pe.transpose(ps[:, b % 4, k, :], xT[:, (b * TPS + k) * P:(b * TPS + k + 1) * P], c["ident"][:])
                mm.then_inc(turned, 1)

        @block.scalar
        def _(act):
            for b in range(NSEQ):
                act.wait_ge(turned, b + 1)
                act.copy(x[:, b * TPS:(b + 1) * TPS, :], ps[:, b % 4, :, :]).then_inc(copied, 1)

        @block.sync
        def _(sp):
            for b in range(NSEQ):
                sp.wait_ge(copied, b + 1)
                sp.dma_start(out[b].rearrange("(k p) d -> p k d", p=P), x[:, b * TPS:(b + 1) * TPS, :]).then_inc(stored, 16)
            sp.wait_ge(stored, 16 * NSEQ)


PHASE_FUNCS = [l0_attn, l0_ffn, l1_attn, l1_ffn, l2_attn, l2_ffn, l3_attn, l3_ffn]


def program(nc, t, out):
    with ExitStack() as ctx:
        ph = Phase(nc, ctx, "main")
        xT = ph.sb("xT", [P, TOK])
        xnT = ph.sb("xnT", [P, TOK])
        c = {n: ph.sb(n, [P, P]) for n in ("ident", "mean", "center", "ones")}
        load_x(nc, xT, c, t)
        for n, f in enumerate(PHASE_FUNCS):
            if n in PHASES and f:
                f(nc, xT, xnT, c, t)
        store_x(nc, xT, c, out)


def constants():
    n = np.arange(P)
    ang = 2 * np.pi * ((n[:, None] * n[None, :]) % P) / P
    c, s = np.cos(ang), np.sin(ang)
    q = np.arange(P)
    d = 2 * ((np.arange(P) % 8) // 2)
    inv_freq = (1.0 / np.float32(10000.0) ** (d.astype(np.float32) / np.float32(8))).astype(np.float32)
    freqs = (np.arange(SEQ, dtype=np.float32)[None, :] * inv_freq[:, None]).astype(np.float32).astype(np.float64)
    sign = np.where(np.arange(P) % 2 == 0, -1.0, 1.0)[:, None]
    head = q // 8
    blocks = np.concatenate([head[:, None] == head[None, :], head[:, None] == np.arange(16)[None, :]], 1)
    sel8 = np.zeros((3, 32, 8, P), np.float32)
    sel8[:, np.arange(8), np.arange(8), :] = 1
    half = np.arange(0, 64, 2, dtype=np.float32)
    inv64 = (np.float32(1.0) / np.float32(10000.0) ** (half / np.float32(64))).astype(np.float32)
    tt = np.arange(SEQ, dtype=np.float32)
    fr = (tt[None, :] * inv64[:, None]).astype(np.float32).astype(np.float64)
    base = ((half + np.float32(25.6)) / np.float32(89.6)).astype(np.float32).astype(np.float64)
    xp = base[:, None] ** ((tt - SEQ // 2) / 32.0)[None, :].astype(np.float64)
    two = lambda first, second: np.concatenate([first, second] * 2, 0)
    cos64, sin64 = np.cos(fr), np.sin(fr)
    xpos = np.stack([8 * two(cos64 * xp, cos64 * xp), 8 * two(-sin64 * xp, sin64 * xp),
                     two(cos64 / xp, cos64 / xp), two(-sin64 / xp, sin64 / xp)], 1)
    m8, f = np.arange(8), np.arange(P)
    statsel = (np.arange(16)[None, None, :] == 2 * m8[None, :, None] + f[:, None, None] // 64).astype(np.float32)
    spread = np.zeros((3, 32, 8, P), np.float32)
    spread[:, :16] = statsel.transpose(2, 1, 0)
    lsel = np.broadcast_to(np.eye(8, dtype=np.float32)[None, :, :, None], (3, 8, 8, P)).reshape(24, 8, P)
    jj = np.arange(192)
    da, dt = f[:, None] + 64 - jj[None, :], jj[None, :] - f[:, None]
    band = np.stack([np.where((d >= 0) & (d <= 64), 0, -1e30) for d in (da, dt)], 1)
    sel32 = np.zeros((3, 32, 16, P), np.float32)
    sel32[:, np.arange(32)[:, None], np.arange(32)[:, None] // 2, np.arange(32)[:, None] % 2 * 64 + np.arange(64)] = 1
    c32 = np.arange(32)
    tri = np.stack([c32[None, :] > c32[:, None], c32[None, :] >= c32[:, None], c32[None, :] == c32[:, None]], 1)
    return {
        "heads4": (q[:, None] // 32 == np.arange(4)[None, :]).astype(np.float32),
        "tri32": np.tile(tri, (4, 1, 1)).astype(np.float32),
        "xpos": xpos.astype(np.float32), "statsel": statsel, "spread": spread.reshape(96, 8, P), "lsel": lsel, "band": band.astype(np.float32),
        "sel32": sel32.reshape(96, 16, P),
        "blocks8": blocks.astype(np.float32),
        "sel8": sel8.reshape(96, 8, P),
        "causal": np.stack([np.where(q[None, :] > q[:, None], -1e30, 0), np.where(q[None, :] < q[:, None], -1e30, 0)]).astype(np.float32),
        "rope8": np.stack([np.cos(freqs), sign * np.sin(freqs)]).astype(np.float32),
        "ident": np.eye(P, dtype=np.float32),
        "ones": np.ones((P, P), np.float32),
        "center": (np.eye(P) - 1.0 / P).astype(np.float32),
        "mean": np.full((P, P), 1.0 / P, np.float32),
        "dft": np.stack([c, s, c / P, -s / P, -s]).astype(np.float32),
    }


def laid_out(inputs):
    x = {n: np.asarray(a) for n, a in inputs.items()}
    x["L0_attn_Wb_wide"] = np.repeat(x.pop("L0_attn_Wb"), 32, 1)
    for n in ("short", "long"):
        x[f"L0_attn_fir_{n}_wp"] = x.pop(f"L0_attn_fir_{n}_w").reshape(P, -1)
    w1 = x.pop("L0_attn_mlp_w1")
    zeros = lambda *shape: np.zeros(shape, w1.dtype)
    x["L0_attn_w1a"] = w1[:P]
    x["L0_attn_w1b"] = np.tile(np.concatenate([w1[P:], zeros(16, P)]), (4, 1))
    x["L0_attn_w2p"] = np.concatenate([x.pop("L0_attn_mlp_w2"), zeros(P, 28)], 1)
    x["L0_attn_b1"] = x.pop("L0_attn_mlp_b1").reshape(P, 1)
    x["L0_attn_b2p"] = np.tile(np.concatenate([x.pop("L0_attn_mlp_b2"), zeros(28)]), 4).reshape(P, 1)
    x["L0_attn_temp"] = np.repeat(x.pop("L0_attn_log_temp").reshape(4), 32).reshape(P, 1)
    x["L0_attn_onorm"] = np.tile(x.pop("L0_attn_o_norm_w"), 4).reshape(P, 1)
    for n in ("Wq", "Wk", "Wv", "Wo"):
        x[f"L1_attn_{n}T"] = x.pop(f"L1_attn_{n}").T
    x["L3_attn_w_swapped"] = x["L3_attn_w_qkv"].reshape(P, 3, P // 2, 2)[:, :2, :, ::-1].reshape(P, 2, P)
    for n in ("gate_w", "sw1", "sw2", "sw3"):
        x[f"L2_ffn_{n}T"] = x.pop(f"L2_ffn_{n}").T
    for n in ("W1", "W3"):
        x[f"L2_ffn_{n}p"] = x.pop(f"L2_ffn_{n}").transpose(1, 0, 2).reshape(P, 16, P)
    x["L2_ffn_W2p"] = x.pop("L2_ffn_W2").reshape(16, P, P).transpose(1, 0, 2)
    swap = lambda a: np.roll(a.reshape(*a.shape[:-1], a.shape[-1] // 64, 2, 32), 1, axis=-2).reshape(a.shape)
    x["L1_ffn_wswap"] = swap(x["L1_ffn_wqkv"][:, :, :1024]).reshape(2, P, 8, P)
    qs, ks = x.pop("L1_ffn_q_scale"), x.pop("L1_ffn_k_scale")
    x["L1_ffn_scales"] = np.tile(np.stack([qs, swap(qs), ks, swap(ks)], -1), (1, 2, 1))
    pad = lambda a, axis: np.concatenate([a, np.zeros_like(np.take(a, range(3 * P - 341), axis))], axis)
    x["L1_ffn_w1u"] = pad(x.pop("L1_ffn_w1").reshape(2, P, 2, 341), 3).reshape(2, P, 2, 3, P)
    x["L1_ffn_b1u"] = pad(x.pop("L1_ffn_b1").reshape(2, 2, 341), 2).reshape(2, 2, 3, P).transpose(0, 3, 1, 2)
    x["L1_ffn_w2u"] = pad(x.pop("L1_ffn_w2"), 1).reshape(2, 3, P, P).transpose(0, 2, 1, 3)
    w1 = x.pop("L3_ffn_mlp1_w").reshape(8, P, 2, P)
    x["L3_ffn_w1T"] = w1.transpose(3, 0, 2, 1)
    x["L3_ffn_b1T"] = x.pop("L3_ffn_mlp1_b").reshape(8, P, 2).transpose(1, 2, 0)
    x["L3_ffn_w2T"] = x.pop("L3_ffn_mlp2_w").transpose(2, 0, 1)
    x["L3_ffn_gate_wT"] = x.pop("L3_ffn_gate_w").T
    return x


def kernel(**inputs):
    import concourse.bacc as bacc
    from concourse.bass_utils import run_bass_kernel_spmd

    nc = bacc.Bacc("TRN2", target_bir_lowering=False, num_devices=1)
    arrays, t = {}, {}
    for name, a in {**laid_out(inputs), **constants()}.items():
        a = np.ascontiguousarray(a)
        arrays[f"in_{name}"] = a
        t[name] = nc.dram_tensor(f"in_{name}", a.shape, mybir.dt.from_np(a.dtype), kind="ExternalInput").ap()
    out = nc.dram_tensor("out_x", (NSEQ, SEQ, P), F32, kind="ExternalOutput").ap()
    program(nc, t, out)
    r = run_bass_kernel_spmd(nc, [arrays], core_ids=[0])
    return r.results[0]["out_x"]
```

```python
from contextlib import ExitStack

import numpy as np

import concourse.bass as bass
from concourse import mybir

ALU = mybir.AluOpType
ACT = mybir.ActivationFunctionType
AX = mybir.AxisListType
F32 = mybir.dt.float32
BF16 = mybir.dt.bfloat16

P = 128
NSEQ = 8
SEQ = 512
TPS = SEQ // P
NT = NSEQ * TPS
TOK = NSEQ * SEQ
EPS = 1e-5


class Phase:

    def __init__(self, nc, ctx, name):
        self.nc, self.ctx, self.name, self.sems = nc, ctx, name, []

    def sb(self, name, shape, dt=F32):
        return self.ctx.enter_context(self.nc.sbuf_tensor(f"{self.name}_{name}", list(shape), dt))

    def ps(self, name, shape, dt=F32):
        return self.ctx.enter_context(self.nc.psum_tensor(f"{self.name}_{name}", list(shape), dt))

    def sem(self, name):
        self.sems.append(self.ctx.enter_context(self.nc.semaphore(f"{self.name}_{name}")))
        return self.sems[-1]


def at_least(engine, sem, n):
    if n > 0:
        engine.wait_ge(sem, n)


def clear(nc, sems):
    ids = sorted(s.num for s in sems)
    nc.gpsimd.sem_clear(range(ids[0], ids[-1] + 1))
    nc.all_engine_barrier()


def bcast(ap, n):
    return ap.unsqueeze(2).to_broadcast([ap.shape[0], ap.shape[1], n])


def cols(x, b, n=1):
    return x[:, bass.ds(b * SEQ, n * SEQ)]


def normalize(nc, xT, xnT, c, name, eps, center=True):
    U = 4
    with ExitStack() as ctx:
        ph = Phase(nc, ctx, name)
        sq, rstd = ph.sb("sq", [P, U, SEQ]), ph.sb("rstd", [P, TOK])
        epst = ph.sb("eps", [P, 1])
        ps_c, ps_v = (ph.ps(n, [P, U, SEQ]) for n in ("psc", "psv"))
        centered, squared, copied, var_ready, logged, rstd_ready, eps_set = (
            ph.sem(n) for n in ("centered", "squared", "copied", "var_ready", "logged", "rstd_ready", "eps_set"))
        ctx.callback(clear, nc, ph.sems)
        block = ctx.enter_context(nc.Block())

        @block.tensor
        def _(pe):
            pe.sem_inc(logged, U)
            with pe.Fori(0, NSEQ // U) as i:
                for j in range(U):
                    pe.wait_ge(copied, U * i + j + 1)
                    pe.matmul(ps_c[:, j, :], c["center" if center else "ident"][:], cols(xT, U * i + j), start=True,
                              stop=True).then_inc(centered, 1)
                for j in range(U):
                    pe.wait_ge(squared, U * i + j + 1)
                    pe.wait_ge(logged, U * i + j + 1)
                    pe.matmul(ps_v[:, j, :], c["mean"][:], sq[:, j, :], start=True, stop=True).then_inc(var_ready, 1)

        @block.scalar
        def _(act):
            act.wait_ge(eps_set, 1)
            with act.Fori(0, NSEQ // U) as i:
                for j in range(U):
                    act.wait_ge(centered, U * i + j + 1)
                    act.activation(sq[:, j, :], ps_c[:, j, :], ACT.Square).then_inc(squared, 1)
                for j in range(U):
                    act.wait_ge(var_ready, U * i + j + 1)
                    act.activation(cols(rstd, U * i + j), ps_v[:, j, :], ACT.Ln, bias=epst[:]).then_inc(logged, 1)
            act.drain()
            for b in range(0, NSEQ, 2):
                act.activation(cols(rstd, b, 2), cols(rstd, b, 2), ACT.Exp, scale=-0.5).then_inc(rstd_ready, 1)

        @block.vector
        def _(dve):
            dve.sem_inc(copied, U)
            dve.memset(epst[:], eps).then_inc(eps_set, 1)
            with dve.Fori(0, NSEQ // U) as i:
                for j in range(U):
                    dve.wait_ge(squared, U * i + j + 1)
                    dve.tensor_copy(cols(xnT, U * i + j), ps_c[:, j, :]).then_inc(copied, 1)
            dve.drain()
            for b in range(0, NSEQ, 2):
                dve.wait_ge(rstd_ready, b // 2 + 1)
                dve.tensor_tensor(cols(xnT, b, 2), cols(xnT, b, 2), cols(rstd, b, 2), ALU.mult)


def add_normed(nc, xT, xnT):
    with nc.Block() as block:
        half = TOK // 2

        @block.vector
        def _(dve):
            dve.tensor_tensor(xT[:, 0:half], xT[:, 0:half], xnT[:, 0:half], ALU.add)

        @block.gpsimd
        def _(pool):
            pool.tensor_tensor(xT[:, half:], xT[:, half:], xnT[:, half:], ALU.add)


def l0_attn(nc, xT, xnT, c, t):
    normalize(nc, xT, xnT, c, "l0an", EPS)
    with ExitStack() as outer:
        ph = Phase(nc, outer, "l0a")
        k, v = ph.sb("k", [P, TOK]), ph.sb("v", [P, TOK])
        heads, tri = ph.sb("heads", [P, L0_H]), ph.sb("tri", [P, 3, L0_C])
        loaded = ph.sem("loaded")
        with nc.Block() as block:
            @block.sync
            def _(sp):
                sp.dma_start(heads[:], t["heads4"]).then_inc(loaded, 16)
                sp.dma_start(tri[:], t["tri32"]).then_inc(loaded, 16)
                sp.wait_ge(loaded, 16 * 2)
        clear(nc, ph.sems)
        with ExitStack() as inner:
            ph = Phase(nc, inner, "l0d")
            q, att, tt = (ph.sb(n, [P, TOK]) for n in ("q", "att", "tt"))
            beta = ph.sb("beta", [P, NSEQ * L0_N])
            delta_inputs(nc, xnT, t, q, k, v, att, tt, beta, heads, tri)
            delta_inverse(nc, tt)
            delta_chunks(nc, q, k, v, att, tt, beta, heads, tri)
            delta_scan(nc, q, k, att, tt, heads)
        with ExitStack() as inner:
            ph = Phase(nc, inner, "l0m")
            short, long = ph.sb("short", [P, TOK]), ph.sb("long", [P, TOK])
            filters(nc, c, t, v, short, long)
            gated_mix(nc, xT, xnT, t, (short, long, k, v))


L0_H, L0_C = 4, 32
L0_N = SEQ // L0_C


def chunks(ap):
    return ap.rearrange("p (n d) -> p n d", d=L0_C)


def each_chunk(ap, n):
    return ap.unsqueeze(1).to_broadcast([P, n, L0_C])


def diagonal(engine, out, x, heads, n):
    return engine.tensor_tensor(out, x.unsqueeze(2).to_broadcast([P, n, L0_H, L0_C]),
                                heads[:].unsqueeze(1).unsqueeze(3).to_broadcast([P, n, L0_H, L0_C]), ALU.mult)


def delta_inputs(nc, xnT, t, q, k, v, att, tt, beta, heads, tri):
    H, C, N, TAPS = L0_H, L0_C, L0_N, 4
    with ExitStack() as ctx:
        ph = Phase(nc, ctx, "l0i")
        w, wt = ph.sb("w", [P, 4, P]), ph.sb("wt", [P, 3, TAPS, P])
        eps = ph.sb("eps", [P, 1])
        y = ph.sb("y", [P, 2, 4, SEQ])
        yK = ph.sb("yk", [P, 2, 3, SEQ])
        bt, kb = ph.sb("bt", [P, SEQ]), ph.sb("kb", [P, 2, SEQ])
        sq = ph.sb("sq", [P, 2, 2, SEQ])
        ss, rn = ph.sb("ss", [P, 2, 2, N]), ph.sb("rn", [P, 2, 2, N])
        kF, kbq = ph.sb("kf", [P, 2, SEQ]), ph.sb("kbq", [P, 2, N, 2, C])
        kbd = ph.sb("kbd", [P, 2, N, H, C])
        ps = ph.ps("ps", [P, 2, 4, SEQ])
        (loaded, proj_ready, silu_ready, beta_ready, turned, squared, ss_ready, root_ready, kf_ready, kbd_ready, kbq_ready,
         am_ready, normed) = (ph.sem(n) for n in (
             "loaded", "proj_ready", "silu_ready", "beta_ready", "turned", "squared", "ss_ready", "root_ready",
             "kf_ready", "kbd_ready", "kbq_ready", "am_ready", "normed"))
        with nc.Block() as block:
            @block.sync
            def _(sp):
                for n, name in enumerate(("Wq", "Wk", "Wv", "Wb_wide")):
                    sp.dma_start(w[:, n, :], t[f"L0_attn_{name}"]).then_inc(loaded, 16)
                sp.dma_start(wt[:], t["L0_attn_taps"].unsqueeze(0).to_broadcast([P, 3, TAPS, P])).then_inc(loaded, 16)
                sp.wait_ge(loaded, 16 * 5)

            @block.vector
            def _(dve):
                dve.memset(eps[:], 1e-6)
                dve.wait_ge(loaded, 16 * 5)
                dve.tensor_tensor(wt[:], wt[:], w[:, 0:3, :].unsqueeze(2).to_broadcast([P, 3, TAPS, P]), ALU.mult)
        clear(nc, ph.sems)

        def section(block, b):
            beta_of = lambda r: beta[:, bass.ds((b + r) * N, N)]
            both = range(2)

            @block.tensor
            def _(pe):
                for r in both:
                    for n in range(3):
                        for s in range(TAPS):
                            mm = pe.matmul(ps[:, r, n, s:], wt[:, n, TAPS - 1 - s, :], xnT[:, bass.ds((b + r) * SEQ, SEQ - s)],
                                           start=(s == 0), stop=True, skip_group_check=True)
                        mm.then_inc(proj_ready, 1)
                    pe.matmul(ps[:, r, 3, :], w[:, 3, :], cols(xnT, b + r), start=True, stop=True).then_inc(proj_ready, 1)
                for r in both:
                    pe.wait_ge(kbd_ready, H * (r + 1))
                    pe.wait_ge(kbq_ready, 2 * (r + 1))
                    for n in range(N):
                        width = 1 if n % 8 == 7 else 2
                        pe.matmul(ps[:, r, n // 8, (n % 8) * 2 * C:(n % 8 + width) * 2 * C], kbd[:, r, n, :, :].rearrange("p h c -> p (h c)"),
                                  kbq[:, r, n:n + width, :, :].rearrange("p n w d -> p (n w d)"), start=True, stop=True).then_inc(am_ready, 1)

            @block.scalar
            def _(act):
                for r in both:
                    for n in range(3):
                        act.wait_ge(proj_ready, 4 * r + n + 1)
                        act.activation(y[:, r, n, :], ps[:, r, n, :], ACT.Silu).then_inc(silu_ready, 1)
                    act.wait_ge(proj_ready, 4 * (r + 1))
                    act.activation(y[:, r, 3, :], ps[:, r, 3, :], ACT.Sigmoid).then_inc(beta_ready, 1)
                    for n in range(2):
                        act.wait_ge(turned, 3 * r + n + 1)
                        act.activation(sq[:, r, n, :], yK[:, r, n, :], ACT.Square).then_inc(squared, 1)
                    act.wait_ge(ss_ready, 2 * (r + 1))
                    act.activation(rn[:, r], ss[:, r], ACT.Sqrt, bias=eps[:]).then_inc(root_ready, 1)
                    act.wait_ge(kf_ready, r + 1)
                    for h in range(H):
                        act.activation(kbd[:, r, :, h, :], chunks(kF[:, r, :]), ACT.Copy, scale=heads[:, h:h + 1]).then_inc(kbd_ready, 1)

            @block.gpsimd
            def _(pool):
                for r in both:
                    pool.wait_ge(turned, 3 * (r + 1))
                    pool.tensor_copy(cols(v, b + r), yK[:, r, 2, :])
                for r in both:
                    pool.wait_ge(normed, 2 * (r + 1))
                    pool.tensor_copy(cols(k, b + r), yK[:, r, 1, :])
                    pool.tensor_copy(cols(q, b + r), yK[:, r, 0, :])

            @block.vector
            def _(dve):
                for r in both:
                    for n in range(3):
                        dve.wait_ge(silu_ready, 3 * r + n + 1)
                        dve.transpose(yK[:, r, n, :], y[:, r, n, :]).then_inc(turned, 1)
                    dve.wait_ge(beta_ready, r + 1)
                    dve.transpose(bt[:], y[:, r, 3, :])
                    dve.drain()
                    dve.tensor_copy(beta_of(r).unsqueeze(2), chunks(bt[:])[:, :, 0:1])
                    dve.drain()
                    for n in range(2):
                        dve.wait_ge(squared, 2 * r + n + 1)
                        dve.tensor_reduce(ss[:, r, n, :], chunks(sq[:, r, n, :]), AX.X, ALU.add).then_inc(ss_ready, 1)
                    dve.wait_ge(root_ready, r + 1)
                    dve.reciprocal(rn[:, r], rn[:, r])
                    dve.drain()
                    for n in (1, 0):
                        dve.tensor_tensor(chunks(yK[:, r, n, :]), chunks(yK[:, r, n, :]), bcast(rn[:, r, n, :], C), ALU.mult).then_inc(normed, 1)
                    dve.drain()
                    dve.transpose(kF[:, r, :], yK[:, r, 1, :]).then_inc(kf_ready, 1)
                    dve.tensor_tensor(chunks(kb[:, r, :]), chunks(yK[:, r, 1, :]), bcast(beta_of(r), C), ALU.mult)
                    dve.transpose(kbq[:, r, :, 1, :], chunks(yK[:, r, 0, :])).then_inc(kbq_ready, 1)
                    dve.drain()
                    dve.transpose(kbq[:, r, :, 0, :], chunks(kb[:, r, :])).then_inc(kbq_ready, 1)
                for r in both:
                    for g in range(2):
                        dve.wait_ge(am_ready, N * r + 8 * (g + 1))
                        two = ps[:, r, g, :].rearrange("p (n w d) -> p n w d", w=2, d=C)
                        for which, dst in enumerate((tt, att)):
                            dve.tensor_tensor(chunks(cols(dst, b + r))[:, 8 * g:8 * g + 8, :], two[:, :, which, :],
                                              each_chunk(tri[:, which, :], 8), ALU.mult)

        with nc.Fori(0, NSEQ // 2) as i:
            with nc.Block() as block:
                section(block, 2 * i)
            clear(nc, ph.sems)


def delta_inverse(nc, tt):
    H, C = L0_H, L0_C
    with ExitStack() as ctx:
        ph = Phase(nc, ctx, "l0t")
        a, x, tmp = (ph.sb(n, [P, H, C, C]) for n in ("a", "x", "tmp"))
        a_scratch = nc.dram_tensor("l0_a_scratch", (P, P, C), F32, kind="Internal").ap()
        t_scratch = nc.dram_tensor("l0_t_scratch", (P, P, C), F32, kind="Internal").ap()
        a_stored, a_loaded, t_stored, t_loaded, solved = (ph.sem(n) for n in ("a_stored", "a_loaded", "t_stored", "t_loaded", "solved"))
        ctx.callback(clear, nc, ph.sems)
        block = ctx.enter_context(nc.Block())
        shares = {"dve": (0, 3), "pool": (3, 4)}

        def solve(engine, lo, hi):
            n = hi - lo
            xs = x[:, lo:hi]
            engine.memset(xs, 0.0)
            engine.drain()
            engine.memset(xs.rearrange("p h c i -> p h (c i)")[:, :, 0:C * C:C + 1], 1.0)
            engine.drain()
            engine.wait_ge(a_loaded, 16 * H)
            for j in range(C - 1):
                rows, rest = j + 1, C - 1 - j
                m = tmp[:, lo:hi, 0:rows, 0:rest]
                engine.tensor_tensor(m, a[:, lo:hi, j:j + 1, j + 1:].to_broadcast([P, n, rows, rest]),
                                     xs[:, :, 0:rows, j:j + 1].to_broadcast([P, n, rows, rest]), ALU.mult)
                engine.drain()
                engine.tensor_tensor(xs[:, :, 0:rows, j + 1:], xs[:, :, 0:rows, j + 1:], m, ALU.subtract)
                engine.drain()
            engine.sem_inc(solved, 1)

        @block.sync
        def _(sp):
            sp.dma_start(a_scratch, tt[:].rearrange("p (n i) -> p n i", i=C)).then_inc(a_stored, 16)
            sp.wait_ge(a_stored, 16)
            for h in range(H):
                sp.dma_start(a[:, h], a_scratch[h * C:(h + 1) * C].rearrange("j n i -> n j i")).then_inc(a_loaded, 16)
            sp.wait_ge(a_loaded, 16 * H)
            sp.wait_ge(solved, 2)
            sp.dma_start(t_scratch, x[:].rearrange("p h c i -> p (h c) i")).then_inc(t_stored, 16)
            sp.wait_ge(t_stored, 16)
            for h in range(H):
                sp.dma_start(tt[h * C:(h + 1) * C].rearrange("p (n i) -> p n i", i=C),
                             t_scratch[:, h * C:(h + 1) * C].rearrange("n c i -> c n i")).then_inc(t_loaded, 16)
            sp.wait_ge(t_loaded, 16 * H)

        @block.vector
        def _(dve):
            solve(dve, *shares["dve"])

        @block.gpsimd
        def _(pool):
            solve(pool, *shares["pool"])


def delta_chunks(nc, q, k, v, att, tt, beta, heads, tri):
    H, C, N = L0_H, L0_C, L0_N
    with ExitStack() as ctx:
        ph = Phase(nc, ctx, "l0c")
        vk, uw = ph.sb("vk", [P, 2, N, 2, C]), ph.sb("uw", [P, 2, N, 2, C])
        tbd, kbd, abd = (ph.sb(n, [P, 2, N, H, C]) for n in ("tbd", "kbd", "abd"))
        qp, qpT, kw, kwT = (ph.sb(n, [P, SEQ]) for n in ("qp", "qpt", "kw", "kwt"))
        ps_uw, ps_k = (ph.ps(n, [P, 2, 2, SEQ]) for n in ("psuw", "psk"))
        ps_a = ps_uw
        vk_ready, tbd_ready, kbd_ready, abd_ready, uw_done, uw_ready, k_done, a_done, q_turned, q_copied = (ph.sem(n) for n in (
            "vk_ready", "tbd_ready", "kbd_ready", "abd_ready", "uw_done", "uw_ready", "k_done", "a_done", "q_turned", "q_copied"))
        flat = lambda x, r, n: x[:, r, n, :, :].rearrange("p h c -> p (h c)")
        half = lambda ps, r, g: ps[:, r, g, :].rearrange("p (n w d) -> p n w d", w=2, d=C)
        width = lambda n: 1 if n % 8 == 7 else 2
        place = lambda r, n: (slice(None), r, n // 8, slice((n % 8) * 2 * C, (n % 8 + width(n)) * 2 * C))
        wide = lambda x, r, n: x[:, r, n:n + width(n), :, :].rearrange("p n w d -> p (n w d)")

        def section(block, b):
            both = range(2)
            beta_of = lambda r: beta[:, bass.ds((b + r) * N, N)]
            at = lambda x, r, g: chunks(cols(x, b + r))[:, 8 * g:8 * g + 8, :]

            @block.tensor
            def _(pe):
                for r in both:
                    pe.wait_ge(vk_ready, 2 * (r + 1))
                    pe.wait_ge(tbd_ready, H * (r + 1))
                    for n in range(N):
                        pe.matmul(ps_uw[place(r, n)], flat(tbd, r, n), wide(vk, r, n), start=True, stop=True).then_inc(uw_done, 1)
                for r in both:
                    pe.wait_ge(kbd_ready, r + 1)
                    for n in range(N):
                        if n % 8 == 0:
                            pe.wait_ge(uw_ready, 2 * r + n // 8 + 1)
                        pe.matmul(ps_k[place(r, n)], flat(kbd, r, n), wide(uw, r, n), start=True, stop=True).then_inc(k_done, 1)
                for r in both:
                    pe.wait_ge(abd_ready, r + 1)
                    for n in range(N):
                        pe.matmul(ps_a[place(r, n)], flat(abd, r, n), wide(uw, r, n), start=True, stop=True).then_inc(a_done, 1)

            @block.scalar
            def _(act):
                for r in both:
                    for h in range(H):
                        act.activation(tbd[:, r, :, h, :], chunks(cols(tt, b + r)), ACT.Copy, scale=heads[:, h:h + 1]).then_inc(tbd_ready, 1)
                for r in both:
                    for g in range(2):
                        act.wait_ge(uw_done, N * r + 8 * (g + 1))
                        act.copy(uw[:, r, 8 * g:8 * g + 8, :, :], half(ps_uw, r, g)).then_inc(uw_ready, 1)
                for r in both:
                    act.wait_ge(q_turned, r + 1)
                    act.copy(cols(q, b + r), qpT[:]).then_inc(q_copied, 1)

            @block.gpsimd
            def _(pool):
                for r in both:
                    diagonal(pool, kbd[:, r], chunks(cols(k, b + r)), heads, N).then_inc(kbd_ready, 1)

            @block.vector
            def _(dve):
                for r in both:
                    dve.tensor_tensor(vk[:, r, :, 0, :], chunks(cols(v, b + r)), bcast(beta_of(r), C), ALU.mult).then_inc(vk_ready, 1)
                    dve.tensor_tensor(vk[:, r, :, 1, :], chunks(cols(k, b + r)), bcast(beta_of(r), C), ALU.mult).then_inc(vk_ready, 1)
                for r in both:
                    diagonal(dve, abd[:, r], chunks(cols(att, b + r)), heads, N).then_inc(abd_ready, 1)
                dve.drain()
                for r in both:
                    for g in range(2):
                        dve.wait_ge(k_done, N * r + 8 * (g + 1))
                        dve.tensor_copy(at(att, r, g), half(ps_k, r, g)[:, :, 0, :])
                        dve.tensor_copy(chunks(kw[:])[:, 8 * g:8 * g + 8, :], half(ps_k, r, g)[:, :, 1, :])
                    dve.drain()
                    dve.transpose(kwT[:], kw[:])
                    dve.drain()
                    dve.tensor_tensor(chunks(cols(tt, b + r)), each_chunk(tri[:, 2, :], N), chunks(kwT[:]), ALU.subtract)
                    dve.drain()
                for r in both:
                    for g in range(2):
                        dve.wait_ge(a_done, N * r + 8 * (g + 1))
                        dve.tensor_copy(at(k, r, g), half(ps_a, r, g)[:, :, 0, :])
                        dve.tensor_tensor(chunks(qp[:])[:, 8 * g:8 * g + 8, :], at(q, r, g), half(ps_a, r, g)[:, :, 1, :], ALU.subtract)
                    dve.drain()
                    at_least(dve, q_copied, r)
                    dve.transpose(qpT[:], qp[:]).then_inc(q_turned, 1)
                    dve.drain()

        with nc.Fori(0, NSEQ // 2) as i:
            with nc.Block() as block:
                section(block, 2 * i)
            clear(nc, ph.sems)


def delta_scan(nc, q, o, bs, ms, heads):
    H, C, N = L0_H, L0_C, L0_N
    with ExitStack() as ctx:
        ph = Phase(nc, ctx, "l0s")
        mbd, qbd = (ph.sb(n, [P, 2, NSEQ, H, C]) for n in ("mbd", "qbd"))
        s = ph.sb("s", [P, 2, NSEQ, C])
        ps_m, ps_o = ph.ps("psm", [P, 2, SEQ]), ph.ps("pso", [P, 2, SEQ])
        mbd_ready, qbd_ready, ms_done, o_done, s_ready, o_taken = (ph.sem(n) for n in (
            "mbd_ready", "qbd_ready", "ms_done", "o_done", "s_ready", "o_taken"))
        at = lambda x, n: x[:].rearrange("p (b n d) -> p b n d", n=N, d=C)[:, :, n, :]
        of_all = lambda ps, n: ps[:, n % 2, 0:NSEQ * C].rearrange("p (b d) -> p b d", d=C)
        flat = lambda x, n, b: x[:, n % 2, b, :, :].rearrange("p h c -> p (h c)")
        place = lambda ps, n, b: ps[:, n % 2, b * C:min(b + 4, NSEQ) * C]
        wide = lambda n, b: s[:, n % 2, b:min(b + 4, NSEQ), :].rearrange("p b d -> p (b d)")
        ctx.callback(clear, nc, ph.sems)
        block = ctx.enter_context(nc.Block())

        @block.gpsimd
        def _(pool):
            for n in range(N - 1):
                at_least(pool, ms_done, n - 1)
                diagonal(pool, mbd[:, n % 2], at(ms, n), heads, NSEQ).then_inc(mbd_ready, 1)

        @block.scalar
        def _(act):
            for n in range(N):
                at_least(act, o_done, n - 1)
                for h in range(H):
                    act.activation(qbd[:, n % 2, :, h, :], at(q, n), ACT.Copy, scale=heads[:, h:h + 1]).then_inc(qbd_ready, 1)

        @block.tensor
        def _(pe):
            for n in range(N):
                pe.wait_ge(s_ready, n + 1)
                if n < N - 1:
                    pe.wait_ge(mbd_ready, n + 1)
                    for b in range(NSEQ):
                        mm = pe.matmul(place(ps_m, n, b), flat(mbd, n, b), wide(n, b), start=True, stop=True)
                    mm.then_inc(ms_done, 1)
                pe.wait_ge(qbd_ready, H * (n + 1))
                at_least(pe, o_taken, n - 1)
                for b in range(NSEQ):
                    mm = pe.matmul(place(ps_o, n, b), flat(qbd, n, b), wide(n, b), start=True, stop=True)
                mm.then_inc(o_done, 1)

        @block.vector
        def _(dve):
            dve.memset(s[:, 0], 0.0).then_inc(s_ready, 1)
            for n in range(N):
                if n < N - 1:
                    dve.wait_ge(ms_done, n + 1)
                    at_least(dve, o_done, n)
                    dve.tensor_tensor(s[:, (n + 1) % 2], of_all(ps_m, n), at(bs, n), ALU.add).then_inc(s_ready, 1)
                dve.wait_ge(o_done, n + 1)
                dve.tensor_tensor(at(o, n), at(o, n), of_all(ps_o, n), ALU.add).then_inc(o_taken, 1)


def filters(nc, c, t, v, short, long):
    C, SHORT, LONG = L0_C, 5, 64
    PE_TAPS, POOL_TAPS = 22, 14
    HALF = NSEQ // 2
    pe_taps = range(PE_TAPS)
    pool_taps = range(PE_TAPS, PE_TAPS + POOL_TAPS)
    dve_taps = range(PE_TAPS + POOL_TAPS, LONG)
    with ExitStack() as ctx:
        ph = Phase(nc, ctx, "l0r")
        ws, wl = ph.sb("ws", [P, SHORT]), ph.sb("wl", [P, LONG])
        vF = ph.sb("vf", [P, NSEQ, LONG + SEQ])
        acc, pacc = (ph.sb(n, [P, NSEQ, SEQ]) for n in ("acc", "pacc"))
        ptmp = ph.sb("ptmp", [P, 2, HALF, SEQ])
        diag = ph.sb("diag", [P, PE_TAPS, P])
        ps = ph.ps("ps", [P, NSEQ, SEQ])
        loaded, v_ready, diag_ready, pe_done, product_ready, added, pool_done = (
            ph.sem(n) for n in ("loaded", "v_ready", "diag_ready", "pe_done", "product_ready", "added", "pool_done"))
        ctx.callback(clear, nc, ph.sems)
        block = ctx.enter_context(nc.Block())
        shifted = lambda s: vF[:, :, LONG - s:LONG - s + SEQ]
        wide = lambda x: x[:].rearrange("p b s -> p (b s)")

        @block.sync
        def _(sp):
            sp.dma_start(ws[:], t["L0_attn_fir_short_wp"]).then_inc(loaded, 16)
            sp.dma_start(wl[:], t["L0_attn_fir_long_wp"]).then_inc(loaded, 16)

        @block.scalar
        def _(act):
            act.wait_ge(loaded, 32)
            for j in pe_taps:
                act.activation(diag[:, j, :], c["ident"][:], ACT.Copy, scale=wl[:, j:j + 1]).then_inc(diag_ready, 1)
            act.wait_ge(v_ready, 1)
            for n, (j, g) in enumerate((j, g) for j in pool_taps for g in range(2)):
                half = slice(g * HALF, (g + 1) * HALF)
                if n < 2:
                    act.activation(pacc[:, half], shifted(LONG - 1 - j)[:, half], ACT.Copy, scale=wl[:, j:j + 1]).then_inc(product_ready, 1)
                    continue
                at_least(act, added, n - 3)
                act.activation(ptmp[:, n % 2], shifted(LONG - 1 - j)[:, half], ACT.Copy, scale=wl[:, j:j + 1]).then_inc(product_ready, 1)

        @block.tensor
        def _(pe):
            pe.wait_ge(v_ready, 1)
            for j in pe_taps:
                pe.wait_ge(diag_ready, j + 1)
                for b in range(NSEQ):
                    mm = pe.matmul(ps[:, b, :], diag[:, j, :], shifted(LONG - 1 - j)[:, b, :], start=(j == 0), stop=(j == PE_TAPS - 1))
            mm.then_inc(pe_done, 1)

        @block.gpsimd
        def _(pool):
            for n in range(2, 2 * POOL_TAPS):
                half = slice(n % 2 * HALF, (n % 2 + 1) * HALF)
                pool.wait_ge(product_ready, n + 1)
                pool.tensor_tensor(pacc[:, half], pacc[:, half], ptmp[:, n % 2], ALU.add)
                pool.drain().then_inc(added, 1)
            pool.sem_inc(pool_done, 1)

        @block.vector
        def _(dve):
            dve.memset(vF[:, :, 0:LONG], 0.0)
            for b in range(NSEQ):
                dve.transpose(vF[:, b, LONG:], cols(v, b))
            dve.drain().then_inc(v_ready, 1)
            dve.wait_ge(loaded, 32)

            def fir(w, taps, total):
                for n, j in enumerate(taps):
                    if n == 0:
                        dve.tensor_scalar(acc[:], shifted(total - 1 - j), w[:, j:j + 1], None, ALU.mult)
                    else:
                        dve.scalar_tensor_tensor(out=acc[:], in0=shifted(total - 1 - j), scalar=w[:, j:j + 1], in1=acc[:], op0=ALU.mult,
                                                 op1=ALU.add)
                    dve.drain()

            fir(ws, range(SHORT), SHORT)
            dve.transpose(short[:], wide(acc))
            dve.drain()
            fir(wl, dve_taps, LONG)
            dve.wait_ge(pool_done, 1)
            dve.tensor_tensor(acc[:], acc[:], pacc[:], ALU.add)
            dve.drain()
            dve.wait_ge(pe_done, 1)
            dve.tensor_tensor(acc[:], acc[:], ps[:], ALU.add)
            dve.drain()
            dve.transpose(long[:], wide(acc))


def gated_mix(nc, xT, xnT, t, branches):
    H, C, N = L0_H, L0_C, L0_N
    FLOOR = 0.05
    with ExitStack() as ctx:
        ph = Phase(nc, ctx, "l0g")
        w1a, w1b, w2, wo = ph.sb("w1a", [P, P]), ph.sb("w1b", [P, P]), ph.sb("w2", [P, C]), ph.sb("wo", [P, P])
        b1, b2, temp, onorm, eps = (ph.sb(n, [P, 1]) for n in ("b1", "b2", "temp", "onorm", "eps"))
        xc, sq, ab = (ph.sb(n, [P, 2, 4, SEQ]) for n in ("xc", "sq", "ab"))
        mean, sumc, sums, sumsq = (ph.sb(n, [P, 2, 4, N]) for n in ("mean", "sumc", "sums", "sumsq"))
        st, stF = ph.sb("st", [P, 2, N, C]), ph.sb("stf", [P, 2, SEQ])
        h1 = ph.sb("h1", [P, 2, SEQ])
        lg, lgK = ph.sb("lg", [P, 2, SEQ]), ph.sb("lgk", [P, N, C])
        pr = ph.sb("pr", [P, 2, N, 4])
        m, rms = ph.sb("m", [P, 2, N]), ph.sb("rms", [P, 2, N])
        mix, mix2 = ph.sb("mix", [P, 2, SEQ]), ph.sb("mix2", [P, SEQ])
        oF = ph.sb("of", [P, 2, SEQ])
        ps_h, ps_l, ps_y = (ph.ps(n, [P, 2, SEQ]) for n in ("psh", "psl", "psy"))
        (loaded, mean_ready, centered, absed, squared, sumsq_ready, st_ready, h_ready, h1_ready, l_done, lg_ready, exp_ready, pr_ready, mix_ready,
         mix_added, mix_squared, rms_ready, norm_ready, root_ready, turned, o_ready, y_ready) = (ph.sem(n) for n in (
             "loaded", "mean_ready", "centered", "absed", "squared", "sumsq_ready", "st_ready", "h_ready", "h1_ready", "l_done", "lg_ready",
             "exp_ready", "pr_ready", "mix_ready", "mix_added", "mix_squared", "rms_ready", "norm_ready", "root_ready", "turned", "o_ready", "y_ready"))
        with nc.Block() as block:
            @block.sync
            def _(sp):
                loads = ((w1a, "w1a"), (w1b, "w1b"), (w2, "w2p"), (wo, "Wo"), (b1, "b1"), (b2, "b2p"), (temp, "temp"), (onorm, "onorm"))
                for dst, name in loads:
                    sp.dma_start(dst[:], t[f"L0_attn_{name}"]).then_inc(loaded, 16)
                sp.wait_ge(loaded, 16 * len(loads))

            @block.scalar
            def _(act):
                act.wait_ge(loaded, 16 * 8)
                act.activation(temp[:], temp[:], ACT.Exp, scale=-1.0)

            @block.vector
            def _(dve):
                dve.memset(eps[:], EPS)
                dve.memset(st[:], 0.0)
        clear(nc, ph.sems)

        def section(block, b):
            stats = lambda r: st[:, r, :, 0:16].rearrange("p n (x s) -> p x s n", s=4)
            both = range(2)

            @block.tensor
            def _(pe):
                def gate(n):
                    r, h = divmod(n, H)
                    pe.wait_ge(h1_ready, n + 1)
                    pe.matmul(ps_l[h * C:(h + 1) * C, r, :], w2[:], h1[:, n % 2, :], start=True, stop=True).then_inc(l_done, 1)

                for n in range(2 * H):
                    r, h = divmod(n, H)
                    at_least(pe, h1_ready, n - 1)
                    pe.matmul(ps_h[:, n % 2, :], w1a[:], cols(xnT, b + r), start=True, stop=False)
                    pe.wait_ge(st_ready, r + 1)
                    pe.matmul(ps_h[:, n % 2, :], w1b[h * C:(h + 1) * C, :], stF[h * C:(h + 1) * C, r, :], start=False, stop=True,
                              tile_position=(h * C, 0)).then_inc(h_ready, 1)
                    if n:
                        gate(n - 1)
                gate(2 * H - 1)
                for r in both:
                    pe.wait_ge(o_ready, r + 1)
                    pe.matmul(ps_y[:, r, :], wo[:], oF[:, r, :], start=True, stop=True).then_inc(y_ready, 1)

            @block.scalar
            def _(act):
                def absolutes(r):
                    for n, x in enumerate(branches):
                        act.activation(ab[:, r, n, :], cols(x, b + r), ACT.Abs).then_inc(absed, 1)

                absolutes(0)
                for r in both:
                    for n in range(4):
                        act.wait_ge(centered, 4 * r + n + 1)
                        act.activation(sq[:, r, n, :], xc[:, r, n, :], ACT.Square).then_inc(squared, 1)
                    if r == 0:
                        absolutes(1)
                    act.wait_ge(sumsq_ready, r + 1)
                    act.activation(stats(r)[:, :, 3, :], sumsq[:, r], ACT.Sqrt).then_inc(norm_ready, 1)
                for n in range(2 * H):
                    act.wait_ge(h_ready, n + 1)
                    at_least(act, l_done, n - 1)
                    act.activation(h1[:, n % 2, :], ps_h[:, n % 2, :], ACT.Gelu, bias=b1[:]).then_inc(h1_ready, 1)
                for r in both:
                    act.wait_ge(lg_ready, r + 1)
                    act.activation(pr[:, r], pr[:, r], ACT.Exp).then_inc(exp_ready, 1)
                for r in both:
                    act.wait_ge(mix_ready, r + 1)
                    act.activation(sq[:, r, 0, :], mix[:, r, :], ACT.Square).then_inc(mix_squared, 1)
                for r in both:
                    act.wait_ge(rms_ready, r + 1)
                    act.activation(rms[:, r], m[:, r], ACT.Sqrt, scale=1.0 / C, bias=eps[:]).then_inc(root_ready, 1)
                for r in both:
                    act.wait_ge(turned, r + 1)
                    act.activation(oF[:, r, :], lg[:, r, :], ACT.Copy, scale=onorm[:]).then_inc(o_ready, 1)

            @block.gpsimd
            def _(pool):
                for r in both:
                    for n, x in enumerate(branches):
                        pool.wait_ge(mean_ready, 4 * r + n + 1)
                        pool.tensor_tensor(chunks(xc[:, r, n, :]), chunks(cols(x, b + r)), bcast(mean[:, r, n, :], C),
                                           ALU.subtract).then_inc(centered, 1)
                for r in both:
                    pool.wait_ge(pr_ready, r + 1)
                    pool.wait_ge(squared, 4 * (r + 1))
                    for n in (2, 3):
                        pool.tensor_tensor(chunks(xc[:, r, n, :]), chunks(cols(branches[n], b + r)), bcast(pr[:, r, :, n], C), ALU.mult)
                    pool.drain().then_inc(mix_added, 1)

            @block.vector
            def _(dve):
                for r in both:
                    for n, x in enumerate(branches):
                        dve.tensor_reduce(sums[:, r, n, :], chunks(cols(x, b + r)), AX.X, ALU.add)
                        dve.drain()
                        dve.tensor_scalar(mean[:, r, n, :], sums[:, r, n, :], 1.0 / C, None, ALU.mult).then_inc(mean_ready, 1)
                dve.drain()
                for r in both:
                    dve.tensor_copy(stats(r)[:, :, 0, :], mean[:, r])
                    for n in range(4):
                        dve.wait_ge(absed, 4 * r + n + 1)
                        dve.tensor_reduce(sums[:, r, n, :], chunks(ab[:, r, n, :]), AX.X, ALU.add)
                    dve.drain()
                    dve.tensor_scalar(stats(r)[:, :, 2, :], sums[:, r], 1.0 / C, None, ALU.mult)
                    for n in range(4):
                        dve.wait_ge(squared, 4 * r + n + 1)
                        dve.tensor_reduce(sumc[:, r, n, :], chunks(sq[:, r, n, :]), AX.X, ALU.add)
                    dve.drain()
                    dve.tensor_scalar(stats(r)[:, :, 1, :], sumc[:, r], 1.0 / C, None, ALU.mult)
                    dve.tensor_tensor(sumsq[:, r], mean[:, r], mean[:, r], ALU.mult)
                    dve.drain()
                    dve.scalar_tensor_tensor(out=sumsq[:, r], in0=sumsq[:, r], scalar=float(C), in1=sumc[:, r], op0=ALU.mult,
                                             op1=ALU.add).then_inc(sumsq_ready, 1)
                    dve.wait_ge(norm_ready, r + 1)
                    dve.drain()
                    dve.transpose(stF[:, r, :], st[:, r].rearrange("p n c -> p (n c)")).then_inc(st_ready, 1)
                for r in both:
                    dve.wait_ge(l_done, H * (r + 1))
                    dve.tensor_scalar(lg[:, r, :], ps_l[:, r, :], b2[:], temp[:], ALU.add, ALU.mult)
                    dve.drain()
                    dve.transpose(lgK[:].rearrange("p n c -> p (n c)"), lg[:, r, :])
                    dve.drain()
                    dve.tensor_reduce(m[:, r], lgK[:, :, 0:4], AX.X, ALU.max)
                    dve.drain()
                    dve.tensor_tensor(pr[:, r], lgK[:, :, 0:4], bcast(m[:, r], 4), ALU.subtract).then_inc(lg_ready, 1)
                    dve.wait_ge(exp_ready, r + 1)
                    dve.tensor_reduce(m[:, r], pr[:, r], AX.X, ALU.add)
                    dve.drain()
                    dve.reciprocal(m[:, r], m[:, r])
                    dve.drain()
                    dve.tensor_tensor(pr[:, r], pr[:, r], bcast(m[:, r], 4), ALU.mult)
                    dve.drain()
                    dve.tensor_scalar(pr[:, r], pr[:, r], 1.0 - 4 * FLOOR, FLOOR, ALU.mult, ALU.add)
                    dve.drain().then_inc(pr_ready, 1)
                    dve.tensor_tensor(chunks(mix[:, r, :]), chunks(cols(branches[0], b + r)), bcast(pr[:, r, :, 0], C), ALU.mult)
                    dve.tensor_tensor(chunks(mix2[:]), chunks(cols(branches[1], b + r)), bcast(pr[:, r, :, 1], C), ALU.mult)
                    dve.drain()
                    dve.tensor_tensor(mix[:, r, :], mix[:, r, :], mix2[:], ALU.add)
                    dve.drain()
                for r in both:
                    dve.wait_ge(mix_added, r + 1)
                    for n in (2, 3):
                        tt = dve.tensor_tensor(mix[:, r, :], mix[:, r, :], xc[:, r, n, :], ALU.add)
                        if n == 2:
                            dve.drain()
                    tt.then_inc(mix_ready, 1)
                for r in both:
                    dve.wait_ge(mix_squared, r + 1)
                    dve.tensor_reduce(m[:, r], chunks(sq[:, r, 0, :]), AX.X, ALU.add).then_inc(rms_ready, 1)
                for r in both:
                    dve.wait_ge(root_ready, r + 1)
                    dve.reciprocal(rms[:, r], rms[:, r])
                    dve.drain()
                    dve.tensor_tensor(chunks(mix[:, r, :]), chunks(mix[:, r, :]), bcast(rms[:, r], C), ALU.mult)
                    dve.drain()
                    dve.transpose(lg[:, r, :], mix[:, r, :]).then_inc(turned, 1)
                for r in both:
                    dve.wait_ge(y_ready, r + 1)
                    dve.tensor_tensor(cols(xT, b + r), cols(xT, b + r), ps_y[:, r, :], ALU.add)

        with nc.Fori(0, NSEQ // 2) as i:
            with nc.Block() as block:
                section(block, 2 * i)
            clear(nc, ph.sems)


def l0_ffn(nc, xT, xnT, c, t):
    normalize(nc, xT, xnT, c, "l0fn", EPS)
    with ExitStack() as ctx:
        ph = Phase(nc, ctx, "l0f")
        wr, wi, cs, sn, csd, snd, snn = (ph.sb(n, [P, P]) for n in ("wr", "wi", "cs", "sn", "csd", "snd", "snn"))
        bias = ph.sb("bias", [P, 1])
        gt, ht, m = (ph.sb(n, [P, P]) for n in ("gt", "ht", "m"))
        ps_m = ph.ps("psm", [P, 2, P])
        ps_y = ph.ps("psy", [P, 2, SEQ])
        loaded, gh_ready, gh_copied, m_ready, m_copied, y_ready, x_done = (
            ph.sem(n) for n in ("loaded", "gh_ready", "gh_copied", "m_ready", "m_copied", "y_ready", "x_done"))
        ctx.callback(clear, nc, ph.sems)
        block = ctx.enter_context(nc.Block())

        @block.sync
        def _(sp):
            for dst, src in ((wr, t["L0_ffn_w_freq_real"]), (wi, t["L0_ffn_w_freq_imag"]), (cs, t["dft"][0]),
                             (sn, t["dft"][1]), (csd, t["dft"][2]), (snd, t["dft"][3]), (snn, t["dft"][4]),
                             (bias, t["L0_ffn_bias"].unsqueeze(1))):
                sp.dma_start(dst[:], src).then_inc(loaded, 16)

        @block.tensor
        def _(pe):
            pe.wait_ge(loaded, 16 * 8)
            pe.matmul(ps_m[:, 0, :], wr[:], cs[:], start=True, stop=False)
            pe.matmul(ps_m[:, 0, :], wi[:], sn[:], start=False, stop=True)
            pe.matmul(ps_m[:, 1, :], wi[:], cs[:], start=True, stop=False)
            pe.matmul(ps_m[:, 1, :], wr[:], snn[:], start=False, stop=True).then_inc(gh_ready, 1)
            pe.wait_ge(gh_copied, 2)
            pe.matmul(ps_m[:, 0, :], gt[:], csd[:], start=True, stop=False)
            pe.matmul(ps_m[:, 0, :], ht[:], snd[:], start=False, stop=True).then_inc(m_ready, 1)
            pe.wait_ge(m_copied, 1)
            with pe.Fori(0, NSEQ // 2) as i:
                pe.wait_ge(x_done, 2 * i + 1)
                for j in range(2):
                    pe.matmul(ps_y[:, j, :], m[:], cols(xnT, 2 * i + j), start=True, stop=True).then_inc(y_ready, 1)

        @block.scalar
        def _(act):
            act.wait_ge(gh_ready, 1)
            act.copy(gt[:], ps_m[:, 0, :]).then_inc(gh_copied, 1)
            act.copy(ht[:], ps_m[:, 1, :]).then_inc(gh_copied, 1)
            act.wait_ge(m_ready, 1)
            act.copy(m[:], ps_m[:, 0, :]).then_inc(m_copied, 1)

        @block.vector
        def _(dve):
            dve.sem_inc(x_done, 1)
            dve.wait_ge(loaded, 16 * 8)
            with dve.Fori(0, NSEQ // 2) as i:
                for j in range(2):
                    dve.wait_ge(y_ready, 2 * i + j + 1)
                    dve.scalar_tensor_tensor(out=cols(xT, 2 * i + j), in0=ps_y[:, j, :], scalar=bias[:], in1=cols(xT, 2 * i + j),
                                             op0=ALU.add, op1=ALU.add).then_inc(x_done, 1)


def attention(nc, xT, xnT, c, t, name, wq, wk, wv, wo, causal, rope):
    normalize(nc, xT, xnT, c, name + "n", EPS)
    H, D, PARTS = 16, 8, 3
    QPART = (0, 1, 0, 2, 0, 1)
    KPART = (0, 0, 1, 0, 2, 1)
    ROWS = 96
    MAXROWS = 2
    SCALE = float(D) ** -0.5
    projections = ["q", "qs", "k", "ks", "v"] if rope else ["q", "k", "v"]
    NPROJ = len(projections)
    V_AT, FIN_FROM, A_FROM, A_TO, PROJECT_FROM = 1, 2, 2, 15, 7
    a_upto = lambda h, kt: ((h - A_FROM) * TPS + kt) * H // (A_TO - A_FROM)
    width = lambda n: (TPS - n) * P if causal else SEQ
    kts = lambda qt: range(qt + 1) if causal else range(TPS)
    with ExitStack() as ctx:
        ph = Phase(nc, ctx, name)
        w = {n: ph.sb("w" + n, [P, P]) for n in projections}
        wo_sb = ph.sb("wo", [P, P])
        if rope:
            cos, sin = ph.sb("cos", [P, SEQ]), ph.sb("sin", [P, SEQ])
        identb = ph.sb("identb", [P, P], BF16)
        maskq, maskk = ph.sb("maskq", [P, P]), ph.sb("maskk", [P, P])
        maskqb, maskkb = ph.sb("maskqb", [P, P], BF16), ph.sb("maskkb", [P, P], BF16)
        full = ph.sb("full", [P, 2, SEQ])
        rot = ph.sb("rot", [P, SEQ])
        parts = ph.sb("parts", [P, 2 * PARTS, SEQ], BF16)
        xb = ph.sb("xb", [P, SEQ])
        qst, kst = (ph.sb(n, [ROWS + MAXROWS, 2, H, SEQ], BF16) for n in ("qst", "kst"))
        v = ph.sb("v", [P, 2, TPS, H // 2, 2, 4, D])
        pt = ph.sb("pt", [P, 2, TPS, SEQ])
        mx = ph.sb("mx", [P, TPS, H])
        negmax = ph.sb("negmax", [H, SEQ])
        nm = ph.sb("nm", [H, MAXROWS, SEQ], BF16)
        rsum = ph.sb("rsum", [P, TPS, H])
        sums = ph.sb("sums", [P, 2, SEQ])
        o = ph.sb("o", [P, TPS, H, D])
        oT = ph.sb("oT", [P, SEQ])
        scratch = nc.dram_tensor(f"{name}_scratch", (2, P, 2 * PARTS, SEQ), BF16, kind="Internal").ap()
        max_scratch = nc.dram_tensor(f"{name}_max_scratch", (2, H, MAXROWS, SEQ), BF16, kind="Internal").ap()
        max_stored = ph.sem("max_stored")
        ps_m = ph.ps("psm", [P, SEQ])
        ps_a = ph.ps("psa", [P, 2, SEQ])
        ps_s = ph.ps("pss", [P, 2, SEQ])
        ps_o = ph.ps("pso", [P, 2, SEQ])
        (loaded, filled, emptied, xb_ready, full_ready, full_taken, v_ready, parts_ready, parts_stored, stacked, a_ready, a_taken,
         maxed, nm_ready, max_stacked, s_ready, exped, pv_done, o_ready, sums_ready) = (
            ph.sem(n) for n in ("loaded", "filled", "emptied", "xb_ready", "full_ready", "full_taken", "v_ready", "parts_ready",
                                "parts_stored", "stacked", "a_ready", "a_taken", "maxed", "nm_ready", "max_stacked",
                                "s_ready", "exped", "pv_done", "o_ready", "sums_ready"))
        NLOAD = NPROJ + 1 + 2 + (2 if rope else 0)


        with nc.Block() as block:
            @block.sync
            def _(sp):
                src = {"q": wq, "k": wk, "v": wv}
                if rope:
                    src.update(qs=t["L3_attn_w_swapped"][:, 0, :], ks=t["L3_attn_w_swapped"][:, 1, :])
                    sp.dma_start(cos[:], t["rope8"][0]).then_inc(loaded, 16)
                    sp.dma_start(sin[:], t["rope8"][1]).then_inc(loaded, 16)
                for n in projections:
                    sp.dma_start(w[n][:], src[n]).then_inc(loaded, 16)
                sp.dma_start(wo_sb[:], wo).then_inc(loaded, 16)
                sp.dma_start(maskq[:], t["causal"][0]).then_inc(loaded, 16)
                sp.dma_start(maskk[:], t["causal"][1]).then_inc(loaded, 16)
                sp.wait_ge(loaded, 16 * NLOAD)

            @block.scalar
            def _(act):
                act.wait_ge(loaded, 16 * NLOAD)
                act.copy(identb[:], c["ident"][:])
                act.copy(maskqb[:], maskq[:])
                act.copy(maskkb[:], maskk[:])
                act.copy(kst[ROWS:, 1, :, :].rearrange("p h (k q) -> p (h k) q", q=P), c["ones"][ROWS:ROWS + MAXROWS, :].unsqueeze(1).to_broadcast([MAXROWS, H * TPS, P]))

            @block.vector
            def _(dve):
                dve.memset(v[:], 0.0)
                dve.drain()
                for e in range(2):
                    dve.memset(v[:, :, :, :, e, 2 * e + 1, :], 1.0)
                dve.memset(qst[0:ROWS, :, :, :].bitcast(F32), 0.0)

            @block.gpsimd
            def _(pool):
                pool.memset(kst[0:ROWS, :, :, :].bitcast(F32), 0.0)
                pool.memset(kst[ROWS:, 0, :, :], 1.0)

        def section(block, b, prep, nsteps, last):
            preps = 1 if prep else nsteps - (1 if last else 0)
            projs = 2 if prep else 0 if last else nsteps
            proj_seq = lambda p: b + p if prep else b + p + 2
            prep_seq = lambda p: b + p if prep else b + p + 1
            prep_buf = lambda p: p % 2 if prep else (p + 1) % 2
            side = {}
            for r in range(max(nsteps, 1)):
                if r < preps:
                    side.setdefault((r, V_AT), []).append(("value", r, 0))
                for p in range(projs) if prep else [r] if r < projs else []:
                    for n in range(NPROJ - 1):
                        side.setdefault((r, 2 + p * (NPROJ - 1) + n if prep else PROJECT_FROM + n), []).append(("project", p, n))
                if r > 0:
                    for n, kind in enumerate(("unturn0", "unturn1", "turn", "output")):
                        side.setdefault((r, FIN_FROM + n), []).append((kind, r - 1, 0))
                if r < preps:
                    side.setdefault((r, H if prep else A_TO), []).append(("maxima", r, 0))
            if nsteps:
                side.setdefault((nsteps - 1, H), []).extend((kind, nsteps - 1, 0) for kind in ("unturn0", "unturn1", "turn", "output"))
            order = [x for at in sorted(side) for x in side[at]]
            fill = {x: n for n, x in enumerate(order)}
            @block.tensor
            def _(pe):
                def project(p, s):
                    at_least(pe, emptied, fill["project", p, s])
                    pe.matmul(ps_m[:], w[projections[s]][:], cols(xnT, proj_seq(p)), start=True, stop=True).then_inc(filled, 1)

                def value(p):
                    at_least(pe, emptied, fill["value", p, 0])
                    pe.wait_ge(xb_ready, p + 1)
                    for k in range(TPS):
                        mm = pe.matmul(ps_m[:, k * P:(k + 1) * P], xb[:, k * P:(k + 1) * P], w["v"][:], start=True, stop=True)
                    mm.then_inc(filled, 1)

                def maxima(p, h, qt):
                    j = prep_buf(p)
                    if h == 0 and qt == 0:
                        pe.wait_ge(stacked, 16 * 2 * len(QPART) * (p + 1))
                    at_least(pe, a_taken, (p * H + h) * TPS + qt - 1)
                    wd = (qt + 1) * P if causal else SEQ
                    mm = pe.matmul(ps_a[:, qt % 2, 0:wd], qst[0:ROWS, j, h, qt * P:(qt + 1) * P], kst[0:ROWS, j, h, 0:wd],
                                   start=True, stop=not causal)
                    if causal:
                        mm = pe.matmul(ps_a[:, qt % 2, qt * P:wd], identb[:], maskqb[:], start=False, stop=True)
                    mm.then_inc(a_ready, 1)

                def turn_maxima(p):
                    at_least(pe, emptied, fill["maxima", p, 0])
                    pe.wait_ge(maxed, p + 1)
                    for qt in range(TPS):
                        mm = pe.transpose(ps_m[0:H, qt * P:(qt + 1) * P], mx[:, qt, :], c["ident"][:])
                    mm.then_inc(filled, 1)

                def scores(r, h, kt):
                    if h == 0 and kt == 0:
                        at_least(pe, max_stacked, 16 * r)
                    j, bank = r % 2, kt % 2
                    at_least(pe, exped, (r * H + h) * TPS + kt - 1)
                    q0 = kt * P if causal else 0
                    mm = pe.matmul(ps_s[:, bank, q0:SEQ], kst[0:ROWS + MAXROWS, j, h, kt * P:(kt + 1) * P],
                                   qst[0:ROWS + MAXROWS, j, h, q0:SEQ], start=True, stop=not causal)
                    if causal:
                        mm = pe.matmul(ps_s[:, bank, q0:q0 + P], identb[:], maskkb[:], start=False, stop=True)
                    mm.then_inc(s_ready, 1)

                def weigh(r, h, kt):
                    if h == 0 and kt == 0:
                        at_least(pe, v_ready, r)
                        at_least(pe, sums_ready, r)
                    if kt == 0:
                        pe.wait_ge(exped, (r * H + h + 1) * TPS)
                    q0 = kt * P if causal else 0
                    g = h // 2 % 4
                    mm = pe.matmul(ps_o[32 * g:32 * (g + 1), h // 8, q0:SEQ],
                                   v[:, r % 2, kt, h // 2, h % 2, :, :].rearrange("p a d -> p (a d)"),
                                   pt[:, h % 2, kt, q0:SEQ], start=(h % 2 == 0 and kt == 0), stop=(h % 2 == 1 and kt == TPS - 1),
                                   tile_position=(0, 32 * g))
                    if kt == TPS - 1:
                        mm.then_inc(pv_done, 1)

                def unturn(r, half):
                    at_least(pe, emptied, fill[f"unturn{half}", r, 0])
                    pe.wait_ge(sums_ready, r + 1)
                    for k in range(TPS):
                        mm = pe.transpose(ps_m[:, k * P:(k + 1) * P], sums[:, half, k * P:(k + 1) * P], c["ident"][:])
                    mm.then_inc(filled, 1)

                def turn(r):
                    at_least(pe, emptied, fill["turn", r, 0])
                    pe.wait_ge(o_ready, 2 * r + 2)
                    for k in range(TPS):
                        mm = pe.transpose(ps_m[:, k * P:(k + 1) * P], o[:, k, :, :].rearrange("p h d -> p (h d)"), c["ident"][:])
                    mm.then_inc(filled, 1)

                def output(r):
                    pe.wait_ge(emptied, fill["output", r, 0])
                    pe.matmul(ps_m[:], wo_sb[:], oT[:], start=True, stop=True).then_inc(filled, 1)

                def beside(r, h):
                    for kind, n, m in side.get((r, h), []):
                        {"project": lambda: project(n, m), "value": lambda: value(n), "maxima": lambda: turn_maxima(n), "unturn0": lambda: unturn(n, 0),
                         "unturn1": lambda: unturn(n, 1), "turn": lambda: turn(n), "output": lambda: output(n)}[kind]()

                if prep:
                    for h in range(H):
                        beside(0, h)
                    for h in range(H):
                        for qt in range(TPS):
                            maxima(0, h, qt)
                    beside(0, H)
                for r in range(nsteps):
                    tiles = [(h, qt) for h in range(H) for qt in range(TPS)] if r < preps else []
                    for h in range(H):
                        beside(r, h)
                        for kt in range(TPS):
                            scores(r, h, kt)
                            if A_FROM <= h < A_TO:
                                for a in tiles[a_upto(h, kt):a_upto(h, kt + 1)]:
                                    maxima(r, *a)
                            if h >= 1:
                                weigh(r, h - 1, kt)
                    for kt in range(TPS):
                        weigh(r, H - 1, kt)
                    beside(r, H)

            @block.scalar
            def _(act):
                def take_v(p):
                    act.wait_ge(filled, fill["value", p, 0] + 1)
                    at_least(act, pv_done, p * H)
                    ps = ps_m[:].rearrange("p (k i e d) -> p k i e d", k=TPS, e=2, d=D)
                    for e in range(2):
                        act.copy(v[:, prep_buf(p), :, :, e, 2 * e, :], ps[:, :, :, e, :])
                    act.drain().then_inc(v_ready, 1)
                    act.sem_inc(emptied, 1)

                def exps(r, h):
                    for kt in range(TPS):
                        act.wait_ge(s_ready, (r * H + h) * TPS + kt + 1)
                        if kt == 0:
                            at_least(act, pv_done, r * H + h - 1)
                        q0 = kt * P if causal else 0
                        act.activation(pt[:, h % 2, kt, q0:SEQ], ps_s[:, kt % 2, q0:SEQ], ACT.Exp, scale=SCALE).then_inc(exped, 1)

                def beside(r, h):
                    for kind, n, m in side.get((r, h), []):
                        if kind == "value":
                            take_v(n)
                        if kind == "turn":
                            act.wait_ge(filled, fill[kind, n, 0] + 1)
                            act.copy(oT[:], ps_m[:]).then_inc(emptied, 1)

                if prep:
                    take_v(0)
                for r in range(nsteps):
                    for h in range(H):
                        exps(r, h)
                        beside(r, h)
                    act.wait_ge(pv_done, (r + 1) * H)
                    if r > 0:
                        act.wait_ge(filled, fill["unturn1", r - 1, 0] + 1)
                    act.copy(sums[:], ps_o[:]).then_inc(sums_ready, 1)
                    beside(r, H)

            @block.vector
            def _(dve):
                def take(p, s):
                    which = 0 if projections[s][0] == "q" else 1
                    dve.wait_ge(filled, fill["project", p, s] + 1)
                    if not rope:
                        at_least(dve, full_taken, 2 * p - 1 + which)
                        dve.tensor_copy(full[:, which, :], ps_m[:]).then_inc(full_ready, 1)
                        dve.drain().then_inc(emptied, 1)
                    elif len(projections[s]) == 1:
                        at_least(dve, full_taken, 2 * p - 1 + which)
                        dve.tensor_tensor(full[:, which, :], ps_m[:], cos[:], ALU.mult).then_inc(emptied, 1)
                    else:
                        dve.tensor_tensor(rot[:], ps_m[:], sin[:], ALU.mult).then_inc(emptied, 1)
                        dve.drain()
                        dve.tensor_tensor(full[:, which, :], full[:, which, :], rot[:], ALU.add).then_inc(full_ready, 1)
                        dve.drain()

                def maxima(p, tiles):
                    for h, qt in tiles:
                        dve.wait_ge(a_ready, (p * H + h) * TPS + qt + 1)
                        wd = (qt + 1) * P if causal else SEQ
                        dve.tensor_reduce(mx[:, qt, h:h + 1], ps_a[:, qt % 2, 0:wd], AX.X, ALU.max).then_inc(a_taken, 1)

                def take_maxima(p):
                    dve.wait_ge(filled, fill["maxima", p, 0] + 1)
                    at_least(dve, max_stored, 16 * p)
                    dve.tensor_scalar(negmax[:], ps_m[0:H, :], -1.0, None, ALU.mult).then_inc(emptied, 1)
                    dve.drain()
                    dve.tensor_copy(nm[:, 0, :], negmax[:])
                    dve.drain()
                    dve.tensor_tensor(nm[:, 1, :], negmax[:], nm[:, 0, :], ALU.subtract).then_inc(nm_ready, 1)
                    dve.drain()

                def normalize_heads(r, half):
                    dve.wait_ge(filled, fill[f"unturn{half}", r, 0] + 1)
                    if half == 0 and r > 0:
                        dve.wait_ge(filled, fill["turn", r - 1, 0] + 1)
                    ps = ps_m[:].rearrange("p (k h a d) -> p k h a d", k=TPS, a=2, d=D)
                    rs = rsum[:, :, half * H // 2:(half + 1) * H // 2]
                    for qt in range(TPS):
                        dve.reciprocal(rs[:, qt, :].unsqueeze(2), ps[:, qt, :, 1, 0:1])
                    dve.drain()
                    for qt in range(TPS):
                        dve.tensor_tensor(o[:, qt, half * H // 2:(half + 1) * H // 2, :], ps[:, qt, :, 0, :], bcast(rs[:, qt, :], D), ALU.mult)
                    dve.drain().then_inc(o_ready, 1)
                    dve.sem_inc(emptied, 1)

                def beside(r, h):
                    for kind, n, m in side.get((r, h), []):
                        if kind == "project":
                            take(n, m)
                        if kind == "maxima":
                            dve.drain().then_inc(maxed, 1)
                            take_maxima(n)
                        if kind in ("unturn0", "unturn1"):
                            normalize_heads(n, int(kind[-1]))
                        if kind == "output":
                            dve.wait_ge(filled, fill[kind, n, 0] + 1)
                            dve.tensor_tensor(cols(xT, b + n), cols(xT, b + n), ps_m[:], ALU.add).then_inc(emptied, 1)

                tiles = [(h, qt) for h in range(H) for qt in range(TPS)]
                if prep:
                    for h in range(H):
                        beside(0, h)
                    maxima(0, tiles)
                    beside(0, H)
                for r in range(nsteps):
                    for h in range(H):
                        beside(r, h)
                        if A_FROM <= h < A_TO and r < preps:
                            maxima(r, tiles[a_upto(h, 0):a_upto(h + 1, 0)])
                    beside(r, H)

            @block.gpsimd
            def _(pool):
                for p in range(max(preps, projs)):
                    if p < preps:
                        at_least(pool, v_ready, p)
                        pool.tensor_copy(xb[:], cols(xnT, prep_seq(p))).then_inc(xb_ready, 1)
                    for which in range(2) if p < projs else ():
                        pool.wait_ge(full_ready, 2 * p + which + 1)
                        if which == 0:
                            at_least(pool, parts_stored, 16 * p)
                        left, part = full[:, which, :], parts[:, which * PARTS:(which + 1) * PARTS, :]
                        pool.tensor_copy(part[:, 0, :], left)
                        pool.drain()
                        pool.tensor_tensor(left, left, part[:, 0, :], ALU.subtract)
                        pool.drain()
                        pool.tensor_copy(part[:, 1, :], left)
                        pool.drain()
                        pool.tensor_tensor(part[:, 2, :], left, part[:, 1, :], ALU.subtract).then_inc(parts_ready, 1)
                        pool.drain().then_inc(full_taken, 1)

            @block.sync
            def _(sp):
                def store_parts(p):
                    sp.wait_ge(parts_ready, 2 * p + 2)
                    sp.dma_start(scratch[p % 2], parts[:]).then_inc(parts_stored, 16)
                    sp.wait_ge(parts_stored, 16 * (p + 1))

                if prep:
                    store_parts(0)
                for p in range(max(preps, projs if not prep else 0)):
                    j = prep_buf(p)
                    if p < preps:
                        at_least(sp, pv_done, p * H)
                        for m in range(len(QPART)):
                            for dst, part in ((qst, QPART[m]), (kst, PARTS + KPART[m])):
                                sp.dma_start(dst[D * m:D * (m + 1), j, :, :],
                                             scratch[j, :, part, :].rearrange("(h d) t -> d h t", d=D)).then_inc(stacked, 16)
                        sp.wait_ge(stacked, 16 * 2 * len(QPART) * (p + 1))
                    if prep:
                        store_parts(1)
                    elif p < projs:
                        store_parts(p)
                    if p < preps:
                        sp.wait_ge(nm_ready, p + 1)
                        sp.dma_start(max_scratch[j], nm[:]).then_inc(max_stored, 16)
                        sp.wait_ge(max_stored, 16 * (p + 1))
                        sp.dma_start(qst[ROWS:ROWS + MAXROWS, j, :, :], max_scratch[j].rearrange("h m t -> m h t")).then_inc(max_stacked, 16)
                        sp.wait_ge(max_stacked, 16 * (p + 1))

        with nc.Block() as block:
            section(block, 0, True, 0, False)
        clear(nc, ph.sems)
        with nc.Fori(0, NSEQ // 2 - 1) as i:
            with nc.Block() as block:
                section(block, 2 * i, False, 2, False)
            clear(nc, ph.sems)
        with nc.Block() as block:
            section(block, NSEQ - 2, False, 2, True)
        clear(nc, ph.sems)


def l1_attn(nc, xT, xnT, c, t):
    attention(nc, xT, xnT, c, t, "l1a", t["L1_attn_WqT"], t["L1_attn_WkT"], t["L1_attn_WvT"], t["L1_attn_WoT"], causal=True, rope=False)


def l3_attn(nc, xT, xnT, c, t):
    w = t["L3_attn_w_qkv"]
    attention(nc, xT, xnT, c, t, "l3a", w[:, 0:P], w[:, P:2 * P], w[:, 2 * P:3 * P], t["L3_attn_w_proj"], causal=False, rope=True)


def l2_attn(nc, xT, xnT, c, t):
    normalize(nc, xT, xnT, c, "l2an", EPS)
    H, D = 16, 8
    NUM = P + H
    EPS_NORM, EPS_DEN = 1e-6, 1e-6
    with ExitStack() as ctx:
        ph = Phase(nc, ctx, "l2a")
        w = ph.sb("w", [P, 3 * P])
        wo, blocks = ph.sb("wo", [P, P]), ph.sb("blocks", [P, NUM])
        nw = ph.sb("nw", [P, 2, P])
        bout = ph.sb("bout", [P, 1])
        xb = ph.sb("xb", [P, 2, SEQ])
        sq = ph.sb("sq", [P, TPS, 2 * P])
        sqsum, var, std, rstd = (ph.sb(n, [P, TPS, 2]) for n in ("sqsum", "var", "std", "rstd"))
        scaled = ph.sb("scaled", [P, TPS, 2, P])
        qk = ph.sb("qk", [P, TPS, 2 * P])
        vo = ph.sb("vo", [P, TPS, P + 1])
        kv = ph.sb("kv", [P, NUM])
        qT = ph.sb("qT", [P, SEQ])
        den = ph.sb("den", [P, TPS, H])
        o = ph.sb("o", [P, TPS, P])
        oT = ph.sb("oT", [P, SEQ])
        ps_qkv = ph.ps("psqkv", [P, TPS, SEQ])
        ps_kv = ph.ps("pskv", [P, SEQ])
        ps_m = ph.ps("psm", [P, SEQ])
        ps_n = ph.ps("psn", [P, 2, SEQ])
        num = lambda k: ps_n[:, k // 2, (k % 2) * NUM:(k % 2 + 1) * NUM]
        (loaded, xb_ready, qkv_ready, squared, var_ready, std_ready, scaled_ready, qk_ready, vo_ready, kv_ready, kv_taken, qT_ready,
         qT_taken, num_ready, o_ready, oT_ready, oT_taken, y_ready, y_taken) = (
            ph.sem(n) for n in ("loaded", "xb_ready", "qkv_ready", "squared", "var_ready", "std_ready", "scaled_ready", "qk_ready",
                                "vo_ready", "kv_ready", "kv_taken", "qT_ready", "qT_taken", "num_ready", "o_ready", "oT_ready",
                                "oT_taken", "y_ready", "y_taken"))
        with nc.Block() as block:
            @block.sync
            def _(sp):
                for dst, src in ((w[:], t["L2_attn_W_qkv"]), (wo[:], t["L2_attn_W_out"]), (blocks[:], t["blocks8"]),
                                 (nw[:, 0, :], t["L2_attn_qn_w"].unsqueeze(0).to_broadcast([P, P])),
                                 (nw[:, 1, :], t["L2_attn_kn_w"].unsqueeze(0).to_broadcast([P, P])),
                                 (bout[:], t["L2_attn_b_out"].unsqueeze(1))):
                    sp.dma_start(dst, src).then_inc(loaded, 16)
                sp.wait_ge(loaded, 16 * 6)

            @block.vector
            def _(dve):
                dve.memset(vo[:], 1.0)
        clear(nc, ph.sems)

        def section(block, b):
            @block.gpsimd
            def _(pool):
                for r in range(2):
                    pool.tensor_copy(xb[:, r, :], cols(xnT, b + r)).then_inc(xb_ready, 1)

            @block.tensor
            def _(pe):
                def project(r):
                    pe.wait_ge(xb_ready, r + 1)
                    at_least(pe, scaled_ready, r)
                    at_least(pe, vo_ready, r)
                    for k in range(TPS):
                        pe.matmul(ps_qkv[:, k, 0:3 * P], xb[:, r, k * P:(k + 1) * P], w[:], start=True, stop=True).then_inc(qkv_ready, 1)

                project(0)
                for r in range(2):
                    pe.wait_ge(qk_ready, r + 1)
                    pe.wait_ge(vo_ready, r + 1)
                    at_least(pe, kv_taken, r)
                    for k in range(TPS):
                        mm = pe.matmul(ps_kv[:, 0:P + 1], qk[:, k, P:2 * P], vo[:, k, :], start=(k == 0), stop=(k == TPS - 1))
                    mm.then_inc(kv_ready, 1)
                    at_least(pe, y_taken, r)
                    for k in range(TPS):
                        mm = pe.transpose(ps_m[:, k * P:(k + 1) * P], qk[:, k, 0:P], c["ident"][:])
                    mm.then_inc(qT_ready, 1)
                    if r == 0:
                        project(1)
                    pe.wait_ge(kv_taken, r + 1)
                    pe.wait_ge(qT_taken, r + 1)
                    at_least(pe, o_ready, r)
                    for k in range(TPS):
                        mm = pe.matmul(num(k), qT[:, k * P:(k + 1) * P], kv[:], start=True, stop=True)
                    mm.then_inc(num_ready, 1)
                    pe.wait_ge(o_ready, r + 1)
                    for k in range(TPS):
                        mm = pe.transpose(ps_m[:, k * P:(k + 1) * P], o[:, k, :], c["ident"][:])
                    mm.then_inc(oT_ready, 1)
                    pe.wait_ge(oT_taken, r + 1)
                    pe.matmul(ps_m[:], wo[:], oT[:], start=True, stop=True).then_inc(y_ready, 1)

            @block.scalar
            def _(act):
                def normalized(r):
                    act.wait_ge(qkv_ready, TPS * (r + 1))
                    act.activation(sq[:], ps_qkv[:, :, 0:2 * P], ACT.Square).then_inc(squared, 1)
                    at_least(act, kv_ready, r)
                    act.copy(vo[:, :, 0:P], ps_qkv[:, :, 2 * P:3 * P]).then_inc(vo_ready, 1)
                    act.wait_ge(var_ready, r + 1)
                    act.activation(std[:], var[:], ACT.Sqrt).then_inc(std_ready, 1)
                    act.wait_ge(scaled_ready, r + 1)
                    at_least(act, qT_ready, r)
                    act.activation(qk[:], scaled[:].rearrange("p k a d -> p k (a d)"), ACT.Relu).then_inc(qk_ready, 1)

                def take_q(r):
                    act.wait_ge(qT_ready, r + 1)
                    act.copy(qT[:], ps_m[:]).then_inc(qT_taken, 1)

                def take_o(r):
                    act.wait_ge(oT_ready, r + 1)
                    act.copy(oT[:], ps_m[:]).then_inc(oT_taken, 1)

                normalized(0)
                take_q(0)
                normalized(1)
                take_o(0)
                take_q(1)
                take_o(1)

            @block.vector
            def _(dve):
                def normalized(r):
                    dve.wait_ge(squared, r + 1)
                    dve.tensor_reduce(sqsum[:], sq[:].rearrange("p k (a d) -> p k a d", a=2), AX.X, ALU.add)
                    dve.drain()
                    dve.tensor_scalar(var[:], sqsum[:], 1.0 / P, EPS_NORM, ALU.mult, ALU.add).then_inc(var_ready, 1)
                    dve.wait_ge(std_ready, r + 1)
                    dve.reciprocal(rstd[:], std[:])
                    dve.drain()
                    dve.wait_ge(vo_ready, r + 1)
                    at_least(dve, qk_ready, r)
                    for k in range(TPS):
                        for a in range(2):
                            dve.scalar_tensor_tensor(out=scaled[:, k, a, :], in0=ps_qkv[:, k, a * P:(a + 1) * P], scalar=rstd[:, k, a:a + 1],
                                                     in1=nw[:, a, :], op0=ALU.mult, op1=ALU.mult)
                    dve.drain().then_inc(scaled_ready, 1)

                def heads_kv(r):
                    dve.wait_ge(kv_ready, r + 1)
                    dve.tensor_tensor(kv[:, 0:P], ps_kv[:, 0:P], blocks[:, 0:P], ALU.mult)
                    dve.tensor_scalar(kv[:, P:NUM], blocks[:, P:NUM], ps_kv[:, P:P + 1], None, ALU.mult)
                    dve.drain().then_inc(kv_taken, 1)

                def quotients(r):
                    dve.wait_ge(num_ready, r + 1)
                    for k in range(TPS):
                        dve.tensor_scalar(den[:, k, :], num(k)[:, P:NUM], EPS_DEN, None, ALU.add)
                    dve.drain()
                    dve.reciprocal(den[:], den[:])
                    dve.drain()
                    for k in range(TPS):
                        dve.tensor_tensor(o[:, k, :].rearrange("p (h d) -> p h d", d=D), num(k)[:, 0:P].rearrange("p (h d) -> p h d", d=D),
                                          bcast(den[:, k, :], D), ALU.mult)
                    dve.drain().then_inc(o_ready, 1)

                def finish(r):
                    dve.wait_ge(y_ready, r + 1)
                    x = cols(xT, b + r)
                    dve.scalar_tensor_tensor(out=x, in0=ps_m[:], scalar=bout[:], in1=x, op0=ALU.add, op1=ALU.add).then_inc(y_taken, 1)

                normalized(0)
                heads_kv(0)
                normalized(1)
                quotients(0)
                finish(0)
                heads_kv(1)
                quotients(1)
                finish(1)

        with nc.Fori(0, NSEQ // 2) as i:
            with nc.Block() as block:
                section(block, 2 * i)
            clear(nc, ph.sems)


def split(dve, gate, gate3, tmp, E):
    for q in range(3):
        dve.tensor_copy(tmp[:], gate[:])
        dve.drain()
        dve.tensor_copy(gate3[:, :, 32 * q:32 * q + E], tmp[:])
        if q < 2:
            dve.tensor_tensor(gate[:], gate[:], tmp[:], ALU.subtract)
        dve.drain()


def experts(nc, xT, xnT, c, ph, U, wa, wb, wo, parts, sel, kind, b_glu=None, b_lin=None, b_out=None, shared=None, bias=None,
            xparts=None):
    swiglu, gates = kind == "swiglu", kind != "geglu"
    LIMIT, ALPHA = 7.0, 1.702
    LAG = 2 if swiglu else 1
    NBUF = LAG + 1
    with ExitStack() as ctx:
        ph2 = Phase(nc, ctx, ph.name + "x")
        NU = U + (1 if shared else 0)
        rows = lambda u: P if u < U else P // 2
        gl, sg, lt, pr, gated = (ph2.sb(n, [P, NBUF, SEQ]) for n in ("gl", "sg", "lt", "pr", "gated"))
        ps_a, ps_b, ps_g, ps_o = (ph2.ps(n, [P, 2, SEQ]) for n in ("psa", "psb", "psg", "pso"))
        a_ready, b_ready, g_ready, a_taken, b_taken, sg_ready, pr_ready, gated_ready, out_done, y_ready, y_taken = (
            ph2.sem(n) for n in ("a_ready", "b_ready", "g_ready", "a_taken", "b_taken", "sg_ready", "pr_ready", "gated_ready",
                                 "out_done", "y_ready", "y_taken"))

        def section(block, b):
            @block.tensor
            def _(pe):
                def product(out, weights, r):
                    if xparts is None:
                        return pe.matmul(out, weights, cols(xnT, b + r), start=True, stop=True)
                    for q in range(3):
                        mm = pe.matmul(out, weights, cols(xparts[:, q, :], b + r), start=(q == 0), stop=(q == 2))
                    return mm

                def front(r, u):
                    n, m = r * NU + u, rows(u)
                    at_least(pe, a_taken, n - 1)
                    A, B = (wa[:, u, :], wb[:, u, :]) if u < U else (shared[0][:], shared[1][:])
                    product(ps_a[0:m, n % 2, :], A, r).then_inc(a_ready, 1)
                    at_least(pe, b_taken, n - 1)
                    product(ps_b[0:m, n % 2, :], B, r).then_inc(b_ready, 1)

                def gates_of(r, u):
                    n = r * NU + u
                    at_least(pe, gated_ready, n - 1)
                    if u < U and gates:
                        pe.matmul(ps_g[:, n % 2, :], sel[:, u, :], cols(parts, b + r), start=True, stop=True).then_inc(g_ready, 1)

                def back(r, u):
                    n, m = r * NU + u, rows(u)
                    pe.wait_ge(gated_ready, n + 1)
                    O = wo[:, u, :] if u < U else shared[2][:]
                    more = b_out is not None
                    pe.matmul(ps_o[:, r, :], O, gated[0:m, n % NBUF, :], start=(u == 0), stop=(u == NU - 1 and not more)).then_inc(out_done, 1)
                    if u == NU - 1:
                        if more:
                            for q in range(3):
                                pe.matmul(ps_o[:, r, :], b_out[:, q, :], cols(parts, b + r), start=False, stop=(q == 2))
                        pe.drain().then_inc(y_ready, 1)

                steps = [(r, u) for r in range(2) for u in range(NU)]
                for i in range(len(steps) + LAG):
                    if i < len(steps):
                        front(*steps[i])
                    if 0 <= i - LAG + 1 < len(steps):
                        gates_of(*steps[i - LAG + 1])
                    if i >= LAG:
                        back(*steps[i - LAG])

            @block.scalar
            def _(act):
                for r in range(2):
                    for u in range(NU):
                        n, m = r * NU + u, rows(u)
                        if swiglu:
                            act.wait_ge(a_taken, n + 1)
                            at_least(act, pr_ready, n - LAG)
                            act.activation(sg[:, n % NBUF, :], gl[:, n % NBUF, :], ACT.Sigmoid, scale=ALPHA).then_inc(sg_ready, 1)
                        elif kind == "geglu":
                            act.wait_ge(b_ready, n + 1)
                            at_least(act, gated_ready, n - 1)
                            act.activation(sg[:, n % NBUF, :], ps_b[:, n % 2, :], ACT.Gelu, bias=b_lin[:, u:u + 1]).then_inc(sg_ready, 1)
                            act.drain().then_inc(b_taken, 1)
                        else:
                            act.wait_ge(a_ready, n + 1)
                            at_least(act, pr_ready, n - 1)
                            act.activation(sg[0:m, n % NBUF, :], ps_a[0:m, n % 2, :], ACT.Silu).then_inc(sg_ready, 1)
                            act.drain().then_inc(a_taken, 1)

            if swiglu:
                @block.gpsimd
                def _(pool):
                    for n in range(2 * NU):
                        pool.wait_ge(sg_ready, n + 1)
                        at_least(pool, gated_ready, n - LAG)
                        pool.tensor_tensor(pr[:, n % NBUF, :], gl[:, n % NBUF, :], sg[:, n % NBUF, :], ALU.mult).then_inc(pr_ready, 1)

            def finish(dve, r):
                dve.wait_ge(y_ready, r + 1)
                x = cols(xT, b + r)
                if bias is None:
                    dve.tensor_tensor(x, x, ps_o[:, r, :], ALU.add).then_inc(y_taken, 1)
                else:
                    dve.scalar_tensor_tensor(out=x, in0=ps_o[:, r, :], scalar=bias[:], in1=x, op0=ALU.add, op1=ALU.add).then_inc(y_taken, 1)

            @block.vector
            def _(dve):
                def front(r, u):
                    n, m = r * NU + u, rows(u)
                    if swiglu:
                        dve.wait_ge(a_ready, n + 1)
                        at_least(dve, pr_ready, n - LAG)
                        dve.tensor_scalar(gl[:, n % NBUF, :], ps_a[:, n % 2, :], b_glu[:, u:u + 1], LIMIT, ALU.add, ALU.min).then_inc(a_taken, 1)
                        dve.wait_ge(b_ready, n + 1)
                        dve.tensor_scalar(lt[:, n % NBUF, :], ps_b[:, n % 2, :], b_lin[:, u:u + 1], 1.0 - LIMIT, ALU.add, ALU.max).then_inc(b_taken, 1)

                def back(r, u):
                    n, m = r * NU + u, rows(u)
                    if kind == "geglu":
                        dve.wait_ge(sg_ready, n + 1)
                        dve.wait_ge(a_ready, n + 1)
                        at_least(dve, out_done, n - LAG)
                        dve.scalar_tensor_tensor(out=gated[:, n % NBUF, :], in0=ps_a[:, n % 2, :], scalar=b_glu[:, u:u + 1], in1=sg[:, n % NBUF, :],
                                                 op0=ALU.add, op1=ALU.mult).then_inc(gated_ready, 1)
                        dve.drain().then_inc(a_taken, 1)
                        return
                    if swiglu:
                        dve.drain()
                        dve.wait_ge(pr_ready, n + 1)
                        dve.scalar_tensor_tensor(out=lt[:, n % NBUF, :], in0=lt[:, n % NBUF, :], scalar=1.0 + LIMIT, in1=pr[:, n % NBUF, :],
                                                 op0=ALU.min, op1=ALU.mult)
                    else:
                        dve.wait_ge(sg_ready, n + 1)
                        dve.wait_ge(b_ready, n + 1)
                        at_least(dve, out_done, n - LAG)
                        dst = lt if u < U else gated
                        dve.tensor_tensor(dst[0:m, n % NBUF, :], sg[0:m, n % NBUF, :], ps_b[0:m, n % 2, :], ALU.mult).then_inc(pr_ready, 1)
                        dve.drain().then_inc(b_taken, 1)
                    if u == U:
                        dve.sem_inc(gated_ready, 1)
                        return
                    if swiglu:
                        dve.drain()
                    dve.wait_ge(g_ready, r * U + u + 1)
                    at_least(dve, out_done, n - LAG)
                    dve.tensor_tensor(gated[:, n % NBUF, :], lt[:, n % NBUF, :], ps_g[:, n % 2, :], ALU.mult).then_inc(gated_ready, 1)

                steps = [(r, u) for r in range(2) for u in range(NU)]
                for i in range(len(steps) + LAG):
                    if i >= LAG:
                        back(*steps[i - LAG])
                        if steps[i - LAG][1] == NU - 1:
                            finish(dve, steps[i - LAG][0])
                    if i < len(steps):
                        front(*steps[i])

        with nc.Fori(0, NSEQ // 2) as i:
            with nc.Block() as block:
                section(block, 2 * i)
            clear(nc, ph2.sems)


def l3_ffn(nc, xT, xnT, c, t):
    normalize(nc, xT, xnT, c, "l3fn", EPS)
    add_normed(nc, xT, xnT)
    normalize(nc, xnT, xnT, c, "l3fm", float(np.finfo(np.float32).eps), center=False)
    E = 8
    with ExitStack() as ctx:
        ph = Phase(nc, ctx, "l3f")
        wa, wb, wo = (ph.sb(n, [P, E, P]) for n in ("wa", "wb", "wo"))
        gw, gb = ph.sb("gw", [P, E]), ph.sb("gb", [P, E])
        b_glu, b_lin = ph.sb("b_glu", [P, E]), ph.sb("b_lin", [P, E])
        normw = ph.sb("normw", [P, 1])
        selF, sel = ph.sb("self", [96, E, P]), ph.sb("sel", [96, E, P], BF16)
        b2, b2left = ph.sb("b2", [96, P]), ph.sb("b2left", [96, P])
        b2p = ph.sb("b2p", [96, 3, P], BF16)
        parts = ph.sb("parts", [96, TOK], BF16)
        with ExitStack() as ctx2:
            g = Phase(nc, ctx2, "l3g")
            logits, e, gate = (g.sb(n, [P, NT, E]) for n in ("logits", "e", "gate"))
            top = g.sb("top", [P, NT, 8])
            total, rtotal = g.sb("total", [P, NT]), g.sb("rtotal", [P, NT])
            gate3, tmp = g.sb("gate3", [P, NT, 96]), g.sb("tmp", [P, NT, E], BF16)
            ps_l = g.ps("psl", [P, NT, E])
            ps_t = g.ps("pst", [P, 4, SEQ])
            loaded, zeroed, gate3_zeroed, scaled, logits_ready, shifted, e_ready, gate_ready, turned, taken = (
                g.sem(n) for n in ("loaded", "zeroed", "gate3_zeroed", "scaled", "logits_ready", "shifted", "e_ready", "gate_ready", "turned", "taken"))
            with nc.Block() as block:
                @block.sync
                def _(sp):
                    sp.dma_start(normw[:], t["L3_ffn_norm_w"].unsqueeze(1)).then_inc(loaded, 16)
                    sp.dma_start(gw[:], t["L3_ffn_gate_wT"]).then_inc(loaded, 16)
                    sp.dma_start(gb[:], t["L3_ffn_gate_b"].unsqueeze(0).to_broadcast([P, E])).then_inc(loaded, 16)
                    sp.dma_start(b_glu[:], t["L3_ffn_b1T"][:, 0, :]).then_inc(loaded, 16)
                    sp.dma_start(b_lin[:], t["L3_ffn_b1T"][:, 1, :]).then_inc(loaded, 16)
                    sp.dma_start(selF[:], t["sel8"]).then_inc(loaded, 16)
                    sp.wait_ge(zeroed, 1)
                    for q in range(3):
                        sp.dma_start(b2[32 * q:32 * q + E, :], t["L3_ffn_mlp2_b"]).then_inc(loaded, 16)
                    sp.dma_start(wa[:], t["L3_ffn_w1T"][:, :, 0, :]).then_inc(loaded, 16)
                    sp.dma_start(wb[:], t["L3_ffn_w1T"][:, :, 1, :]).then_inc(loaded, 16)
                    sp.dma_start(wo[:], t["L3_ffn_w2T"]).then_inc(loaded, 16)

                @block.gpsimd
                def _(pool):
                    pool.memset(b2[:], 0.0).then_inc(zeroed, 1)
                    pool.memset(gate3[:], 0.0).then_inc(gate3_zeroed, 1)

                @block.scalar
                def _(act):
                    act.wait_ge(loaded, 16 * 12)
                    for b in range(NSEQ):
                        act.activation(cols(xnT, b), cols(xnT, b), ACT.Copy, scale=normw[:]).then_inc(scaled, 1)
                    act.copy(sel[:], selF[:])
                    act.wait_ge(shifted, 1)
                    act.activation(e[:], e[:], ACT.Exp).then_inc(e_ready, 1)
                    for b in range(NSEQ):
                        act.wait_ge(turned, b + 1)
                        act.copy(cols(parts, b), ps_t[0:96, b % 4, :]).then_inc(taken, 1)

                @block.tensor
                def _(pe):
                    for k in range(NT):
                        if k % TPS == 0:
                            pe.wait_ge(scaled, k // TPS + 1)
                        mm = pe.matmul(ps_l[:, k, :], xnT[:, k * P:(k + 1) * P], gw[:], start=True, stop=True)
                    mm.then_inc(logits_ready, 1)
                    pe.wait_ge(gate_ready, 1)
                    for b in range(NSEQ):
                        at_least(pe, taken, b - 3)
                        for k in range(TPS):
                            mm = pe.transpose(ps_t[0:96, b % 4, k * P:(k + 1) * P], gate3[:, b * TPS + k, :], c["ident"][:])
                        mm.then_inc(turned, 1)

                @block.vector
                def _(dve):
                    dve.wait_ge(loaded, 16 * 12)
                    dve.tensor_scalar(b_lin[:], b_lin[:], 1.0, None, ALU.add)
                    dve.wait_ge(logits_ready, 1)
                    dve.tensor_tensor(logits[:], ps_l[:], gb[:].unsqueeze(1).to_broadcast([P, NT, E]), ALU.add)
                    dve.drain()
                    for k in range(NT):
                        dve.max(top[:, k, :], logits[:, k, :])
                    dve.drain()
                    dve.tensor_tensor(e[:], logits[:], bcast(top[:, :, 0], E), ALU.subtract).then_inc(shifted, 1)
                    dve.tensor_tensor(gate[:], logits[:], bcast(top[:, :, 1], E), ALU.is_ge)
                    dve.wait_ge(e_ready, 1)
                    dve.drain()
                    dve.tensor_tensor(gate[:], gate[:], e[:], ALU.mult)
                    dve.drain()
                    dve.tensor_reduce(total[:], gate[:], AX.X, ALU.add)
                    dve.drain()
                    dve.reciprocal(rtotal[:], total[:])
                    dve.drain()
                    dve.tensor_tensor(gate[:], gate[:], bcast(rtotal[:], E), ALU.mult)
                    dve.drain()
                    dve.wait_ge(gate3_zeroed, 1)
                    split(dve, gate, gate3, tmp, E)
                    dve.sem_inc(gate_ready, 1)
            clear(nc, g.sems)
        with nc.Block() as block:
            @block.vector
            def _(dve):
                dve.tensor_copy(b2p[:, 0, :], b2[:])
                dve.drain()
                dve.tensor_tensor(b2left[:], b2[:], b2p[:, 0, :], ALU.subtract)
                dve.drain()
                dve.tensor_copy(b2p[:, 1, :], b2left[:])
                dve.drain()
                dve.tensor_tensor(b2p[:, 2, :], b2left[:], b2p[:, 1, :], ALU.subtract)
        experts(nc, xT, xnT, c, ph, E, wa, wb, wo, parts, sel, "swiglu", b_glu, b_lin, b2p)


def l2_ffn(nc, xT, xnT, c, t):
    normalize(nc, xT, xnT, c, "l2fn", EPS)
    E, TOP, CAPACITY = 32, 4, 2 * 512 * 4 // 32
    U = E // 2
    with ExitStack() as ctx:
        ph = Phase(nc, ctx, "l2f")
        wa, wb, wo = ph.sb("wa", [P, U, P], BF16), ph.sb("wb", [P, U, P], BF16), ph.sb("wo", [P, U, P])
        s1, s3, s2 = ph.sb("s1", [P, P // 2], BF16), ph.sb("s3", [P, P // 2], BF16), ph.sb("s2", [P // 2, P])
        xparts = ph.sb("xparts", [P, 3, TOK], BF16)
        sel = ph.sb("sel", [96, U, P], BF16)
        parts = ph.sb("parts", [96, TOK], BF16)
        with ExitStack() as ctx2:
            g = Phase(nc, ctx2, "l2g")
            raw = g.sb("raw", [P, U, P], BF16)
            raws = g.sb("raws", [P, 2, P], BF16)
            left = g.sb("left", [P, SEQ])
            selF = g.sb("self", [96, U // 4, P])
            gw, gb = g.sb("gw", [P, E]), g.sb("gb", [P, E])
            scores, biased, mask, gate = (g.sb(n, [P, NT, E]) for n in ("scores", "biased", "mask", "gate"))
            top = g.sb("top", [P, NT, 8])
            total, rtotal = g.sb("total", [P, NT]), g.sb("rtotal", [P, NT])
            gate3, mask3, tmp = g.sb("gate3", [P, NT, 96]), g.sb("mask3", [P, NT, 3, E]), g.sb("tmp", [P, NT, E], BF16)
            maskT, zeros = g.sb("maskT", [96, TOK]), g.sb("zeros", [96, TOK])
            ps_l = g.ps("psl", [P, NT, E])
            ps_t = g.ps("pst", [P, 4, SEQ])
            loaded, zeroed, reused, small_ready, logits_ready, scores_ready, mask_ready, gate_ready, mask_turned, mask_taken, turned, taken = (
                g.sem(n) for n in ("loaded", "zeroed", "reused", "small_ready", "logits_ready", "scores_ready", "mask_ready", "gate_ready",
                                   "mask_turned", "mask_taken", "turned", "taken"))
            with nc.Block() as block:
                @block.sync
                def _(sp):
                    sp.dma_start(gb[:], t["L2_ffn_bias"].unsqueeze(0).to_broadcast([P, E])).then_inc(loaded, 16)
                    sp.dma_start(raws[:, 0, 0:E], t["L2_ffn_gate_wT"]).then_inc(loaded, 16)
                    sp.dma_start(raws[0:P // 2, 1, :], t["L2_ffn_sw2T"]).then_inc(loaded, 16)
                    sp.dma_start(s1[:], t["L2_ffn_sw1T"]).then_inc(loaded, 16)
                    sp.dma_start(s3[:], t["L2_ffn_sw3T"]).then_inc(loaded, 16)
                    sp.dma_start(wa[:], t["L2_ffn_W1p"]).then_inc(loaded, 16)
                    sp.dma_start(wb[:], t["L2_ffn_W3p"]).then_inc(loaded, 16)
                    sp.dma_start(raw[:], t["L2_ffn_W2p"]).then_inc(loaded, 16)
                    sp.wait_ge(loaded, 16 * 8)
                    for n in range(4):
                        at_least(sp, reused, 1 + n)
                        sp.dma_start(selF[:], t["sel32"][:, 4 * n:4 * n + 4, :]).then_inc(loaded, 16)

                @block.gpsimd
                def _(pool):
                    pool.memset(zeros[:], 0.0).then_inc(zeroed, 1)
                    pool.wait_ge(loaded, 16 * 8)
                    pool.tensor_copy(wo[:], raw[:]).then_inc(reused, 1)
                    for n in range(4):
                        pool.wait_ge(loaded, 16 * (9 + n))
                        pool.tensor_copy(sel[:, 4 * n:4 * n + 4, :], selF[:]).then_inc(reused, 1)
                    for b in range(NSEQ):
                        part = lambda q: cols(xparts[:, q, :], b)
                        pool.tensor_copy(part(0), cols(xnT, b))
                        pool.drain()
                        pool.tensor_tensor(left[:], cols(xnT, b), part(0), ALU.subtract)
                        pool.drain()
                        pool.tensor_copy(part(1), left[:])
                        pool.drain()
                        pool.tensor_tensor(part(2), left[:], part(1), ALU.subtract)
                        pool.drain()

                @block.scalar
                def _(act):
                    act.wait_ge(loaded, 16 * 8)
                    act.copy(gw[:], raws[:, 0, 0:E]).then_inc(small_ready, 1)
                    act.copy(s2[:], raws[0:P // 2, 1, :])
                    act.wait_ge(logits_ready, 1)
                    act.activation(scores[:], ps_l[:], ACT.Sigmoid).then_inc(scores_ready, 1)
                    for b in range(NSEQ):
                        act.wait_ge(mask_turned, b + 1)
                        act.copy(cols(maskT, b), ps_t[0:96, b % 4, :]).then_inc(mask_taken, 1)

                @block.tensor
                def _(pe):
                    pe.wait_ge(small_ready, 1)
                    for k in range(NT):
                        mm = pe.matmul(ps_l[:, k, :], xnT[:, k * P:(k + 1) * P], gw[:], start=True, stop=True)
                    mm.then_inc(logits_ready, 1)
                    pe.wait_ge(mask_ready, 1)
                    for b in range(NSEQ):
                        at_least(pe, mask_taken, b - 3)
                        for k in range(TPS):
                            mm = pe.transpose(ps_t[0:96, b % 4, k * P:(k + 1) * P],
                                              mask3[:, b * TPS + k, :, :].rearrange("p q e -> p (q e)"), c["ident"][:])
                        mm.then_inc(mask_turned, 1)
                    pe.wait_ge(gate_ready, 1)
                    pe.wait_ge(mask_taken, NSEQ)
                    for b in range(NSEQ):
                        at_least(pe, taken, b - 3)
                        for k in range(TPS):
                            mm = pe.transpose(ps_t[0:96, b % 4, k * P:(k + 1) * P], gate3[:, b * TPS + k, :], c["ident"][:])
                        mm.then_inc(turned, 1)

                @block.vector
                def _(dve):
                    dve.wait_ge(loaded, 16 * 8)
                    dve.wait_ge(scores_ready, 1)
                    dve.tensor_tensor(biased[:], scores[:], gb[:].unsqueeze(1).to_broadcast([P, NT, E]), ALU.add)
                    dve.drain()
                    for k in range(NT):
                        dve.max(top[:, k, :], biased[:, k, :])
                    dve.drain()
                    dve.tensor_tensor(mask[:], biased[:], bcast(top[:, :, TOP - 1], E), ALU.is_ge)
                    dve.drain()
                    dve.tensor_copy(mask3[:], mask[:].unsqueeze(2).to_broadcast([P, NT, 3, E])).then_inc(mask_ready, 1)
                    dve.tensor_tensor(gate[:], mask[:], scores[:], ALU.mult)
                    dve.drain()
                    dve.tensor_reduce(total[:], gate[:], AX.X, ALU.add)
                    dve.drain()
                    dve.tensor_scalar(total[:], total[:], 1e-12, None, ALU.max)
                    dve.drain()
                    dve.reciprocal(rtotal[:], total[:])
                    dve.drain()
                    dve.tensor_tensor(gate[:], gate[:], bcast(rtotal[:], E), ALU.mult)
                    dve.drain()
                    split(dve, gate, gate3, tmp, E)
                    dve.sem_inc(gate_ready, 1)
                    dve.wait_ge(zeroed, 1)
                    dve.wait_ge(mask_taken, NSEQ)
                    dve.tensor_tensor_scan(maskT[:], maskT[:], zeros[:], 0.0, ALU.add, ALU.add)
                    dve.drain()
                    for b in range(NSEQ):
                        dve.wait_ge(turned, b + 1)
                        dve.scalar_tensor_tensor(out=cols(parts, b), in0=cols(maskT, b), scalar=float(CAPACITY), in1=ps_t[0:96, b % 4, :],
                                                 op0=ALU.is_le, op1=ALU.mult).then_inc(taken, 1)
            clear(nc, g.sems)
        experts(nc, xT, xnT, c, ph, U, wa, wb, wo, parts, sel, "silu", shared=(s1, s3, s2), xparts=xparts)


def l1_ffn(nc, xT, xnT, c, t):
    normalize(nc, xT, xnT, c, "l1fn", EPS)
    for layer in range(2):
        local_attention(nc, xnT, c, t, layer)
        geglu(nc, xnT, c, t, layer)
    add_normed(nc, xT, xnT)


def local_attention(nc, yT, c, t, layer):
    H, D, WINDOW, PARTS = 8, 64, 64, 3
    PAIRS = H // 2
    INNER = H * D
    TURN_AT = 4
    NQK = 2 * PAIRS
    with ExitStack() as ctx:
        ph = Phase(nc, ctx, f"l1l{layer}")
        w = ph.sb("w", [P, 3 * INNER])
        wswap = ph.sb("wswap", [P, NQK, P])
        wo = ph.sb("wo", [P, PAIRS, P])
        tables = ph.sb("tables", [P, 4, SEQ])
        scales = ph.sb("scales", [P, 4])
        statsel = ph.sb("statsel", [P, NQK, 2 * H])
        spreadF, spread = ph.sb("spreadf", [96, NQK, P]), ph.sb("spread", [96, NQK, P], BF16)
        lselF, lsel = ph.sb("lself", [PARTS * H, H, P]), ph.sb("lsel", [PARTS * H, H, P], BF16)
        identb = ph.sb("identb", [P, P], BF16)
        maskF, maskA, maskT = ph.sb("maskf", [P, 2, P + WINDOW]), ph.sb("maska", [P, P + WINDOW], BF16), ph.sb("maskt", [P, P + WINDOW], BF16)
        h = ph.sb("h", [P, SEQ])
        sq, t1, t2 = (ph.sb(n, [P, 2, SEQ]) for n in ("sq", "t1", "t2"))
        raw = ph.sb("raw", [P, NQK, SEQ])
        q = ph.sb("q", [P, PAIRS, SEQ])
        kz = ph.sb("kz", [P, 2, PAIRS, SEQ])
        v = ph.sb("v", [P, TPS, INNER])
        norm, rnorm, left = (ph.sb(n, [2 * H, SEQ]) for n in ("norm", "rnorm", "left"))
        mid = ph.sb("mid", [2 * H, SEQ], BF16)
        rparts = ph.sb("rparts", [96, SEQ], BF16)
        nm, s, shift = (ph.sb(n, [P, TPS, H]) for n in ("nm", "s", "shift"))
        sparts, spart = ph.sb("sparts", [P, TPS, PARTS, H]), ph.sb("spart", [P, TPS, H], BF16)
        junk = ph.sb("junk", [P, P + WINDOW], BF16)
        lrows = ph.sb("lrows", [PARTS * H, SEQ], BF16)
        pt = ph.sb("pt", [P, 4, 2, P + WINDOW])
        oT = ph.sb("ot", [P, PAIRS, SEQ])
        zeros = ph.sb("zeros", [P, SEQ], BF16)
        ps_w = ph.ps("psw", [P, 4, SEQ])
        ps_s = ph.ps("pss", [P, SEQ])
        ps_t = ph.ps("pst", [P, SEQ])
        ps_o = ph.ps("pso", [P, 2, SEQ])
        names = ("loaded", "h_ready", "proj_ready", "swap_ready", "squared", "t1_ready", "t2_ready", "t_taken", "v_ready", "v_taken",
                 "stats_done", "norm_ready", "rparts_ready", "spread_ready", "spread_taken", "sa_ready", "max_ready", "sum_ready",
                 "ln_ready", "shift_ready", "turned", "lrows_ready", "st_ready", "p_ready", "pv_done", "o_taken", "y_ready")
        (loaded, h_ready, proj_ready, swap_ready, squared, t1_ready, t2_ready, t_taken, v_ready, v_taken, stats_done,
         norm_ready, rparts_ready, spread_ready, spread_taken, sa_ready, max_ready, sum_ready, ln_ready, shift_ready, turned, lrows_ready,
         st_ready, p_ready, pv_done, o_taken, y_ready) = (ph.sem(n) for n in names)
        with nc.Block() as block:
            @block.sync
            def _(sp):
                for dst, src in ((w[:], t["L1_ffn_wqkv"][layer]), (wswap[:], t["L1_ffn_wswap"][layer]),
                                 (wo[:], t["L1_ffn_wo"][layer].rearrange("(i p) d -> p i d", p=P)), (tables[:], t["xpos"]),
                                 (scales[:], t["L1_ffn_scales"][layer]), (statsel[:], t["statsel"]), (spreadF[:], t["spread"]),
                                 (lselF[:], t["lsel"]), (maskF[:], t["band"])):
                    sp.dma_start(dst, src).then_inc(loaded, 16)
                sp.wait_ge(loaded, 16 * 9)

            @block.scalar
            def _(act):
                act.wait_ge(loaded, 16 * 9)
                for n in range(4):
                    act.activation(tables[:, n, :], tables[:, n, :], ACT.Copy, scale=scales[:, n:n + 1])
                act.copy(identb[:], c["ident"][:])
                act.copy(spread[:], spreadF[:])
                act.copy(lsel[:], lselF[:])
                act.copy(maskA[:], maskF[:, 0, :])
                act.copy(maskT[:], maskF[:, 1, :])

            @block.gpsimd
            def _(pool):
                pool.memset(h[:], 0.0)
                pool.memset(rparts[:], 0.0)
                pool.memset(zeros[:], 0.0)

            @block.vector
            def _(dve):
                dve.memset(kz[:], 0.0)
        clear(nc, ph.sems)

        units_a = [(hd, qt) for hd in range(H) for qt in range(TPS)]
        units_b = [(i, kt) for i in range(PAIRS) for kt in range(TPS)]
        wide = lambda kt: min(P + WINDOW, SEQ - kt * P)

        NA, NB = len(units_a), len(units_b)

        def section(block, b, main, front):
            y = cols(yT, b) if main else None
            yn = cols(yT, b + 1) if front else None

            @block.gpsimd
            def _(pool):
                if not front:
                    return
                pool.tensor_copy(h[0:64, :], yn[0:64, :])
                pool.tensor_copy(h[64:P, 1:SEQ], yn[64:P, 0:SEQ - 1])
                pool.drain().then_inc(h_ready, 1)
                for m in range(NQK):
                    pool.wait_ge(t2_ready, m + 1)
                    pool.tensor_tensor(raw[:, m, :], t1[:, m % 2, :], t2[:, m % 2, :], ALU.add).then_inc(t_taken, 1)

            @block.tensor
            def _(pe):
                def stats(m):
                    pe.wait_ge(squared, m + 1)
                    mm = pe.matmul(ps_s[0:2 * H, :], statsel[:, m, :], sq[:, m % 2, :], start=(m == 0), stop=(m == NQK - 1))
                    mm.then_inc(stats_done, 1)

                def turn_shift():
                    pe.wait_ge(shift_ready, 1)
                    for k in range(TPS):
                        mm = pe.transpose(ps_t[0:PARTS * H, k * P:(k + 1) * P], sparts[:, k, :, :].rearrange("p a h -> p (a h)"), c["ident"][:])
                    mm.then_inc(turned, 1)

                def weigh(n):
                    i, kt = units_b[n]
                    wd = wide(kt)
                    pe.wait_ge(p_ready, n + 1)
                    if kt == 0:
                        at_least(pe, o_taken, i - 1)
                        pe.matmul(ps_o[:, i % 2, :], zeros[:, 0:P], zeros[:], start=True, stop=True)
                    for e in range(2):
                        mm = pe.matmul(ps_o[64 * e:64 * e + 64, i % 2, kt * P:kt * P + wd], v[:, kt, (2 * i + e) * D:(2 * i + e + 1) * D],
                                       pt[:, n % 4, e, 0:wd], start=False, stop=True, skip_group_check=True)
                    mm.then_inc(pv_done, 1)

                if main:
                    for n, (hd, qt) in enumerate(units_a):
                        i, e = hd // 2, hd % 2
                        at_least(pe, sum_ready, n - 3)
                        k0 = max(qt * P - WINDOW, 0)
                        wd = (qt + 1) * P - k0
                        pe.matmul(ps_w[:, n % 4, 0:wd], q[:, i, qt * P:(qt + 1) * P], kz[:, e, i, k0:k0 + wd], start=True, stop=False)
                        pe.matmul(ps_w[:, n % 4, 0:wd], identb[:], maskA[:, P + WINDOW - wd:], start=False, stop=True).then_inc(sa_ready, 1)
                if front:
                    pe.wait_ge(h_ready, 1)
                    if main:
                        pe.wait_ge(sum_ready, NA)
                    for m in range(NQK):
                        at_least(pe, t1_ready, m - 1)
                        pe.matmul(ps_w[:, m % 2, :], w[:, m * P:(m + 1) * P], h[:], start=True, stop=True).then_inc(proj_ready, 1)
                        at_least(pe, t2_ready, m - 1)
                        pe.matmul(ps_w[:, 2 + m % 2, :], wswap[:, m, :], h[:], start=True, stop=True).then_inc(swap_ready, 1)
                        if m:
                            stats(m - 1)
                        if main and m == TURN_AT:
                            turn_shift()
                    stats(NQK - 1)
                    pe.wait_ge(t2_ready, NQK)
                elif main:
                    turn_shift()
                if main:
                    pe.wait_ge(sum_ready, NA)
                    pe.wait_ge(lrows_ready, 1)
                    for n, (i, kt) in enumerate(units_b):
                        wd = wide(kt)
                        at_least(pe, p_ready, n - 1)
                        for e in range(2):
                            out = ps_w[:, 2 * (n % 2) + e, 0:wd]
                            pe.matmul(out, kz[:, e, i, kt * P:(kt + 1) * P], q[:, i, kt * P:kt * P + wd], start=True, stop=False)
                            pe.matmul(out, identb[:], maskT[:, 0:wd], start=False, stop=False)
                            mm = pe.matmul(out, lsel[:, 2 * i + e, :], lrows[:, kt * P:kt * P + wd], start=False, stop=True)
                        mm.then_inc(st_ready, 1)
                        if n >= 2:
                            weigh(n - 2)
                    weigh(NB - 2)
                    weigh(NB - 1)
                for m in range(NQK) if front else ():
                    if m == 0:
                        pe.wait_ge(rparts_ready, 1)
                    at_least(pe, spread_taken, m - 1)
                    pe.matmul(ps_w[:, 2 + m % 2, :], spread[:, m, :], rparts[:], start=True, stop=True).then_inc(spread_ready, 1)
                    if m == 1 and main:
                        for i in range(PAIRS):
                            pe.wait_ge(o_taken, i + 1)
                            mm = pe.matmul(ps_s[:], wo[:, i, :], oT[:, i, :], start=(i == 0), stop=(i == PAIRS - 1))
                        mm.then_inc(y_ready, 1)
                for k in range(TPS) if front else ():
                    at_least(pe, v_taken, k - 1)
                    pe.matmul(ps_w[:, k % 2, :], h[:, k * P:(k + 1) * P], w[:, 2 * INNER:], start=True, stop=True).then_inc(v_ready, 1)
                if main and not front:
                    for i in range(PAIRS):
                        pe.wait_ge(o_taken, i + 1)
                        mm = pe.matmul(ps_s[:], wo[:, i, :], oT[:, i, :], start=(i == 0), stop=(i == PAIRS - 1))
                    mm.then_inc(y_ready, 1)

            @block.scalar
            def _(act):
                def take_shift():
                    act.wait_ge(turned, 1)
                    act.copy(lrows[:], ps_t[0:PARTS * H, :]).then_inc(lrows_ready, 1)

                if main:
                    for n, (hd, qt) in enumerate(units_a):
                        wd = (qt + 1) * P - max(qt * P - WINDOW, 0)
                        act.wait_ge(max_ready, n + 1)
                        act.activation(junk[:, 0:wd], ps_w[:, n % 4, 0:wd], ACT.Exp, bias=nm[:, qt, hd:hd + 1], accum_out=s[:, qt, hd:hd + 1])
                        act.drain().then_inc(sum_ready, 1)
                    act.activation(shift[:], s[:], ACT.Ln).then_inc(ln_ready, 1)
                if front:
                    for m in range(NQK):
                        act.wait_ge(proj_ready, m + 1)
                        at_least(act, stats_done, m - 1)
                        act.activation(sq[:, m % 2, :], ps_w[:, m % 2, :], ACT.Square).then_inc(squared, 1)
                        if main and m == TURN_AT + 1:
                            take_shift()
                    act.wait_ge(stats_done, NQK)
                    act.activation(norm[:], ps_s[0:2 * H, :], ACT.Sqrt).then_inc(norm_ready, 1)
                elif main:
                    take_shift()
                for n, (i, kt) in enumerate(units_b) if main else ():
                    wd = wide(kt)
                    act.wait_ge(st_ready, n + 1)
                    at_least(act, pv_done, n - 3)
                    act.activation(pt[:, n % 4, :, 0:wd], ps_w[:, 2 * (n % 2):2 * (n % 2) + 2, 0:wd], ACT.Exp).then_inc(p_ready, 1)
                for k in range(TPS) if front else ():
                    act.wait_ge(v_ready, k + 1)
                    act.copy(v[:, k, :], ps_w[:, k % 2, :]).then_inc(v_taken, 1)

            @block.vector
            def _(dve):
                for n, (hd, qt) in enumerate(units_a) if main else ():
                    wd = (qt + 1) * P - max(qt * P - WINDOW, 0)
                    dve.wait_ge(sa_ready, n + 1)
                    dve.tensor_reduce(nm[:, qt, hd:hd + 1], ps_w[:, n % 4, 0:wd], AX.X, ALU.max, negate=True).then_inc(max_ready, 1)
                if main:
                    dve.wait_ge(ln_ready, 1)
                    dve.tensor_tensor(shift[:], nm[:], shift[:], ALU.subtract)
                    dve.drain()
                    for n in range(PARTS):
                        dve.tensor_copy(spart[:], shift[:])
                        dve.drain()
                        dve.tensor_copy(sparts[:, :, n, :], spart[:])
                        if n < PARTS - 1:
                            dve.tensor_tensor(shift[:], shift[:], spart[:], ALU.subtract)
                        dve.drain()
                    dve.sem_inc(shift_ready, 1)
                if front:
                    for m in range(NQK):
                        tab = 0 if m < PAIRS else 2
                        dve.wait_ge(squared, m + 1)
                        at_least(dve, t_taken, m - 1)
                        dve.tensor_tensor(t1[:, m % 2, :], ps_w[:, m % 2, :], tables[:, tab, :], ALU.mult).then_inc(t1_ready, 1)
                        dve.wait_ge(swap_ready, m + 1)
                        dve.tensor_tensor(t2[:, m % 2, :], ps_w[:, 2 + m % 2, :], tables[:, tab + 1, :], ALU.mult)
                        dve.drain().then_inc(t2_ready, 1)
                    dve.wait_ge(norm_ready, 1)
                    dve.tensor_scalar(norm[:], norm[:], 1e-12, None, ALU.max)
                    dve.drain()
                    dve.reciprocal(rnorm[:], norm[:])
                    dve.drain()
                    R = 2 * H
                    dve.tensor_copy(rparts[0:R, :], rnorm[:])
                    dve.drain()
                    dve.tensor_tensor(left[:], rnorm[:], rparts[0:R, :], ALU.subtract)
                    dve.drain()
                    dve.tensor_copy(mid[:], left[:])
                    dve.drain()
                    dve.tensor_copy(rparts[32:32 + R, :], mid[:])
                    dve.tensor_tensor(left[:], left[:], mid[:], ALU.subtract)
                    dve.drain()
                    dve.tensor_copy(rparts[64:64 + R, :], left[:])
                    dve.drain().then_inc(rparts_ready, 1)
                for i in range(PAIRS) if main else ():
                    dve.wait_ge(pv_done, TPS * (i + 1))
                    dve.tensor_copy(oT[:, i, :], ps_o[:, i % 2, :]).then_inc(o_taken, 1)
                if front:
                    dve.wait_ge(t_taken, NQK)
                    for m in range(NQK):
                        dve.wait_ge(spread_ready, m + 1)
                        if m < PAIRS:
                            dve.tensor_tensor(q[:, m, :], raw[:, m, :], ps_w[:, 2 + m % 2, :], ALU.mult).then_inc(spread_taken, 1)
                        else:
                            for e in range(2):
                                rows = slice(64 * e, 64 * e + 64)
                                tt = dve.tensor_tensor(kz[rows, e, m - PAIRS, :], raw[rows, m, :], ps_w[rows, 2 + m % 2, :], ALU.mult)
                            tt.then_inc(spread_taken, 1)
                        if m == 2 and main:
                            dve.wait_ge(y_ready, 1)
                            dve.tensor_tensor(y, y, ps_s[:], ALU.add)
                elif main:
                    dve.wait_ge(y_ready, 1)
                    dve.tensor_tensor(y, y, ps_s[:], ALU.add)

        with nc.Block() as block:
            section(block, -1, False, True)
        clear(nc, ph.sems)
        with nc.Fori(0, NSEQ - 1) as b:
            with nc.Block() as block:
                section(block, b, True, True)
            clear(nc, ph.sems)
        with nc.Block() as block:
            section(block, NSEQ - 1, True, False)
        clear(nc, ph.sems)


def geglu(nc, yT, c, t, layer):
    U = 3
    with ExitStack() as ctx:
        ph = Phase(nc, ctx, f"l1g{layer}")
        hT = ph.sb("ht", [P, TOK])
        wa, wb, wo = (ph.sb(n, [P, U, P]) for n in ("wa", "wb", "wo"))
        b_a, b_g = ph.sb("b_a", [P, U]), ph.sb("b_g", [P, U])
        b2, lg, lb = ph.sb("b2", [P, 1]), ph.sb("lg", [P, 1]), ph.sb("lb", [P, 1])
        loaded = ph.sem("loaded")
        with nc.Block() as block:
            @block.sync
            def _(sp):
                for dst, src in ((wa, t["L1_ffn_w1u"][layer, :, 0]), (wb, t["L1_ffn_w1u"][layer, :, 1]), (wo, t["L1_ffn_w2u"][layer]),
                                 (b_a, t["L1_ffn_b1u"][layer, :, 0]), (b_g, t["L1_ffn_b1u"][layer, :, 1]),
                                 (b2, t["L1_ffn_b2"][layer].unsqueeze(1)), (lg, t["L1_ffn_ln_g"][layer].unsqueeze(1)),
                                 (lb, t["L1_ffn_ln_b"][layer].unsqueeze(1))):
                    sp.dma_start(dst[:], src).then_inc(loaded, 16)
                sp.wait_ge(loaded, 16 * 8)

            h3 = hT[:].rearrange("p (b s) -> p b s", s=SEQ)
            y3 = yT[:].rearrange("p (b s) -> p b s", s=SEQ)

            @block.vector
            def _(dve):
                dve.tensor_copy(hT[0:64, :], yT[0:64, :])
                dve.memset(h3[64:P, :, 0:1], 0.0)

            @block.scalar
            def _(act):
                act.copy(h3[64:P, :, 1:SEQ], y3[64:P, :, 0:SEQ - 1])
        clear(nc, ph.sems)
        normalize(nc, hT, hT, c, f"l1gn{layer}", EPS)
        with nc.Block() as block:
            @block.scalar
            def _(act):
                act.activation(hT[:], hT[:], ACT.Identity, scale=lg[:], bias=lb[:])
        experts(nc, yT, hT, c, ph, U, wa, wb, wo, None, None, "geglu", b_a, b_g, None, bias=b2)


def load_x(nc, xT, c, t):
    with ExitStack() as ctx:
        ph = Phase(nc, ctx, "load")
        x = ph.sb("x", [P, NT, P])
        ps = ph.ps("ps", [P, 4, TPS, P])
        loaded, turned, copied = (ph.sem(n) for n in ("loaded", "turned", "copied"))
        ctx.callback(clear, nc, ph.sems)
        block = ctx.enter_context(nc.Block())

        @block.sync
        def _(sp):
            for n in c:
                sp.dma_start(c[n][:], t[n]).then_inc(loaded, 16)
            sp.dma_start(x[:], t["L0_attn_hidden_states"].rearrange("b (k p) d -> p (b k) d", p=P)).then_inc(loaded, 16)

        @block.tensor
        def _(pe):
            pe.wait_ge(loaded, 16 * (len(c) + 1))
            for b in range(NSEQ):
                if b >= 4:
                    pe.wait_ge(copied, b - 3)
                for k in range(TPS):
                    mm = pe.transpose(ps[:, b % 4, k, :], x[:, b * TPS + k, :], c["ident"][:])
                mm.then_inc(turned, 1)

        @block.scalar
        def _(act):
            for b in range(NSEQ):
                act.wait_ge(turned, b + 1)
                act.copy(cols(xT, b), ps[:, b % 4, :, :].rearrange("p k q -> p (k q)")).then_inc(copied, 1)


def store_x(nc, xT, c, out):
    with ExitStack() as ctx:
        ph = Phase(nc, ctx, "store")
        x = ph.sb("x", [P, NT, P])
        ps = ph.ps("ps", [P, 4, TPS, P])
        turned, copied, stored = (ph.sem(n) for n in ("turned", "copied", "stored"))
        ctx.callback(clear, nc, ph.sems)
        block = ctx.enter_context(nc.Block())

        @block.tensor
        def _(pe):
            for b in range(NSEQ):
                if b >= 4:
                    pe.wait_ge(copied, b - 3)
                for k in range(TPS):
                    mm = pe.transpose(ps[:, b % 4, k, :], xT[:, (b * TPS + k) * P:(b * TPS + k + 1) * P], c["ident"][:])
                mm.then_inc(turned, 1)

        @block.scalar
        def _(act):
            for b in range(NSEQ):
                act.wait_ge(turned, b + 1)
                act.copy(x[:, b * TPS:(b + 1) * TPS, :], ps[:, b % 4, :, :]).then_inc(copied, 1)

        @block.sync
        def _(sp):
            for b in range(NSEQ):
                sp.wait_ge(copied, b + 1)
                sp.dma_start(out[b].rearrange("(k p) d -> p k d", p=P), x[:, b * TPS:(b + 1) * TPS, :]).then_inc(stored, 16)
            sp.wait_ge(stored, 16 * NSEQ)


def program(nc, t, out):
    with ExitStack() as ctx:
        ph = Phase(nc, ctx, "main")
        xT = ph.sb("xT", [P, TOK])
        xnT = ph.sb("xnT", [P, TOK])
        c = {n: ph.sb(n, [P, P]) for n in ("ident", "mean", "center", "ones")}
        load_x(nc, xT, c, t)
        for stage in (l0_attn, l0_ffn, l1_attn, l1_ffn, l2_attn, l2_ffn, l3_attn, l3_ffn):
            stage(nc, xT, xnT, c, t)
        store_x(nc, xT, c, out)


def constants():
    n = np.arange(P)
    ang = 2 * np.pi * ((n[:, None] * n[None, :]) % P) / P
    c, s = np.cos(ang), np.sin(ang)
    q = np.arange(P)
    d = 2 * ((np.arange(P) % 8) // 2)
    inv_freq = (1.0 / np.float32(10000.0) ** (d.astype(np.float32) / np.float32(8))).astype(np.float32)
    freqs = (np.arange(SEQ, dtype=np.float32)[None, :] * inv_freq[:, None]).astype(np.float32).astype(np.float64)
    sign = np.where(np.arange(P) % 2 == 0, -1.0, 1.0)[:, None]
    head = q // 8
    blocks = np.concatenate([head[:, None] == head[None, :], head[:, None] == np.arange(16)[None, :]], 1)
    sel8 = np.zeros((3, 32, 8, P), np.float32)
    sel8[:, np.arange(8), np.arange(8), :] = 1
    half = np.arange(0, 64, 2, dtype=np.float32)
    inv64 = (np.float32(1.0) / np.float32(10000.0) ** (half / np.float32(64))).astype(np.float32)
    tt = np.arange(SEQ, dtype=np.float32)
    fr = (tt[None, :] * inv64[:, None]).astype(np.float32).astype(np.float64)
    base = ((half + np.float32(25.6)) / np.float32(89.6)).astype(np.float32).astype(np.float64)
    xp = base[:, None] ** ((tt - SEQ // 2) / 32.0)[None, :].astype(np.float64)
    two = lambda first, second: np.concatenate([first, second] * 2, 0)
    cos64, sin64 = np.cos(fr), np.sin(fr)
    xpos = np.stack([8 * two(cos64 * xp, cos64 * xp), 8 * two(-sin64 * xp, sin64 * xp),
                     two(cos64 / xp, cos64 / xp), two(-sin64 / xp, sin64 / xp)], 1)
    m8, f = np.arange(8), np.arange(P)
    statsel = (np.arange(16)[None, None, :] == 2 * m8[None, :, None] + f[:, None, None] // 64).astype(np.float32)
    spread = np.zeros((3, 32, 8, P), np.float32)
    spread[:, :16] = statsel.transpose(2, 1, 0)
    lsel = np.broadcast_to(np.eye(8, dtype=np.float32)[None, :, :, None], (3, 8, 8, P)).reshape(24, 8, P)
    jj = np.arange(192)
    da, dt = f[:, None] + 64 - jj[None, :], jj[None, :] - f[:, None]
    band = np.stack([np.where((d >= 0) & (d <= 64), 0, -1e30) for d in (da, dt)], 1)
    sel32 = np.zeros((3, 32, 16, P), np.float32)
    sel32[:, np.arange(32)[:, None], np.arange(32)[:, None] // 2, np.arange(32)[:, None] % 2 * 64 + np.arange(64)] = 1
    c32 = np.arange(32)
    tri = np.stack([c32[None, :] > c32[:, None], c32[None, :] >= c32[:, None], c32[None, :] == c32[:, None]], 1)
    return {
        "heads4": (q[:, None] // 32 == np.arange(4)[None, :]).astype(np.float32),
        "tri32": np.tile(tri, (4, 1, 1)).astype(np.float32),
        "xpos": xpos.astype(np.float32), "statsel": statsel, "spread": spread.reshape(96, 8, P), "lsel": lsel, "band": band.astype(np.float32),
        "sel32": sel32.reshape(96, 16, P),
        "blocks8": blocks.astype(np.float32),
        "sel8": sel8.reshape(96, 8, P),
        "causal": np.stack([np.where(q[None, :] > q[:, None], -1e30, 0), np.where(q[None, :] < q[:, None], -1e30, 0)]).astype(np.float32),
        "rope8": np.stack([np.cos(freqs), sign * np.sin(freqs)]).astype(np.float32),
        "ident": np.eye(P, dtype=np.float32),
        "ones": np.ones((P, P), np.float32),
        "center": (np.eye(P) - 1.0 / P).astype(np.float32),
        "mean": np.full((P, P), 1.0 / P, np.float32),
        "dft": np.stack([c, s, c / P, -s / P, -s]).astype(np.float32),
    }


def laid_out(inputs):
    x = {n: np.asarray(a) for n, a in inputs.items()}
    x["L0_attn_Wb_wide"] = np.repeat(x.pop("L0_attn_Wb"), 32, 1)
    for n in ("short", "long"):
        x[f"L0_attn_fir_{n}_wp"] = x.pop(f"L0_attn_fir_{n}_w").reshape(P, -1)
    x["L0_attn_taps"] = np.stack([x.pop(f"L0_attn_conv_{n}_w").T for n in ("q", "k", "v")])
    w1 = x.pop("L0_attn_mlp_w1")
    zeros = lambda *shape: np.zeros(shape, w1.dtype)
    x["L0_attn_w1a"] = w1[:P]
    x["L0_attn_w1b"] = np.tile(np.concatenate([w1[P:], zeros(16, P)]), (4, 1))
    x["L0_attn_w2p"] = np.concatenate([x.pop("L0_attn_mlp_w2"), zeros(P, 28)], 1)
    x["L0_attn_b1"] = x.pop("L0_attn_mlp_b1").reshape(P, 1)
    x["L0_attn_b2p"] = np.tile(np.concatenate([x.pop("L0_attn_mlp_b2"), zeros(28)]), 4).reshape(P, 1)
    x["L0_attn_temp"] = np.repeat(x.pop("L0_attn_log_temp").reshape(4), 32).reshape(P, 1)
    x["L0_attn_onorm"] = np.tile(x.pop("L0_attn_o_norm_w"), 4).reshape(P, 1)
    for n in ("Wq", "Wk", "Wv", "Wo"):
        x[f"L1_attn_{n}T"] = x.pop(f"L1_attn_{n}").T
    x["L3_attn_w_swapped"] = x["L3_attn_w_qkv"].reshape(P, 3, P // 2, 2)[:, :2, :, ::-1].reshape(P, 2, P)
    for n in ("gate_w", "sw1", "sw2", "sw3"):
        x[f"L2_ffn_{n}T"] = x.pop(f"L2_ffn_{n}").T
    for n in ("W1", "W3"):
        x[f"L2_ffn_{n}p"] = x.pop(f"L2_ffn_{n}").transpose(1, 0, 2).reshape(P, 16, P)
    x["L2_ffn_W2p"] = x.pop("L2_ffn_W2").reshape(16, P, P).transpose(1, 0, 2)
    swap = lambda a: np.roll(a.reshape(*a.shape[:-1], a.shape[-1] // 64, 2, 32), 1, axis=-2).reshape(a.shape)
    x["L1_ffn_wswap"] = swap(x["L1_ffn_wqkv"][:, :, :1024]).reshape(2, P, 8, P)
    qs, ks = x.pop("L1_ffn_q_scale"), x.pop("L1_ffn_k_scale")
    x["L1_ffn_scales"] = np.tile(np.stack([qs, swap(qs), ks, swap(ks)], -1), (1, 2, 1))
    pad = lambda a, axis: np.concatenate([a, np.zeros_like(np.take(a, range(3 * P - 341), axis))], axis)
    x["L1_ffn_w1u"] = pad(x.pop("L1_ffn_w1").reshape(2, P, 2, 341), 3).reshape(2, P, 2, 3, P)
    x["L1_ffn_b1u"] = pad(x.pop("L1_ffn_b1").reshape(2, 2, 341), 2).reshape(2, 2, 3, P).transpose(0, 3, 1, 2)
    x["L1_ffn_w2u"] = pad(x.pop("L1_ffn_w2"), 1).reshape(2, 3, P, P).transpose(0, 2, 1, 3)
    w1 = x.pop("L3_ffn_mlp1_w").reshape(8, P, 2, P)
    x["L3_ffn_w1T"] = w1.transpose(3, 0, 2, 1)
    x["L3_ffn_b1T"] = x.pop("L3_ffn_mlp1_b").reshape(8, P, 2).transpose(1, 2, 0)
    x["L3_ffn_w2T"] = x.pop("L3_ffn_mlp2_w").transpose(2, 0, 1)
    x["L3_ffn_gate_wT"] = x.pop("L3_ffn_gate_w").T
    return x


def kernel(**inputs):
    import concourse.bacc as bacc
    from concourse.bass_utils import run_bass_kernel_spmd

    nc = bacc.Bacc("TRN2", target_bir_lowering=False, num_devices=1)
    arrays, t = {}, {}
    for name, a in {**laid_out(inputs), **constants()}.items():
        a = np.ascontiguousarray(a)
        arrays[f"in_{name}"] = a
        t[name] = nc.dram_tensor(f"in_{name}", a.shape, mybir.dt.from_np(a.dtype), kind="ExternalInput").ap()
    out = nc.dram_tensor("out_x", (NSEQ, SEQ, P), F32, kind="ExternalOutput").ap()
    program(nc, t, out)
    r = run_bass_kernel_spmd(nc, [arrays], core_ids=[0])
    return r.results[0]["out_x"]
```
